# Optimizing a Trainium2 kernel written in Bass

```python
import numpy as np
import jax
import jax.numpy as jnp

def _softmax(x, axis=-1):
    return jax.nn.softmax(x, axis=axis)

def _gelu(x):
    return jax.nn.gelu(x, approximate=True)

def _silu(x):
    return jax.nn.silu(x)

def _sigmoid(x):
    return jax.nn.sigmoid(x)

def _layernorm(x, axis=-1, eps=1e-05):
    m = jnp.mean(x, axis=axis, keepdims=True)
    v = jnp.var(x, axis=axis, keepdims=True)
    return (x - m) / jnp.sqrt(v + eps)

def _scatter_add(tgt, idx, src, axis=0):
    return tgt.at[idx].add(src)

def _segment_sum(src, seg, n):
    return jax.ops.segment_sum(src, seg, n)
kernel_name = 'mk_xattn_seq_d4_seqx_r8_01e98c'

def setup_inputs(seed: int=0):
    np.random.seed(seed)
    _w = jnp.asarray

    def _rec_inputs():
        import jax
        import jax.numpy as jnp
        _rk = jax.random.key(seed)
        x = -0.000125 + 0.9999 * jax.random.normal(jax.random.fold_in(_rk, 1), (16, 128, 256), jnp.float32)
        _lenS = 128 - jax.random.randint(jax.random.fold_in(_rk, 7), (16,), 0, max(1, 128 // 4) + 1, jnp.int32)
        _lenS2 = 128 - jax.random.randint(jax.random.fold_in(_rk, 8), (16,), 0, max(1, 128 // 4) + 1, jnp.int32)
        _ctx_1024P = jax.random.normal(jax.random.fold_in(_rk, 11), (16, 16, 128), jnp.float32)
        _ctx_1024c = jax.random.dirichlet(jax.random.fold_in(_rk, 511), 0.3 * jnp.ones((16,), jnp.float32), (16, 128))
        _ctx_1024t = jnp.einsum('bsk,bkd->bsd', _ctx_1024c, _ctx_1024P)
        _ctx_1024t = _ctx_1024t * jax.lax.rsqrt(jnp.mean(jnp.square(_ctx_1024t)) + 1e-12) * 0.953939
        ctx_1024 = 4.13588e-05 + 0.999923 * (_ctx_1024t + 0.3 * jax.random.normal(jax.random.fold_in(_rk, 611), (16, 128, 128), jnp.float32))
        pos_1xS = jnp.broadcast_to(jnp.arange(128, dtype=jnp.int32), (1, 128))
        _validS = jnp.arange(128)[None, :] < _lenS[:, None]
        _validS2 = jnp.arange(128)[None, :] < _lenS2[:, None]
        _causal = jnp.tril(jnp.ones((128, 128), dtype=bool))
        mask_BxS_ik0 = jnp.where(jnp.broadcast_to(_validS[:, :], (16, 128)), 0, 1).astype(jnp.int32)
        mask_BxS2_bk0 = jnp.logical_not(jnp.broadcast_to(_validS2[:, :], (16, 128)))
        return (x, ctx_1024, pos_1xS, mask_BxS_ik0, mask_BxS2_bk0)
    x, ctx_1024, pos_1xS, mask_BxS_ik0, mask_BxS2_bk0 = _rec_inputs()

    def _L0_xattn_setup():
        import jax, jax.numpy as jnp
        import numpy as np
        EPS = 1e-06

        def _rmsnorm(x, w):
            var = jnp.mean(jnp.square(x), axis=-1, keepdims=True)
            return x * jax.lax.rsqrt(var + EPS) * w
        key = jax.random.key(seed)
        ks = jax.random.split(key, 6)
        B, N, M = (4, 512, 256)
        d_model, memory_dim = (256, 128)
        hidden_states = jax.random.normal(ks[0], (B, N, d_model), dtype=jnp.float32)
        memory = jax.random.normal(ks[1], (B, M, memory_dim), dtype=jnp.float32)
        W_mem = jax.random.normal(ks[2], (d_model, memory_dim), dtype=jnp.float32) / np.sqrt(memory_dim)
        W_gate = jax.random.normal(ks[3], (d_model, 2 * d_model), dtype=jnp.float32) / np.sqrt(2 * d_model)
        b_gate = jax.random.normal(ks[4], (d_model,), dtype=jnp.float32) * 0.01
        norm_w = jnp.ones((d_model,), dtype=jnp.float32)
        return {'hidden_states': hidden_states, 'memory': memory, 'W_mem': W_mem, 'W_gate': W_gate, 'b_gate': b_gate, 'norm_w': norm_w}
    _L0_xattn_all = _L0_xattn_setup()
    _L0_xattn_in = {k: v for k, v in _L0_xattn_all.items() if k in ('W_mem', 'W_gate', 'b_gate', 'norm_w')}
    del _L0_xattn_all

    def _L1_xattn_setup():
        import jax, jax.numpy as jnp
        import numpy as np
        H = 256
        NH = 16
        HD = H // NH
        CH = 128
        CC = 128
        CHD = CC // NH
        I = 688
        B = 2
        L = 256
        LE = 128
        EPS = 1e-06

        def rms_norm(x, w):
            xf = x.astype(jnp.float32)
            var = jnp.mean(xf * xf, axis=-1, keepdims=True)
            return (w * (xf * jax.lax.rsqrt(var + EPS))).astype(x.dtype)

        def expert_mask(tt):
            vm = jnp.zeros(tt.shape, dtype=bool)
            vm = vm.at[:, :-1].set((tt[:, :-1] == 1) & (tt[:, 1:] == 1))
            return vm

        def rotate_half(x):
            d = x.shape[-1] // 2
            return jnp.concatenate([-x[..., d:], x[..., :d]], axis=-1)

        def apply_rotary(q, k, position_ids, seq_len):
            inv = 1.0 / 10000.0 ** (jnp.arange(0, HD, 2, dtype=jnp.float32) / HD)
            t = jnp.arange(seq_len, dtype=jnp.float32)
            freqs = jnp.outer(t, inv)
            emb = jnp.concatenate([freqs, freqs], axis=-1)
            cos = jnp.cos(emb)[position_ids][:, None].astype(q.dtype)
            sin = jnp.sin(emb)[position_ids][:, None].astype(q.dtype)
            return (q * cos + rotate_half(q) * sin, k * cos + rotate_half(k) * sin)

        def sdpa(q, k, v, causal):
            scale = 1.0 / np.sqrt(q.shape[-1])
            scores = jnp.einsum('bhqd,bhkd->bhqk', q * scale, k)
            if causal:
                mask = jnp.tril(jnp.ones((q.shape[-2], k.shape[-2]), dtype=bool))
                scores = jnp.where(mask, scores, jnp.finfo(jnp.float32).min)
            p = jax.nn.softmax(scores.astype(jnp.float32), axis=-1).astype(q.dtype)
            return jnp.einsum('bhqk,bhkd->bhqd', p, v)

        def heads(x, nh, hd):
            b, l, _ = x.shape
            return x.reshape(b, l, nh, hd).transpose(0, 2, 1, 3)
        key = jax.random.key(seed)
        ks = jax.random.split(key, 20)
        s = 0.02
        f32 = jnp.float32
        return {'hidden_states': jax.random.normal(ks[0], (B, L, H), f32), 'encoder_outputs': jax.random.normal(ks[1], (B, LE, CH), f32), 'token_type_ids': jax.random.randint(ks[2], (B, L), 0, 2, jnp.int32), 'position_ids': jnp.arange(L, dtype=jnp.int32)[None, :], 'ln_in_w': jnp.ones((H,), f32), 'ln_post_attn_w': jnp.ones((H,), f32), 'ln_post_cross_w': jnp.ones((H,), f32), 'v_qkv': jax.random.normal(ks[3], (H, 3 * H), f32) * s, 'l_qkv': jax.random.normal(ks[4], (H, 3 * H), f32) * s, 'v_dense': jax.random.normal(ks[5], (H, H), f32) * s, 'l_dense': jax.random.normal(ks[6], (H, H), f32) * s, 'cq_w': jax.random.normal(ks[7], (H, CC), f32) * s, 'ckv_w': jax.random.normal(ks[8], (CH, 2 * CC), f32) * s, 'cdense_w': jax.random.normal(ks[9], (CC, H), f32) * s, 'v_gate': jax.random.normal(ks[10], (H, I), f32) * s, 'v_up': jax.random.normal(ks[11], (H, I), f32) * s, 'v_down': jax.random.normal(ks[12], (I, H), f32) * s, 'l_gate': jax.random.normal(ks[13], (H, I), f32) * s, 'l_up': jax.random.normal(ks[14], (H, I), f32) * s, 'l_down': jax.random.normal(ks[15], (I, H), f32) * s}
    _L1_xattn_all = _L1_xattn_setup()
    _L1_xattn_in = {k: v for k, v in _L1_xattn_all.items() if k in ('ln_in_w', 'ln_post_attn_w', 'ln_post_cross_w', 'v_qkv', 'l_qkv', 'v_dense', 'l_dense', 'cq_w', 'ckv_w', 'cdense_w', 'v_gate', 'v_up', 'v_down', 'l_gate', 'l_up', 'l_down')}
    del _L1_xattn_all

    def _L2_xattn_setup():
        import jax, jax.numpy as jnp
        import numpy as np
        DIM = 256
        DIM_MEDIA = 128
        HEADS = 16
        DIM_HEAD = 64
        INNER = HEADS * DIM_HEAD
        FF_INNER = 4 * DIM
        B, N_TOK, N_LAT = (4, 256, 64)
        EPS = 1e-05

        def layernorm(x, g, b):
            mu = jnp.mean(x, axis=-1, keepdims=True)
            var = jnp.var(x, axis=-1, keepdims=True)
            return (x - mu) * jax.lax.rsqrt(var + EPS) * g + b
        key = jax.random.key(seed)
        ks = jax.random.split(key, 12)
        x = jax.random.normal(ks[0], (B, N_TOK, DIM), dtype=jnp.float32)
        media = jax.random.normal(ks[1], (B, N_LAT, DIM_MEDIA), dtype=jnp.float32)
        media_mask = jax.random.randint(ks[2], (B, N_LAT), 0, 2).astype(bool)
        media_mask = media_mask.at[:, 0].set(True)
        s = lambda d: 1.0 / np.sqrt(d)
        Wq = jax.random.normal(ks[3], (DIM, INNER), dtype=jnp.float32) * s(DIM)
        Wkv = jax.random.normal(ks[4], (DIM_MEDIA, 2 * INNER), dtype=jnp.float32) * s(DIM_MEDIA)
        Wo = jax.random.normal(ks[5], (INNER, DIM), dtype=jnp.float32) * s(INNER)
        W1 = jax.random.normal(ks[6], (DIM, FF_INNER), dtype=jnp.float32) * s(DIM)
        W2 = jax.random.normal(ks[7], (FF_INNER, DIM), dtype=jnp.float32) * s(FF_INNER)
        return {'x': x, 'media': media, 'media_mask': media_mask, 'ln_q_g': jnp.ones((DIM,), jnp.float32), 'ln_q_b': jnp.zeros((DIM,), jnp.float32), 'Wq': Wq, 'Wkv': Wkv, 'Wo': Wo, 'attn_gate': jax.random.normal(ks[8], (1,), jnp.float32) * 0.5, 'ln_ff_g': jnp.ones((DIM,), jnp.float32), 'ln_ff_b': jnp.zeros((DIM,), jnp.float32), 'W1': W1, 'W2': W2, 'ff_gate': jax.random.normal(ks[9], (1,), jnp.float32) * 0.5}
    _L2_xattn_all = _L2_xattn_setup()
    _L2_xattn_in = {k: v for k, v in _L2_xattn_all.items() if k in ('ln_q_g', 'ln_q_b', 'Wq', 'Wkv', 'Wo', 'attn_gate', 'ln_ff_g', 'ln_ff_b', 'W1', 'W2', 'ff_gate')}
    del _L2_xattn_all

    def _L3_xattn_setup():
        import jax, jax.numpy as jnp
        import numpy as np
        DIM = 256
        DIM_MEDIA = 128
        HEADS = 16
        DIM_HEAD = 64
        INNER = HEADS * DIM_HEAD
        FF_INNER = 4 * DIM
        B, N_TOK, N_LAT = (4, 256, 64)
        EPS = 1e-05

        def layernorm(x, g, b):
            mu = jnp.mean(x, axis=-1, keepdims=True)
            var = jnp.var(x, axis=-1, keepdims=True)
            return (x - mu) * jax.lax.rsqrt(var + EPS) * g + b
        key = jax.random.key(seed)
        ks = jax.random.split(key, 12)
        x = jax.random.normal(ks[0], (B, N_TOK, DIM), dtype=jnp.float32)
        media = jax.random.normal(ks[1], (B, N_LAT, DIM_MEDIA), dtype=jnp.float32)
        media_mask = jax.random.randint(ks[2], (B, N_LAT), 0, 2).astype(bool)
        media_mask = media_mask.at[:, 0].set(True)
        s = lambda d: 1.0 / np.sqrt(d)
        Wq = jax.random.normal(ks[3], (DIM, INNER), dtype=jnp.float32) * s(DIM)
        Wkv = jax.random.normal(ks[4], (DIM_MEDIA, 2 * INNER), dtype=jnp.float32) * s(DIM_MEDIA)
        Wo = jax.random.normal(ks[5], (INNER, DIM), dtype=jnp.float32) * s(INNER)
        W1 = jax.random.normal(ks[6], (DIM, FF_INNER), dtype=jnp.float32) * s(DIM)
        W2 = jax.random.normal(ks[7], (FF_INNER, DIM), dtype=jnp.float32) * s(FF_INNER)
        return {'x': x, 'media': media, 'media_mask': media_mask, 'ln_q_g': jnp.ones((DIM,), jnp.float32), 'ln_q_b': jnp.zeros((DIM,), jnp.float32), 'Wq': Wq, 'Wkv': Wkv, 'Wo': Wo, 'attn_gate': jax.random.normal(ks[8], (1,), jnp.float32) * 0.5, 'ln_ff_g': jnp.ones((DIM,), jnp.float32), 'ln_ff_b': jnp.zeros((DIM,), jnp.float32), 'W1': W1, 'W2': W2, 'ff_gate': jax.random.normal(ks[9], (1,), jnp.float32) * 0.5}
    _L3_xattn_all = _L3_xattn_setup()
    _L3_xattn_in = {k: v for k, v in _L3_xattn_all.items() if k in ('ln_q_g', 'ln_q_b', 'Wq', 'Wkv', 'Wo', 'attn_gate', 'ln_ff_g', 'ln_ff_b', 'W1', 'W2', 'ff_gate')}
    del _L3_xattn_all
    return {'x': x, 'ctx_1024': ctx_1024, 'pos_1xS': pos_1xS, 'mask_BxS_ik0': mask_BxS_ik0, 'mask_BxS2_bk0': mask_BxS2_bk0, 'L0_xattn_W_mem': _L0_xattn_in['W_mem'], 'L0_xattn_W_gate': _L0_xattn_in['W_gate'], 'L0_xattn_b_gate': _L0_xattn_in['b_gate'], 'L0_xattn_norm_w': _L0_xattn_in['norm_w'], 'L1_xattn_ln_in_w': _L1_xattn_in['ln_in_w'], 'L1_xattn_ln_post_attn_w': _L1_xattn_in['ln_post_attn_w'], 'L1_xattn_ln_post_cross_w': _L1_xattn_in['ln_post_cross_w'], 'L1_xattn_v_qkv': _L1_xattn_in['v_qkv'], 'L1_xattn_l_qkv': _L1_xattn_in['l_qkv'], 'L1_xattn_v_dense': _L1_xattn_in['v_dense'], 'L1_xattn_l_dense': _L1_xattn_in['l_dense'], 'L1_xattn_cq_w': _L1_xattn_in['cq_w'], 'L1_xattn_ckv_w': _L1_xattn_in['ckv_w'], 'L1_xattn_cdense_w': _L1_xattn_in['cdense_w'], 'L1_xattn_v_gate': _L1_xattn_in['v_gate'], 'L1_xattn_v_up': _L1_xattn_in['v_up'], 'L1_xattn_v_down': _L1_xattn_in['v_down'], 'L1_xattn_l_gate': _L1_xattn_in['l_gate'], 'L1_xattn_l_up': _L1_xattn_in['l_up'], 'L1_xattn_l_down': _L1_xattn_in['l_down'], 'L2_xattn_ln_q_g': _L2_xattn_in['ln_q_g'], 'L2_xattn_ln_q_b': _L2_xattn_in['ln_q_b'], 'L2_xattn_Wq': _L2_xattn_in['Wq'], 'L2_xattn_Wkv': _L2_xattn_in['Wkv'], 'L2_xattn_Wo': _L2_xattn_in['Wo'], 'L2_xattn_attn_gate': _L2_xattn_in['attn_gate'], 'L2_xattn_ln_ff_g': _L2_xattn_in['ln_ff_g'], 'L2_xattn_ln_ff_b': _L2_xattn_in['ln_ff_b'], 'L2_xattn_W1': _L2_xattn_in['W1'], 'L2_xattn_W2': _L2_xattn_in['W2'], 'L2_xattn_ff_gate': _L2_xattn_in['ff_gate'], 'L3_xattn_ln_q_g': _L3_xattn_in['ln_q_g'], 'L3_xattn_ln_q_b': _L3_xattn_in['ln_q_b'], 'L3_xattn_Wq': _L3_xattn_in['Wq'], 'L3_xattn_Wkv': _L3_xattn_in['Wkv'], 'L3_xattn_Wo': _L3_xattn_in['Wo'], 'L3_xattn_attn_gate': _L3_xattn_in['attn_gate'], 'L3_xattn_ln_ff_g': _L3_xattn_in['ln_ff_g'], 'L3_xattn_ln_ff_b': _L3_xattn_in['ln_ff_b'], 'L3_xattn_W1': _L3_xattn_in['W1'], 'L3_xattn_W2': _L3_xattn_in['W2'], 'L3_xattn_ff_gate': _L3_xattn_in['ff_gate']}

def reference(x, ctx_1024, pos_1xS, mask_BxS_ik0, mask_BxS2_bk0, L0_xattn_W_mem, L0_xattn_W_gate, L0_xattn_b_gate, L0_xattn_norm_w, L1_xattn_ln_in_w, L1_xattn_ln_post_attn_w, L1_xattn_ln_post_cross_w, L1_xattn_v_qkv, L1_xattn_l_qkv, L1_xattn_v_dense, L1_xattn_l_dense, L1_xattn_cq_w, L1_xattn_ckv_w, L1_xattn_cdense_w, L1_xattn_v_gate, L1_xattn_v_up, L1_xattn_v_down, L1_xattn_l_gate, L1_xattn_l_up, L1_xattn_l_down, L2_xattn_ln_q_g, L2_xattn_ln_q_b, L2_xattn_Wq, L2_xattn_Wkv, L2_xattn_Wo, L2_xattn_attn_gate, L2_xattn_ln_ff_g, L2_xattn_ln_ff_b, L2_xattn_W1, L2_xattn_W2, L2_xattn_ff_gate, L3_xattn_ln_q_g, L3_xattn_ln_q_b, L3_xattn_Wq, L3_xattn_Wkv, L3_xattn_Wo, L3_xattn_attn_gate, L3_xattn_ln_ff_g, L3_xattn_ln_ff_b, L3_xattn_W1, L3_xattn_W2, L3_xattn_ff_gate):
    import jax
    import jax.numpy as jnp

    def _L0_xattn_ref(hidden_states, memory, W_mem, W_gate, b_gate, norm_w):
        import jax, jax.numpy as jnp
        import numpy as np
        EPS = 1e-06

        def _rmsnorm(x, w):
            var = jnp.mean(jnp.square(x), axis=-1, keepdims=True)
            return x * jax.lax.rsqrt(var + EPS) * w
        D = hidden_states.shape[-1]
        memory_proj = jnp.einsum('bme,de->bmd', memory, W_mem)
        scores = jnp.einsum('bnd,bmd->bnm', hidden_states, memory_proj) / jnp.sqrt(jnp.float32(D))
        attn = jax.nn.softmax(scores, axis=-1)
        memory_context = jnp.einsum('bnm,bmd->bnd', attn, memory_proj)
        gate_input = jnp.concatenate([hidden_states, memory_context], axis=-1)
        gate = jax.nn.sigmoid(jnp.einsum('bnf,df->bnd', gate_input, W_gate) + b_gate)
        fused = hidden_states + gate * memory_context
        return _rmsnorm(fused, norm_w)

    def _L1_xattn_ref(hidden_states, encoder_outputs, token_type_ids, position_ids, ln_in_w, ln_post_attn_w, ln_post_cross_w, v_qkv, l_qkv, v_dense, l_dense, cq_w, ckv_w, cdense_w, v_gate, v_up, v_down, l_gate, l_up, l_down):
        import jax, jax.numpy as jnp
        import numpy as np
        H = 256
        NH = 16
        HD = H // NH
        CH = 128
        CC = 128
        CHD = CC // NH
        I = 688
        B = 2
        L = 256
        LE = 128
        EPS = 1e-06

        def rms_norm(x, w):
            xf = x.astype(jnp.float32)
            var = jnp.mean(xf * xf, axis=-1, keepdims=True)
            return (w * (xf * jax.lax.rsqrt(var + EPS))).astype(x.dtype)

        def expert_mask(tt):
            vm = jnp.zeros(tt.shape, dtype=bool)
            vm = vm.at[:, :-1].set((tt[:, :-1] == 1) & (tt[:, 1:] == 1))
            return vm

        def rotate_half(x):
            d = x.shape[-1] // 2
            return jnp.concatenate([-x[..., d:], x[..., :d]], axis=-1)

        def apply_rotary(q, k, position_ids, seq_len):
            inv = 1.0 / 10000.0 ** (jnp.arange(0, HD, 2, dtype=jnp.float32) / HD)
            t = jnp.arange(seq_len, dtype=jnp.float32)
            freqs = jnp.outer(t, inv)
            emb = jnp.concatenate([freqs, freqs], axis=-1)
            cos = jnp.cos(emb)[position_ids][:, None].astype(q.dtype)
            sin = jnp.sin(emb)[position_ids][:, None].astype(q.dtype)
            return (q * cos + rotate_half(q) * sin, k * cos + rotate_half(k) * sin)

        def sdpa(q, k, v, causal):
            scale = 1.0 / np.sqrt(q.shape[-1])
            scores = jnp.einsum('bhqd,bhkd->bhqk', q * scale, k)
            if causal:
                mask = jnp.tril(jnp.ones((q.shape[-2], k.shape[-2]), dtype=bool))
                scores = jnp.where(mask, scores, jnp.finfo(jnp.float32).min)
            p = jax.nn.softmax(scores.astype(jnp.float32), axis=-1).astype(q.dtype)
            return jnp.einsum('bhqk,bhkd->bhqd', p, v)

        def heads(x, nh, hd):
            b, l, _ = x.shape
            return x.reshape(b, l, nh, hd).transpose(0, 2, 1, 3)
        b, l, _ = hidden_states.shape
        vm = expert_mask(token_type_ids)[..., None]
        residual = hidden_states
        x = rms_norm(hidden_states, ln_in_w)
        mixed = jnp.where(vm, x @ v_qkv, x @ l_qkv)
        q, k, v = jnp.split(mixed, 3, axis=-1)
        q, k, v = (heads(q, NH, HD), heads(k, NH, HD), heads(v, NH, HD))
        q, k = apply_rotary(q, k, position_ids, l)
        ctx = sdpa(q, k, v, causal=True)
        ctx = ctx.transpose(0, 2, 1, 3).reshape(b, l, H)
        attn_out = jnp.where(vm, ctx @ v_dense, ctx @ l_dense)
        hidden_states = residual + attn_out
        ci = rms_norm(hidden_states, ln_post_cross_w)
        cq = heads(ci @ cq_w, NH, CHD)
        ckv = encoder_outputs @ ckv_w
        ck, cv = jnp.split(ckv, 2, axis=-1)
        ck, cv = (heads(ck, NH, CHD), heads(cv, NH, CHD))
        cctx = sdpa(cq, ck, cv, causal=False)
        cctx = cctx.transpose(0, 2, 1, 3).reshape(b, l, CC)
        hidden_states = hidden_states + cctx @ cdense_w
        mi = rms_norm(hidden_states, ln_post_attn_w)
        v_out = jax.nn.silu(mi @ v_gate) * (mi @ v_up) @ v_down
        l_out = jax.nn.silu(mi @ l_gate) * (mi @ l_up) @ l_down
        hidden_states = hidden_states + jnp.where(vm, v_out, l_out)
        return hidden_states

    def _L2_xattn_ref(x, media, media_mask, ln_q_g, ln_q_b, Wq, Wkv, Wo, attn_gate, ln_ff_g, ln_ff_b, W1, W2, ff_gate):
        import jax, jax.numpy as jnp
        import numpy as np
        DIM = 256
        DIM_MEDIA = 128
        HEADS = 16
        DIM_HEAD = 64
        INNER = HEADS * DIM_HEAD
        FF_INNER = 4 * DIM
        B, N_TOK, N_LAT = (4, 256, 64)
        EPS = 1e-05

        def layernorm(x, g, b):
            mu = jnp.mean(x, axis=-1, keepdims=True)
            var = jnp.var(x, axis=-1, keepdims=True)
            return (x - mu) * jax.lax.rsqrt(var + EPS) * g + b
        scale = DIM_HEAD ** (-0.5)
        qn = layernorm(x, ln_q_g, ln_q_b)
        q = qn @ Wq * scale
        kv = media @ Wkv
        k, v = jnp.split(kv, 2, axis=-1)
        split_heads = lambda t: t.reshape(t.shape[0], t.shape[1], HEADS, DIM_HEAD).transpose(0, 2, 1, 3)
        q, k, v = (split_heads(q), split_heads(k), split_heads(v))
        sim = jnp.einsum('bhid,bhjd->bhij', q, k)
        neg_inf = jnp.finfo(sim.dtype).min
        sim = jnp.where(media_mask[:, None, None, :], sim, neg_inf)
        attn = jax.nn.softmax(sim, axis=-1)
        out = jnp.einsum('bhij,bhjd->bhid', attn, v)
        out = out.transpose(0, 2, 1, 3).reshape(x.shape[0], x.shape[1], INNER)
        attn_out = out @ Wo
        x = x + jnp.tanh(attn_gate) * attn_out
        h = layernorm(x, ln_ff_g, ln_ff_b)
        h = jax.nn.gelu(h @ W1, approximate=False) @ W2
        x = x + jnp.tanh(ff_gate) * h
        return x

    def _L3_xattn_ref(x, media, media_mask, ln_q_g, ln_q_b, Wq, Wkv, Wo, attn_gate, ln_ff_g, ln_ff_b, W1, W2, ff_gate):
        import jax, jax.numpy as jnp
        import numpy as np
        DIM = 256
        DIM_MEDIA = 128
        HEADS = 16
        DIM_HEAD = 64
        INNER = HEADS * DIM_HEAD
        FF_INNER = 4 * DIM
        B, N_TOK, N_LAT = (4, 256, 64)
        EPS = 1e-05

        def layernorm(x, g, b):
            mu = jnp.mean(x, axis=-1, keepdims=True)
            var = jnp.var(x, axis=-1, keepdims=True)
            return (x - mu) * jax.lax.rsqrt(var + EPS) * g + b
        scale = DIM_HEAD ** (-0.5)
        qn = layernorm(x, ln_q_g, ln_q_b)
        q = qn @ Wq * scale
        kv = media @ Wkv
        k, v = jnp.split(kv, 2, axis=-1)
        split_heads = lambda t: t.reshape(t.shape[0], t.shape[1], HEADS, DIM_HEAD).transpose(0, 2, 1, 3)
        q, k, v = (split_heads(q), split_heads(k), split_heads(v))
        sim = jnp.einsum('bhid,bhjd->bhij', q, k)
        neg_inf = jnp.finfo(sim.dtype).min
        sim = jnp.where(media_mask[:, None, None, :], sim, neg_inf)
        attn = jax.nn.softmax(sim, axis=-1)
        out = jnp.einsum('bhij,bhjd->bhid', attn, v)
        out = out.transpose(0, 2, 1, 3).reshape(x.shape[0], x.shape[1], INNER)
        attn_out = out @ Wo
        x = x + jnp.tanh(attn_gate) * attn_out
        h = layernorm(x, ln_ff_g, ln_ff_b)
        h = jax.nn.gelu(h @ W1, approximate=False) @ W2
        x = x + jnp.tanh(ff_gate) * h
        return x
    x = _L0_xattn_ref(x, ctx_1024, L0_xattn_W_mem, L0_xattn_W_gate, L0_xattn_b_gate, L0_xattn_norm_w)
    x = _L1_xattn_ref(x, ctx_1024, mask_BxS_ik0, pos_1xS, L1_xattn_ln_in_w, L1_xattn_ln_post_attn_w, L1_xattn_ln_post_cross_w, L1_xattn_v_qkv, L1_xattn_l_qkv, L1_xattn_v_dense, L1_xattn_l_dense, L1_xattn_cq_w, L1_xattn_ckv_w, L1_xattn_cdense_w, L1_xattn_v_gate, L1_xattn_v_up, L1_xattn_v_down, L1_xattn_l_gate, L1_xattn_l_up, L1_xattn_l_down)
    x = _L2_xattn_ref(x, ctx_1024, mask_BxS2_bk0, L2_xattn_ln_q_g, L2_xattn_ln_q_b, L2_xattn_Wq, L2_xattn_Wkv, L2_xattn_Wo, L2_xattn_attn_gate, L2_xattn_ln_ff_g, L2_xattn_ln_ff_b, L2_xattn_W1, L2_xattn_W2, L2_xattn_ff_gate)
    x = _L3_xattn_ref(x, ctx_1024, mask_BxS2_bk0, L3_xattn_ln_q_g, L3_xattn_ln_q_b, L3_xattn_Wq, L3_xattn_Wkv, L3_xattn_Wo, L3_xattn_attn_gate, L3_xattn_ln_ff_g, L3_xattn_ln_ff_b, L3_xattn_W1, L3_xattn_W2, L3_xattn_ff_gate)
    return x

_drawn_inputs = setup_inputs


def setup_inputs(seed=0):
    import zlib

    import numpy as np

    out = dict(_drawn_inputs(seed))
    spreads = {'L0_xattn_norm_w': (1.0, 0.2),
     'L1_xattn_ln_in_w': (1.0, 0.6),
     'L1_xattn_ln_post_attn_w': (1.0, 0.6),
     'L1_xattn_ln_post_cross_w': (1.0, 0.6),
     'L2_xattn_ln_q_g': (1.0, 0.6),
     'L2_xattn_ln_q_b': (0.0, 2.0),
     'L2_xattn_ln_ff_g': (1.0, 0.6),
     'L2_xattn_ln_ff_b': (0.0, 2.0),
     'L3_xattn_ln_q_g': (1.0, 0.6),
     'L3_xattn_ln_q_b': (0.0, 2.0),
     'L3_xattn_ln_ff_g': (1.0, 0.6),
     'L3_xattn_ln_ff_b': (0.0, 2.0)}
    factors = {'L0_xattn_b_gate': 8.0,
     'L1_xattn_v_qkv': 8.0,
     'L1_xattn_v_dense': 7.49,
     'L1_xattn_cq_w': 64.0,
     'L1_xattn_v_gate': 6.369,
     'L1_xattn_v_up': 6.298,
     'L1_xattn_v_down': 6.335,
     'L2_xattn_W1': 12.676,
     'L3_xattn_W1': 12.796,
     'L1_xattn_l_dense': 5.763,
     'L1_xattn_ckv_w': 8.0,
     'L1_xattn_cdense_w': 8.0,
     'L1_xattn_l_gate': 6.57,
     'L1_xattn_l_up': 6.401,
     'L1_xattn_l_down': 6.439,
     'L2_xattn_Wq': 16.876,
     'L2_xattn_W2': 3.656,
     'L3_xattn_Wq': 18.649,
     'L3_xattn_W2': 3.562,
     'L2_xattn_Wkv': 4.357,
     'L2_xattn_Wo': 4.364,
     'L3_xattn_Wkv': 4.368,
     'L3_xattn_Wo': 4.349}
    for name, (base, spread) in spreads.items():
        noise = np.random.default_rng([zlib.crc32(name.encode()), seed]).standard_normal(out[name].shape)
        drawn = base * np.exp(spread * noise) if base else spread * noise
        out[name] = jnp.asarray(drawn.astype(out[name].dtype))
    for name, factor in factors.items():
        out[name] = (out[name] * factor).astype(out[name].dtype)
    return out
```

```python
from contextlib import ExitStack

import numpy as np

import concourse.bass as bass
from concourse import mybir

F32 = mybir.dt.float32
BF16 = mybir.dt.bfloat16
I32 = mybir.dt.int32
U8 = mybir.dt.uint8
ALU = mybir.AluOpType
ACT = mybir.ActivationFunctionType
AX_X = mybir.AxisListType.X

P = 128
B = 16
D = 256
DC = D // P
ROWS = 2
UNITS = 2
ITERS = B // (ROWS * UNITS)
TOK = ROWS * P
BANKS = 8
BANK = 512

HEADS = 16
QUAD = 4
GROUPS = HEADS // QUAD
HD1 = D // HEADS
HDC = P // HEADS
HD2 = 64
INNER = HEADS * HD2
IC = INNER // P
EXPERTS = 2
FF1 = 688
F1C = -(-FF1 // P)
FF2 = 1024
F2C = FF2 // P
ROPE_BASE = 10000.0
EPS_RMS = 1e-6
EPS_LN = 1e-5
MASKED = -(2.0 ** 100)

P_RING = 3
SKEW_T = 2
SKEW_O = 3



def layout(parts):
    table, at = {}, 0
    for name, chunks, width in parts:
        table[name] = (at, chunks, width)
        at += chunks * width
    return table, at


W0, W0_COLS = layout([("mem", 1, D), ("gate", 2 * DC, D)])
W1A, W1A_COLS = layout([("qkv0", DC, 3 * D), ("qkv1", DC, 3 * D), ("dense0", DC, D), ("dense1", DC, D),
                        ("cq", DC, P), ("ckv", 1, 2 * P), ("cdense", 1, D)])
W1B, W1B_COLS = layout([("gate0", DC, F1C * P), ("up0", DC, F1C * P), ("gate1", DC, F1C * P),
                        ("up1", DC, F1C * P), ("down0", F1C, D), ("down1", F1C, D)])
W2A, W2A_COLS = layout([("q", DC, INNER), ("kv", 1, 2 * INNER), ("o", IC, D)])
W2B, W2B_COLS = layout([("w1", DC, FF2), ("w2", F2C, D)])
WA_COLS = max(W1A_COLS, W2A_COLS)
WF_COLS = max(W0_COLS, W1B_COLS, W2B_COLS)

VEC = {n: DC * i for i, n in enumerate(
    ["self_w", "cross_w", "mlp_w", "q_g2", "q_b2", "ff_g2", "ff_b2", "q_g3", "q_b3", "ff_g3", "ff_b3"])}



def both(*kinds):
    return [(k, u) for k in kinds for u in range(UNITS)]


def attention_order(kind):
    groups = [(u, b, g) for u in range(UNITS) for b in range(ROWS) for g in range(GROUPS)]
    steps = []
    for i in range(len(groups) + SKEW_O):
        if i < len(groups):
            steps.append(("scores", kind, i) + groups[i])
        if 0 <= i - SKEW_T < len(groups):
            steps.append(("turn", kind, i - SKEW_T) + groups[i - SKEW_T])
        if 0 <= i - SKEW_O < len(groups):
            steps.append(("values", kind, i - SKEW_O) + groups[i - SKEW_O])
    return steps


def steps_memory():
    return both("load", "memT", "mem", "score0", "turn0", "mix0", "mixT", "gate0", "out0", "end")


def steps_self():
    s = both("load", "norm_self", "xvT", "xlT")
    for u in range(UNITS):
        s += [("qk", u, 0), ("qk", u, 1), ("v1", u)]
    s += both("qT", "kT")
    s += attention_order("self")
    for u in range(UNITS):
        s += [("maskedT", u, 0), ("maskedT", u, 1)]
    s += both("dense")
    s += both("norm_cross", "nT", "cq", "ck", "cv")
    s += attention_order("cross")
    s += both("coT", "cdense", "end")
    return s


def steps_mlp1():
    s = both("norm_mlp", "xvT", "xlT")
    for u in range(UNITS):
        for e in range(EXPERTS):
            for j in range(F1C // 2):
                s += [("gate1", u, e, j), ("up1", u, e, j)]
    return s + both("down", "end")


def steps_attn2():
    s = both("load", "norm_q", "nT")
    for u in range(UNITS):
        s += [("q2", u, j) for j in range(IC // 2)] + [("k2", u, j) for j in range(IC // 2)]
        s += [("v2", u, b, j) for b in range(ROWS) for j in range(2)]
    s += attention_order("media")
    for u in range(UNITS):
        s += [("oT2", u, b, j) for b in range(ROWS) for j in range(2)]
    return s + both("wo", "end")


def steps_ff2():
    s = both("norm_ff", "nT")
    for u in range(UNITS):
        s += [("w1", u, j) for j in range(F2C // 2)]
    return s + both("w2", "end")



EVENTS = {
    "memT": "mm copied", "mem": "mm copied", "score0": "mm max exp", "turn0": "mm copied",
    "mix0": "mm rinv normed", "mixT": "mm copied", "gate0": "mm biased",
    "out0": "tanh gated fused stats aggr square mean eps rstd",
    "norm_self": "stats aggr square mean eps pow rstd xn", "norm_mlp": "stats aggr square mean eps pow rstd xn",
    "norm_cross": "stats aggr square mean eps rstd xn", "norm_q": "stats aggr eps rstd xn",
    "norm_ff": "stats aggr eps rstd xn",
    "xvT": "mm copied", "xlT": "mm copied", "qk": "mm halves sum", "v1": "mm copied", "qT": "mm copied",
    "kT": "mm copied", "scores": "mm max exp", "turn": "mm copied", "values": "mm rinv normed",
    "maskedT": "masked mm copied", "dense": "mm added", "nT": "mm copied", "cq": "mm copied", "ck": "mm copied",
    "cv": "mm copied", "coT": "mm copied", "cdense": "mm", "gate1": "mm silu", "up1": "mm h",
    "down": "mm", "q2": "mm copied", "k2": "mm copied", "v2": "mm copied", "oT2": "mm copied",
    "wo": "mm", "w1": "mm gelu", "w2": "mm", "end": "done",
}
EVENTS = {kind: events.split() for kind, events in EVENTS.items()}
EMPTIED = {k: e[-1] for k, e in EVENTS.items()} | {"qk": "halves"}
LAST = {"cdense", "down", "wo", "w2"}


class Phase:

    def __init__(self, index, layer, steps, before):
        self.index, self.layer, self.steps = index, layer, steps
        self.of_kind, self.place = {}, {}
        for s in steps:
            n = self.of_kind.get(s[0], 0)
            self.place[s] = n
            self.of_kind[s[0]] = n + 1
        self.base = dict(before)
        self.after = {k: before.get(k, 0) + ITERS * self.of_kind.get(k, 0) for k in {*before, *self.of_kind}}
        jobs = [s for s in steps if "mm" in EVENTS.get(s[0], ())]
        self.bank = {s: i % BANKS for i, s in enumerate(jobs)}
        last = {self.bank[s]: s for s in jobs}
        self.held_by = {}
        now = {}
        for s in jobs:
            k = self.bank[s]
            self.held_by[s] = (now[k], 0) if k in now else (last[k], 1)
            now[k] = s

    def count(self, step, event, it, back=0):
        kind = step[0]
        per = self.of_kind[kind]
        before = PRIME.get((kind, event), 0) + self.base.get(kind, 0)
        return it * per + (before + self.place[step] + 1 - back * per)

    def earlier(self, step, n):
        same = [s for s in self.steps if s[0] == step[0]]
        at = self.place[step] - n
        return same[at % len(same)], -(at // len(same))


PHASES = []
for _layer, _steps in [(0, steps_memory()), (1, steps_self()), (1, steps_mlp1()), (2, steps_attn2()),
                       (2, steps_ff2()), (3, steps_attn2()), (3, steps_ff2())]:
    PHASES.append(Phase(len(PHASES), _layer, _steps, PHASES[-1].after if PHASES else {}))
PRIME = {(k, EMPTIED[k]): max(ph.of_kind.get(k, 0) for ph in PHASES) for k in EVENTS}
for _k in LAST:
    del PRIME[_k, "mm"]
for _k in ("cv", "v2", "mem", "values"):
    PRIME[_k, "mm"] = max(ph.of_kind.get(_k, 0) for ph in PHASES)


def build(nc, dram, out):
    with ExitStack() as ctx:
        def sb(name, shape, dt=F32):
            return ctx.enter_context(nc.sbuf_tensor(name, shape, dt))

        sems = {}
        for kind, events in EVENTS.items():
            for e in events:
                sems[kind, e] = ctx.enter_context(nc.semaphore(f"{kind}_{e}"))

        def sem(name):
            return ctx.enter_context(nc.semaphore(name))

        consts_in = sem("consts_in")
        weights_att = sem("weights_att")
        weights_ff = sem("weights_ff")
        x_in = [sem(f"x_in{u}") for u in range(UNITS)]
        xT_in = [sem(f"xT_in{u}") for u in range(UNITS)]
        ctx_in = [sem(f"ctx_in{u}") for u in range(UNITS)]
        setup_v = sem("setup_vector")
        setup_p = sem("setup_pool")
        setup_pe = sem("setup_tensor")
        setup_a = sem("setup_scalar")
        zeroed = sem("zeroed")
        primed = sem("primed")
        out_done = sem("out_done")
        settled = {n: sem(f"settled_{n}") for n in ("vector", "tensor")}

        x_all = sb("x_all", [P, B, D])
        w_att = sb("w_att", [P, WA_COLS])
        w_ff = sb("w_ff", [P, WF_COLS])
        ctxT = [sb(f"ctxT{u}", [P, TOK]) for u in range(UNITS)]
        xn = [sb(f"xn{u}", [P, ROWS, EXPERTS, D]) for u in range(UNITS)]
        xT = [sb(f"xT{u}", [P, EXPERTS, DC, TOK]) for u in range(UNITS)]
        hT = [sb(f"hT{u}", [P, EXPERTS * F1C * TOK]) for u in range(UNITS)]
        kbd = [sb(f"kbd{u}", [P, IC * ROWS * 2 * P]) for u in range(UNITS)]
        v = [sb(f"v{u}", [P, ROWS * HEADS * (HD2 + 1)]) for u in range(UNITS)]
        o = [sb(f"o{u}", [P, ROWS * INNER]) for u in range(UNITS)]
        p_ring = [sb(f"p{i}", [P, BANK]) for i in range(P_RING)]
        pT_ring = [sb(f"pT{i}", [P, BANK]) for i in range(P_RING)]
        nmax = sb("nmax", [P, P_RING + 1, QUAD])
        rinv = sb("rinv", [P, 2, QUAD])
        rsum0 = sb("rsum0", [P, UNITS, ROWS])
        rinv0 = sb("rinv0", [P, UNITS, ROWS])
        stats = sb("stats", [P, UNITS, ROWS, 6])
        aggr = sb("aggr", [P, UNITS, ROWS, 2])
        ms = sb("ms", [P, UNITS, 4, ROWS])
        rstd = sb("rstd", [P, UNITS, ROWS, EXPERTS])
        vm_here = sb("vm_here", [P, UNITS, ROWS, EXPERTS])
        minus_half = sb("minus_half", [P, ROWS])
        eps = sb("eps", [P, 2, ROWS])
        ident = sb("ident", [P, P])
        ident16 = sb("ident16", [P, P], BF16)
        causal = p_ring[1][:, 0:P]
        causal16 = sb("causal16", [P, P], BF16)
        head_rows = sb("head_rows", [P, 8 + HEADS])
        rope_tab = sb("rope_tab", [P, 2 * HD1])
        rope = sb("rope", [P, 2, HD1])
        vec = sb("vec", [P, DC * 11])
        rows0 = sb("rows0", [P, 2, D])
        gates = sb("gates", [P, 4])
        tgates = sb("tgates", [P, 4])
        tt = sb("tt", [P, 2, B], I32)
        vm = sb("vm", [P, B, EXPERTS])
        media = p_ring[2][0:1, :].bitcast(U8)
        media16 = sb("media16", [1, B, P], BF16)
        ones16 = sb("ones16", [1, P], BF16)
        pos_i = pT_ring[0][:, 0:P].bitcast(I32)
        pos_f = pT_ring[1][:, 0:2 * P].rearrange("p (a t) -> p a t", a=2)
        pos_hot = p_ring[0][:, 0:P]
        token = sb("token", [P, 1])
        ps = [ctx.enter_context(nc.psum_tensor(f"bank{k}", [P, BANK], F32)) for k in range(BANKS)]

        silu = [o[i][:, 0:BANK] for i in range(2)]

        def rot_of(u, b):
            both_ = (hT[u][:, 2048:3072], o[u][:, 1024:2048])[b]
            return both_[:, 0:BANK], both_[:, BANK:2 * BANK]

        def qk_of(u, b):
            return o[u][:, b * BANK:(b + 1) * BANK]

        def weight(buf, table, name):
            at, chunks, width = table[name]
            return buf[:, at:at + chunks * width].rearrange("p (c n) -> p c n", c=chunks)

        def head_width(kind):
            return {"self": HD1, "cross": HDC, "media": HD2}[kind]

        def v_view(kind, u):
            w = head_width(kind) + 1
            at = ROWS * HEADS * (HD1 + 1) if kind == "cross" else 0
            return v[u][:, at:at + ROWS * HEADS * w].rearrange("p (b h w) -> p b h w", b=ROWS, h=HEADS)

        class View:
            pass

        views = []
        for u in range(UNITS):
            w = View()
            h = hT[u]
            w.qT1 = h[:, 0:512].rearrange("p (b c t) -> p b c t", b=ROWS, c=DC)
            w.oT1 = h[:, 512:1536].rearrange("p (b e c t) -> p b e c t", b=ROWS, e=EXPERTS, c=DC)
            w.cqT = h[:, 1536:1792]
            w.coT = h[:, 1792:2048]
            w.qT2 = h[:, 0:IC * TOK].rearrange("p (m t) -> p m t", m=IC)
            w.oT2 = w.qT2
            w.h1 = h[:, :].rearrange("p (e f t) -> p e f t", e=EXPERTS, f=F1C)
            w.h2 = h[:, 0:F2C * TOK].rearrange("p (f t) -> p f t", f=F2C)
            w.k1 = kbd[u][:, :].rearrange("p (b h t) -> p b h t", b=ROWS, h=HEADS)
            w.k2 = kbd[u][:, :].rearrange("p (m b s t) -> p m b s t", m=IC, b=ROWS, s=2)
            w.x0 = o[u][:, 0:512].rearrange("p (b d) -> p b d", b=ROWS)
            w.mix = o[u][:, 512:1024].rearrange("p (b d) -> p b d", b=ROWS)
            w.z = o[u][:, 1024:1536].rearrange("p (b d) -> p b d", b=ROWS)
            w.fused = o[u][:, 1536:2048].rearrange("p (b d) -> p b d", b=ROWS)
            w.xT0 = h[:, 0:512].rearrange("p (c t) -> p c t", c=DC)
            w.memT = h[:, 512:1024].rearrange("p (c t) -> p c t", c=DC)
            w.mixT = h[:, 1024:1536].rearrange("p (b c t) -> p b c t", b=ROWS, c=DC)
            w.mem = v[u][:, 0:512].rearrange("p (b d) -> p b d", b=ROWS)
            views.append(w)

        def out_of(kind, u, b, g):
            w = head_width(kind)
            at = {"self": b * D, "cross": 512 + b * P, "media": b * INNER}[kind] + (1024 if kind != "media" else 0)
            return o[u][:, at + g * QUAD * w:at + (g + 1) * QUAD * w].rearrange("p (h w) -> p h w", w=w)

        def rows(it, u):
            return bass.ds(it * (UNITS * ROWS) + u * ROWS, ROWS)

        def row(it, u, b):
            return bass.ds(it * (UNITS * ROWS) + (u * ROWS + b), 1)

        def wait(eng, ph, it, step, event, back=0):
            eng.wait_ge(sems[step[0], event], ph.count(step, event, it, back))

        def settle(eng, name):
            eng.sem_inc(settled[name], 1)

        def phase_start(eng, ph):
            if ph.index:
                eng.wait_ge(sems["end", "done"], PRIME["end", "done"] + ph.base["end"])
            else:
                eng.wait_ge(primed, 1)

        def unit_free(eng, ph, it, u):
            wait(eng, ph, it, ("end", u), "done", back=1)

        def final(ph, s):
            return [t for t in ph.steps if t[0] in (LAST | {"out0"}) and t[1] == s[1]][-1]

        VECTOR_SETUP = 17
        SCALAR_SETUP = 1
        ATT_LOADS = {1: 1, 3: 2, 5: 3}
        FF_LOADS = {0: 1, 2: 2, 4: 3, 6: 4}
        CTX_BEFORE = {0: 0, 1: ITERS, 3: 2 * ITERS, 5: 3 * ITERS}

        block = ctx.enter_context(nc.Block())

        @block.sync
        def _(sp):
            for dst, src in ((rope_tab, "rope_tab"), (token, "token"), (pos_i, "pos"), (tt, "tt"), (media, "media"),
                             (gates, "gates"), (ident, "ident"), (causal, "causal"), (head_rows, "head_rows"),
                             (vec, "vec"), (rows0, "rows0")):
                sp.dma_start(dst[:, :] if len(dst.shape) == 2 else dst[:, :, :], dram[src]).then_inc(consts_in, 16)
            sp.dma_start(w_ff[:, 0:W0_COLS], dram["w0"]).then_inc(weights_ff, 16)
            sp.dma_start(w_att[:, 0:W1A_COLS], dram["w1a"]).then_inc(weights_att, 16)
            for (kind, event), n in PRIME.items():
                if n:
                    sp.sem_inc(sems[kind, event], n)
            sp.sem_inc(primed, 1)

            def load_ctx(ph, it, u, reader):
                wait(sp, ph, it, reader, "mm", back=1)
                sp.dma_start(ctxT[u][:, :].rearrange("p (b t) -> p b t", b=ROWS),
                             dram["ctxT"][:, rows(it, u), :]).then_inc(ctx_in[u], 16)

            for ph in PHASES:
                phase_start(sp, ph)
                if ph.index == 1:
                    sp.dma_start(w_ff[:, 0:W1B_COLS], dram["w1b"]).then_inc(weights_ff, 16)
                if ph.index in (2, 4):
                    sp.dma_start(w_att[:, 0:W2A_COLS], dram["w2a" if ph.index == 2 else "w3a"])\
                      .then_inc(weights_att, 16)
                if ph.index in (3, 5):
                    sp.dma_start(w_ff[:, 0:W2B_COLS], dram["w2b" if ph.index == 3 else "w3b"])\
                      .then_inc(weights_ff, 16)
                if ph.index in (2, 4):
                    continue
                with sp.Fori(0, ITERS) as it:
                    for u in range(UNITS):
                        if ph.index == 0:
                            unit_free(sp, ph, it, u)
                            sp.dma_start(views[u].x0, dram["x"][:, rows(it, u), :]).then_inc(x_in[u], 16)
                            sp.dma_start(views[u].xT0, dram["xT"][:, :, bass.ds(it * (UNITS * TOK) + u * TOK, TOK)])\
                              .then_inc(xT_in[u], 16)
                            load_ctx(ph, it, u, ("mem", u))
                        elif ph.index == 1:
                            load_ctx(ph, it, u, ("cv", u))
                        elif ph.index in (3, 5):
                            load_ctx(ph, it, u, ("v2", u, ROWS - 1, 1))
                        else:
                            wait(sp, ph, it, ("end", u), "done")
                            sp.dma_start(out[:, rows(it, u), :], x_all[:, rows(it, u), :]).then_inc(out_done, 16)
            sp.wait_ge(out_done, 16 * ITERS * UNITS)

        @block.tensor
        def _(pe):
            def mm(dst, lhsT, rhs, first, last):
                return pe.matmul(dst, lhsT, rhs, start=first, stop=last)

            def done(ins, s):
                ins.then_inc(sems[s[0], "mm"], 1)

            def turn(s, dst_of, blocks):
                bank = ps[dst_of]
                for i, src in enumerate(blocks):
                    t = pe.transpose(bank[:, i * P:(i + 1) * P], src, ident[:])
                done(t, s)

            def memT(ph, it, s, bank):
                u = s[1]
                pe.wait_ge(ctx_in[u], it * 16 + 16)
                w = weight(w_ff, W0, "mem")
                for c in range(DC):
                    t = mm(bank[:, c * TOK:(c + 1) * TOK], w[:, 0, c * P:(c + 1) * P], ctxT[u][:, :], True, True)
                done(t, s)

            def mem(ph, it, s, bank):
                u = s[1]
                w = weight(w_ff, W0, "mem")
                for b in range(ROWS):
                    t = mm(bank[:, b * D:(b + 1) * D], ctxT[u][:, b * P:(b + 1) * P], w[:, 0, :], True, True)
                done(t, s)

            def score0(ph, it, s, bank):
                u = s[1]
                w = views[u]
                pe.wait_ge(xT_in[u], it * 16 + 16)
                wait(pe, ph, it, ("memT", u), "copied")
                for b in range(ROWS):
                    for c in range(DC):
                        t = mm(bank[:, b * P:(b + 1) * P], w.xT0[:, c, b * P:(b + 1) * P],
                               w.memT[:, c, b * P:(b + 1) * P], c == 0, c == DC - 1)
                done(t, s)

            def turn0(ph, it, s, bank):
                wait(pe, ph, it, ("score0", s[1]), "exp")
                turn(s, ph.bank[s], [p_ring[s[1]][:, b * P:(b + 1) * P] for b in range(ROWS)])

            def mix0(ph, it, s, bank):
                u = s[1]
                wait(pe, ph, it, ("turn0", u), "copied")
                wait(pe, ph, it, ("mem", u), "copied")
                for b in range(ROWS):
                    t = mm(bank[:, b * D:(b + 1) * D], pT_ring[u][:, b * P:(b + 1) * P], views[u].mem[:, b, :], True, True)
                done(t, s)

            def mixT(ph, it, s, bank):
                u = s[1]
                wait(pe, ph, it, ("mix0", u), "normed")
                turn(s, ph.bank[s], [views[u].mix[:, b, c * P:(c + 1) * P] for b in range(ROWS) for c in range(DC)])

            def gate0(ph, it, s, bank):
                u = s[1]
                wg = weight(w_ff, W0, "gate")
                wait(pe, ph, it, ("mixT", u), "copied")
                for b in range(ROWS):
                    for c in range(2 * DC):
                        lhsT = views[u].xT0[:, c, b * P:(b + 1) * P] if c < DC else views[u].mixT[:, b, c - DC, :]
                        t = mm(bank[:, b * D:(b + 1) * D], lhsT, wg[:, c, :], c == 0, c == 2 * DC - 1)
                done(t, s)

            def expertT(ph, it, s, bank):
                u, e = s[1], 0 if s[0] == "xvT" else 1
                wait(pe, ph, it, ("norm_self" if ph.index == 1 else "norm_mlp", u), "xn")
                turn(s, ph.bank[s], [xn[u][:, b, e, c * P:(c + 1) * P] for c in range(DC) for b in range(ROWS)])

            def qk(ph, it, s, bank):
                u, b = s[1:]
                wait(pe, ph, it, ("xvT", u), "copied")
                wait(pe, ph, it, ("xlT", u), "copied")
                for e in range(EXPERTS):
                    for c in range(DC):
                        t = mm(bank[:, :], xT[u][:, e, c, b * P:(b + 1) * P],
                               weight(w_att, W1A, f"qkv{e}")[:, c, 0:2 * D], e + c == 0, e + c == 2)
                done(t, s)

            def v1(ph, it, s, bank):
                u = s[1]
                for b in range(ROWS):
                    for e in range(EXPERTS):
                        for c in range(DC):
                            t = mm(bank[:, b * D:(b + 1) * D], xT[u][:, e, c, b * P:(b + 1) * P],
                                   weight(w_att, W1A, f"qkv{e}")[:, c, 2 * D:3 * D], e + c == 0, e + c == 2)
                done(t, s)

            def qkT(ph, it, s, bank):
                u, at = s[1], 0 if s[0] == "qT" else D
                wait(pe, ph, it, ("qk", u, ROWS - 1), "sum")
                turn(s, ph.bank[s], [qk_of(u, b)[:, at + c * P:at + (c + 1) * P] for b in range(ROWS) for c in range(DC)])

            def scores(ph, it, s, bank):
                kind, i, u, b, g = s[1:]
                w = views[u]
                heads = slice(g * QUAD, (g + 1) * QUAD)
                if kind == "self":
                    wait(pe, ph, it, ("qT", u), "copied")
                    wait(pe, ph, it, ("kT", u), "copied")
                    mm(bank[:, :], ident16[:, :], causal16[:, :].unsqueeze(1).broadcast_to([P, QUAD, P]), True, False)
                    t = mm(bank[:, :], w.qT1[:, b, g // 2, :], w.k1[:, b, heads, :], False, True)
                elif kind == "cross":
                    wait(pe, ph, it, ("cq", u), "copied")
                    wait(pe, ph, it, ("ck", u), "copied")
                    t = mm(bank[:, :], w.cqT[:, b * P:(b + 1) * P], w.k1[:, b, heads, :], True, True)
                else:
                    wait(pe, ph, it, ("q2", u, g), "copied")
                    wait(pe, ph, it, ("k2", u, g), "copied")
                    settle(pe, "tensor")
                    mm(bank[:, :], ones16[0:1, :], media16[0:1, row(it, u, b), :].broadcast_to([1, QUAD, P]), True, False)
                    for m in (2 * g, 2 * g + 1):
                        half = (m % 2) * 2 * P
                        t = mm(bank[:, half:half + 2 * P], w.qT2[:, m, b * P:(b + 1) * P], w.k2[:, m, b, :, :],
                               False, m % 2 == 1)
                done(t, s)

            def turn_p(ph, it, s, bank):
                i = s[2]
                wait(pe, ph, it, ("scores",) + s[1:], "exp")
                turn(s, ph.bank[s], [p_ring[i % P_RING][:, j * P:(j + 1) * P] for j in range(QUAD)])

            def values(ph, it, s, bank):
                kind, i, u, b, g = s[1:]
                wait(pe, ph, it, ("turn",) + s[1:], "copied")
                if (b, g) == (0, 0):
                    wait(pe, ph, it, {"self": ("v1", u), "cross": ("cv", u), "media": ("v2", u, ROWS - 1, 1)}[kind], "copied")
                w = head_width(kind) + 1
                for j in range(QUAD):
                    t = mm(bank[:, j * w:(j + 1) * w], pT_ring[i % P_RING][:, j * P:(j + 1) * P],
                           v_view(kind, u)[:, b, g * QUAD + j, :], True, True)
                done(t, s)

            def maskedT(ph, it, s, bank):
                u, b = s[1:]
                wait(pe, ph, it, s, "masked")
                turn(s, ph.bank[s], [xn[u][:, b, e, c * P:(c + 1) * P] for e in range(EXPERTS) for c in range(DC)])

            def dense(ph, it, s, bank):
                u = s[1]
                for b in range(ROWS):
                    wait(pe, ph, it, ("maskedT", u, b), "copied")
                    for e in range(EXPERTS):
                        for c in range(DC):
                            t = mm(bank[:, b * D:(b + 1) * D], views[u].oT1[:, b, e, c, :],
                                   weight(w_att, W1A, f"dense{e}")[:, c, :], e + c == 0, e + c == 2)
                done(t, s)

            def nT(ph, it, s, bank):
                u = s[1]
                wait(pe, ph, it, ({1: "norm_cross", 3: "norm_q", 5: "norm_q", 4: "norm_ff", 6: "norm_ff"}[ph.index], u), "xn")
                turn(s, ph.bank[s], [xn[u][:, b, 0, c * P:(c + 1) * P] for c in range(DC) for b in range(ROWS)])

            def cq(ph, it, s, bank):
                u = s[1]
                wait(pe, ph, it, ("nT", u), "copied")
                for c in range(DC):
                    t = mm(bank[:, 0:TOK], weight(w_att, W1A, "cq")[:, c, :], xT[u][:, 0, c, :], c == 0, c == DC - 1)
                done(t, s)

            def ctx_here(ph, it, u):
                pe.wait_ge(ctx_in[u], it * 16 + 16 * (CTX_BEFORE[ph.index] + 1))

            def ck(ph, it, s, bank):
                u = s[1]
                ctx_here(ph, it, u)
                done(mm(bank[:, 0:TOK], weight(w_att, W1A, "ckv")[:, 0, 0:P], ctxT[u][:, :], True, True), s)

            def cv(ph, it, s, bank):
                u = s[1]
                for b in range(ROWS):
                    t = mm(bank[:, b * P:(b + 1) * P], ctxT[u][:, b * P:(b + 1) * P],
                           weight(w_att, W1A, "ckv")[:, 0, P:2 * P], True, True)
                done(t, s)

            def coT(ph, it, s, bank):
                u = s[1]
                wait(pe, ph, it, ("values", "cross", UNITS * ROWS * GROUPS - 1 - (UNITS - 1 - u) * ROWS * GROUPS,
                                  u, ROWS - 1, GROUPS - 1), "normed")
                turn(s, ph.bank[s], [o[u][:, 1536 + b * P:1536 + (b + 1) * P] for b in range(ROWS)])

            def cdense(ph, it, s, bank):
                u = s[1]
                wait(pe, ph, it, ("coT", u), "copied")
                for b in range(ROWS):
                    t = mm(bank[:, b * D:(b + 1) * D], views[u].coT[:, b * P:(b + 1) * P],
                           weight(w_att, W1A, "cdense")[:, 0, :], True, True)
                done(t, s)

            def hidden1(ph, it, s, bank):
                u, e, j = s[1:]
                wait(pe, ph, it, ("xvT" if e == 0 else "xlT", u), "copied")
                w = weight(w_ff, W1B, ("gate" if s[0] == "gate1" else "up") + str(e))
                for k in range(2):
                    f = 2 * j + k
                    for c in range(DC):
                        t = mm(bank[:, k * TOK:(k + 1) * TOK], w[:, c, f * P:(f + 1) * P], xT[u][:, e, c, :],
                               c == 0, c == DC - 1)
                done(t, s)

            def down(ph, it, s, bank):
                u = s[1]
                wait(pe, ph, it, ("up1", u, EXPERTS - 1, F1C // 2 - 1), "h")
                for b in range(ROWS):
                    for e in range(EXPERTS):
                        for f in range(F1C):
                            t = mm(bank[:, b * D:(b + 1) * D], views[u].h1[:, e, f, b * P:(b + 1) * P],
                                   weight(w_ff, W1B, f"down{e}")[:, f, :], e + f == 0, e == 1 and f == F1C - 1)
                done(t, s)

            def q2(ph, it, s, bank):
                u, j = s[1:]
                wait(pe, ph, it, ("nT", u), "copied")
                for k in range(2):
                    m = 2 * j + k
                    for c in range(DC):
                        t = mm(bank[:, k * TOK:(k + 1) * TOK], weight(w_att, W2A, "q")[:, c, m * P:(m + 1) * P],
                               xT[u][:, 0, c, :], c == 0, c == DC - 1)
                done(t, s)

            def k2(ph, it, s, bank):
                u, j = s[1:]
                if j == 0:
                    ctx_here(ph, it, u)
                for k in range(2):
                    m = 2 * j + k
                    t = mm(bank[:, k * TOK:(k + 1) * TOK], weight(w_att, W2A, "kv")[:, 0, m * P:(m + 1) * P],
                           ctxT[u][:, :], True, True)
                done(t, s)

            def v2(ph, it, s, bank):
                u, b, j = s[1:]
                at = INNER + j * BANK
                done(mm(bank[:, :], ctxT[u][:, b * P:(b + 1) * P], weight(w_att, W2A, "kv")[:, 0, at:at + BANK],
                        True, True), s)

            def oT2(ph, it, s, bank):
                u, b, j = s[1:]
                i = (u * ROWS + b) * GROUPS + GROUPS - 1
                wait(pe, ph, it, ("values", "media", i, u, b, GROUPS - 1), "normed")
                turn(s, ph.bank[s], [o[u][:, b * INNER + m * P:b * INNER + (m + 1) * P] for m in range(4 * j, 4 * j + 4)])

            def wo(ph, it, s, bank):
                u = s[1]
                wait(pe, ph, it, ("oT2", u, ROWS - 1, 1), "copied")
                for b in range(ROWS):
                    for m in range(IC):
                        t = mm(bank[:, b * D:(b + 1) * D], views[u].oT2[:, m, b * P:(b + 1) * P],
                               weight(w_att, W2A, "o")[:, m, :], m == 0, m == IC - 1)
                done(t, s)

            def w1(ph, it, s, bank):
                u, j = s[1:]
                wait(pe, ph, it, ("nT", u), "copied")
                for k in range(2):
                    f = 2 * j + k
                    for c in range(DC):
                        t = mm(bank[:, k * TOK:(k + 1) * TOK], weight(w_ff, W2B, "w1")[:, c, f * P:(f + 1) * P],
                               xT[u][:, 0, c, :], c == 0, c == DC - 1)
                done(t, s)

            def w2(ph, it, s, bank):
                u = s[1]
                wait(pe, ph, it, ("w1", u, F2C // 2 - 1), "gelu")
                for b in range(ROWS):
                    for f in range(F2C):
                        t = mm(bank[:, b * D:(b + 1) * D], views[u].h2[:, f, b * P:(b + 1) * P],
                               weight(w_ff, W2B, "w2")[:, f, :], f == 0, f == F2C - 1)
                done(t, s)

            stages = dict(memT=memT, mem=mem, score0=score0, turn0=turn0, mix0=mix0, mixT=mixT, gate0=gate0,
                          xvT=expertT, xlT=expertT, qk=qk, v1=v1, qT=qkT, kT=qkT, scores=scores, turn=turn_p,
                          values=values, maskedT=maskedT, dense=dense, nT=nT, cq=cq, ck=ck, cv=cv, coT=coT,
                          cdense=cdense, gate1=hidden1, up1=hidden1, down=down, q2=q2, k2=k2, v2=v2, oT2=oT2,
                          wo=wo, w1=w1, w2=w2)

            pe.wait_ge(consts_in, 16 * 11)
            pe.wait_ge(setup_v, 5)
            pe.matmul(ps[0][:, 0:2 * HD1], pos_hot, rope_tab[:], start=True, stop=True).then_inc(setup_pe, 1)
            pe.wait_ge(setup_v, VECTOR_SETUP)

            for ph in PHASES:
                phase_start(pe, ph)
                if ph.index in ATT_LOADS:
                    pe.wait_ge(weights_att, 16 * ATT_LOADS[ph.index])
                    if ph.index < 5:
                        pe.wait_ge(zeroed, 1 if ph.index == 1 else 2)
                else:
                    pe.wait_ge(weights_ff, 16 * FF_LOADS[ph.index])
                with pe.Fori(0, ITERS) as it:
                    for s in ph.steps:
                        if s in ph.bank:
                            prev, back = ph.held_by[s]
                            if prev[0] in LAST:
                                prev = ("end", prev[1])
                            wait(pe, ph, it, prev, EMPTIED[prev[0]], back)
                            stages[s[0]](ph, it, s, ps[ph.bank[s]])

        @block.vector
        def _(dve):
            def done(ins, s, event):
                ins.then_inc(sems[s[0], event], 1)

            def copy(ph, it, s, dst, src):
                wait(dve, ph, it, s, "mm")
                done(dve.tensor_copy(dst, src), s, "copied")

            def mem(ph, it, s, bank):
                copy(ph, it, s, views[s[1]].mem, bank[:, :].rearrange("p (b d) -> p b d", b=ROWS))

            def score0(ph, it, s, bank):
                u = s[1]
                wait(dve, ph, it, s, "mm")
                done(dve.tensor_reduce(nmax[:, u, 0:ROWS], bank[:, 0:TOK].rearrange("p (b t) -> p b t", b=ROWS),
                                       AX_X, ALU.max, negate=True), s, "max")

            def mix0(ph, it, s, bank):
                u = s[1]
                wait(dve, ph, it, ("score0", u), "exp")
                done(dve.reciprocal(rinv0[:, u, :], rsum0[:, u, :]), s, "rinv")
                wait(dve, ph, it, s, "mm")
                wait(dve, ph, it, s, "rinv")
                done(dve.tensor_tensor(views[u].mix, bank[:, :].rearrange("p (b d) -> p b d", b=ROWS),
                                       rinv0[:, u, :].unsqueeze(2).broadcast_to([P, ROWS, D]), ALU.mult), s, "normed")

            def gate0(ph, it, s, bank):
                wait(dve, ph, it, s, "mm")
                done(dve.tensor_tensor(views[s[1]].z, bank[:, :].rearrange("p (b d) -> p b d", b=ROWS),
                                       rows0[:, 0:1, :].broadcast_to([P, ROWS, D]), ALU.add), s, "biased")

            def spread(ph, it, s, of):
                u = s[1]
                settle(dve, "vector")
                for b in range(ROWS):
                    t = dve.bn_stats(stats[:, u, b, :], of(b))
                done(t, s, "stats")
                wait(dve, ph, it, s, "stats")
                settle(dve, "vector")
                for b in range(ROWS):
                    t = dve.bn_aggr(aggr[:, u, b, :], stats[:, u, b, :])
                done(t, s, "aggr")

            def out0(ph, it, s, bank):
                u = s[1]
                w = views[u]
                wait(dve, ph, it, s, "tanh")
                done(dve.scalar_tensor_tensor(out=w.z, in0=w.z, scalar=1.0, in1=w.mix, op0=ALU.add, op1=ALU.mult),
                     s, "gated")
                wait(dve, ph, it, s, "gated")
                dve.wait_ge(x_in[u], it * 16 + 16)
                done(dve.scalar_tensor_tensor(out=w.fused, in0=w.z, scalar=0.5, in1=w.x0, op0=ALU.mult, op1=ALU.add),
                     s, "fused")
                wait(dve, ph, it, s, "fused")
                spread(ph, it, s, lambda b: w.fused[:, b, :])

            def norm(ph, it, s, bank):
                u = s[1]
                if s[0] == "norm_cross":
                    wait(dve, ph, it, ("dense", u), "added")
                else:
                    unit_free(dve, ph, it, u)
                spread(ph, it, s, lambda b: x_all[:, row(it, u, b), :])
                wait(dve, ph, it, s, "rstd")
                for b in range(ROWS):
                    x_b = x_all[:, row(it, u, b), :]
                    if s[0] in ("norm_self", "norm_mlp"):
                        for e in range(EXPERTS):
                            t = dve.tensor_scalar(xn[u][:, b, e:e + 1, :], x_b, rstd[:, u, b, e:e + 1], None, ALU.mult)
                    elif s[0] == "norm_cross":
                        t = dve.tensor_scalar(xn[u][:, b, 0:1, :], x_b, rstd[:, u, b, 0:1], None, ALU.mult)
                    else:
                        t = dve.tensor_scalar(xn[u][:, b, 0:1, :], x_b, aggr[:, u, b, 0:1], rstd[:, u, b, 0:1],
                                              ALU.subtract, ALU.mult)
                done(t, s, "xn")

            def qk(ph, it, s, bank):
                u, b = s[1:]
                r = rot_of(u, b)
                wait(dve, ph, it, s, "mm")
                heads = bank[:, :].rearrange("p (h d) -> p h d", d=HD1)
                half = HD1 // 2
                by_cos = r[0][:, :].rearrange("p (h d) -> p h d", d=HD1)
                by_sin = r[1][:, :].rearrange("p (h d) -> p h d", d=HD1)
                n = 2 * HEADS
                dve.tensor_tensor(by_cos, heads, rope[:, 0:1, :].broadcast_to([P, n, HD1]), ALU.mult)
                dve.tensor_tensor(by_sin[:, :, 0:half], heads[:, :, half:HD1],
                                  rope[:, 1:2, 0:half].broadcast_to([P, n, half]), ALU.mult)
                done(dve.tensor_tensor(by_sin[:, :, half:HD1], heads[:, :, 0:half],
                                       rope[:, 1:2, half:HD1].broadcast_to([P, n, half]), ALU.mult), s, "halves")

            def kT(ph, it, s, bank):
                u = s[1]
                wait(dve, ph, it, s, "mm")
                k = P // HD1
                for b in range(ROWS):
                    t = dve.tensor_tensor(
                        views[u].k1[:, b, :, :].rearrange("p (c h) t -> p c h t", c=DC),
                        bank[:, b * D:(b + 1) * D].rearrange("p (c t) -> p c t", c=DC).unsqueeze(2).broadcast_to([P, DC, k, P]),
                        head_rows[:, 0:k].unsqueeze(1).unsqueeze(3).broadcast_to([P, DC, k, P]), ALU.mult)
                done(t, s, "copied")

            def ck(ph, it, s, bank):
                u = s[1]
                wait(dve, ph, it, s, "mm")
                for b in range(ROWS):
                    t = dve.tensor_tensor(
                        views[u].k1[:, b, :, :], bank[:, b * P:(b + 1) * P].unsqueeze(1).broadcast_to([P, HEADS, P]),
                        head_rows[:, 8:8 + HEADS].unsqueeze(2).broadcast_to([P, HEADS, P]), ALU.mult)
                done(t, s, "copied")

            def scores(ph, it, s, bank):
                i = s[2]
                wait(dve, ph, it, s, "mm")
                done(dve.tensor_reduce(nmax[:, i % (P_RING + 1), :], bank[:, :].rearrange("p (h t) -> p h t", h=QUAD),
                                       AX_X, ALU.max, negate=True), s, "max")

            def turn(ph, it, s, bank):
                copy(ph, it, s, pT_ring[s[2] % P_RING][:, :], bank[:, :])

            def values(ph, it, s, bank):
                kind, i, u, b, g = s[1:]
                w = head_width(kind) + 1
                r = bank[:, 0:QUAD * w].rearrange("p (h w) -> p h w", w=w)
                wait(dve, ph, it, s, "mm")
                done(dve.reciprocal(rinv[:, i % 2, :], r[:, :, w - 1]), s, "rinv")
                wait(dve, ph, it, s, "rinv")
                done(dve.tensor_tensor(out_of(kind, u, b, g), r[:, :, 0:w - 1],
                                       rinv[:, i % 2, :].unsqueeze(2).broadcast_to([P, QUAD, w - 1]), ALU.mult),
                     s, "normed")

            def dense(ph, it, s, bank):
                u = s[1]
                wait(dve, ph, it, s, "mm")
                x_u = x_all[:, rows(it, u), :]
                done(dve.tensor_tensor(x_u, bank[:, :].rearrange("p (b d) -> p b d", b=ROWS), x_u, ALU.add), s, "added")

            def up1(ph, it, s, bank):
                u, e, j = s[1:]
                wait(dve, ph, it, ("gate1", u, e, j), "silu")
                wait(dve, ph, it, s, "mm")
                done(dve.tensor_tensor(views[u].h1[:, e, 2 * j:2 * j + 2, :], bank[:, :].rearrange("p (f t) -> p f t", f=2),
                                       silu[ph.place[s] % 2].rearrange("p (f t) -> p f t", f=2), ALU.mult), s, "h")

            def k2(ph, it, s, bank):
                u, j = s[1:]
                wait(dve, ph, it, s, "mm")
                for h in range(2):
                    part = slice(h * HD2, (h + 1) * HD2)
                    t = dve.tensor_copy(views[u].k2[part, 2 * j:2 * j + 2, :, h, :],
                                        bank[part, :].rearrange("p (m b t) -> p m b t", m=2, b=ROWS))
                done(t, s, "copied")

            def end(ph, it, s, bank):
                u = s[1]
                x_u = x_all[:, rows(it, u), :]
                if ph.index == 0:
                    wait(dve, ph, it, ("out0", u), "rstd")
                    for b in range(ROWS):
                        t = dve.scalar_tensor_tensor(out=x_all[:, row(it, u, b), :], in0=views[u].fused[:, b:b + 1, :],
                                                     scalar=rstd[:, u, b, 0:1], in1=rows0[:, 1:2, :],
                                                     op0=ALU.mult, op1=ALU.mult)
                    return done(t, s, "done")
                job = final(ph, s)
                wait(dve, ph, it, job, "mm")
                r = ps[ph.bank[job]][:, :].rearrange("p (b d) -> p b d", b=ROWS)
                if ph.layer == 1:
                    t = dve.tensor_tensor(x_u, r, x_u, ALU.add)
                else:
                    n = {("wo", 2): 0, ("w2", 2): 1, ("wo", 3): 2, ("w2", 3): 3}[job[0], ph.layer]
                    t = dve.scalar_tensor_tensor(out=x_u, in0=r, scalar=tgates[:, n:n + 1], in1=x_u,
                                                 op0=ALU.mult, op1=ALU.add)
                done(t, s, "done")

            stages = dict(mem=mem, score0=score0, mix0=mix0, gate0=gate0, out0=out0, norm_self=norm, norm_cross=norm,
                          norm_mlp=norm, norm_q=norm, norm_ff=norm, qk=qk, kT=kT, ck=ck, scores=scores, turn=turn,
                          values=values, dense=dense, up1=up1, k2=k2, end=end)

            dve.wait_ge(consts_in, 16 * 11)
            dve.tensor_copy(pos_f[:, 0, :], pos_i[:, :]).then_inc(setup_v, 1)
            dve.wait_ge(setup_v, 1)
            dve.tensor_scalar(pos_f[:, 1, :], pos_f[:, 0, :], 0.0, float(P), ALU.is_lt, ALU.mult).then_inc(setup_v, 1)
            dve.wait_ge(setup_v, 2)
            dve.tensor_tensor(pos_f[:, 0, :], pos_f[:, 0, :], pos_f[:, 1, :], ALU.add).then_inc(setup_v, 1)
            dve.wait_ge(setup_v, 3)
            dve.tensor_scalar(pos_f[:, 1, :], pos_f[:, 0, :], 0.0, float(P - 1), ALU.max, ALU.min).then_inc(setup_v, 1)
            dve.wait_ge(setup_v, 4)
            dve.tensor_scalar(pos_hot, pos_f[:, 1, :], token[:, 0:1], None, ALU.is_equal).then_inc(setup_v, 1)
            dve.tensor_scalar(vm[:, :, 0], tt[:, 0, :], 1.0, None, ALU.is_equal).then_inc(setup_v, 1)
            dve.tensor_scalar(vm[:, :, 1], tt[:, 1, :], 1.0, None, ALU.is_equal).then_inc(setup_v, 1)
            dve.wait_ge(setup_v, 7)
            dve.tensor_tensor(vm[:, :, 0], vm[:, :, 0], vm[:, :, 1], ALU.mult).then_inc(setup_v, 1)
            dve.wait_ge(setup_v, 8)
            dve.tensor_scalar(vm[:, :, 1], vm[:, :, 0], -1.0, 1.0, ALU.mult, ALU.add).then_inc(setup_v, 1)
            dve.tensor_scalar(media16[:, :, :], media[:, :].rearrange("p (b t) -> p b t", b=B), 0.0, MASKED,
                              ALU.is_equal, ALU.mult).then_inc(setup_v, 1)
            dve.memset(ones16[:, :], 1.0).then_inc(setup_v, 1)
            dve.tensor_copy(ident16[:, :], ident[:, :]).then_inc(setup_v, 1)
            dve.tensor_copy(causal16[:, :], causal[:, :]).then_inc(setup_v, 1)
            dve.memset(minus_half[:, :], -0.5).then_inc(setup_v, 1)
            dve.memset(eps[:, 0, :], EPS_RMS).then_inc(setup_v, 1)
            dve.memset(eps[:, 1, :], EPS_LN).then_inc(setup_v, 1)
            dve.wait_ge(setup_pe, 1)
            dve.tensor_copy(rope[:, :, :], ps[0][:, 0:2 * HD1].rearrange("p (a d) -> p a d", a=2)).then_inc(setup_v, 1)
            dve.wait_ge(setup_v, VECTOR_SETUP)
            dve.wait_ge(setup_a, SCALAR_SETUP)

            for ph in PHASES:
                phase_start(dve, ph)
                if ph.index == 3:
                    dve.wait_ge(zeroed, 2)
                with dve.Fori(0, ITERS) as it:
                    for s in ph.steps:
                        if s[0] in stages:
                            stages[s[0]](ph, it, s, ps[ph.bank[s]] if s in ph.bank else None)

        @block.scalar
        def _(act):
            def done(ins, s, event):
                ins.then_inc(sems[s[0], event], 1)

            def copy(ph, it, s, dst, src, scale=1.0, event="copied", func=ACT.Copy):
                wait(act, ph, it, s, "mm")
                done(act.activation(dst, src, func, scale=scale), s, event)

            def memT(ph, it, s, bank):
                copy(ph, it, s, views[s[1]].memT, bank[:, :].rearrange("p (c t) -> p c t", c=DC), D ** -0.5)

            def score0(ph, it, s, bank):
                u = s[1]
                wait(act, ph, it, s, "max")
                for b in range(ROWS):
                    t = act.activation(p_ring[u][:, b * P:(b + 1) * P], bank[:, b * P:(b + 1) * P], ACT.Exp,
                                       bias=nmax[:, u, b:b + 1], accum_out=rsum0[:, u, b:b + 1])
                done(t, s, "exp")

            def turn0(ph, it, s, bank):
                copy(ph, it, s, pT_ring[s[1]][:, 0:TOK], bank[:, 0:TOK])

            def mixT(ph, it, s, bank):
                copy(ph, it, s, hT[s[1]][:, 1024:1536], bank[:, :])

            def out0(ph, it, s, bank):
                w = views[s[1]]
                wait(act, ph, it, ("gate0", s[1]), "biased")
                done(act.activation(w.z, w.z, ACT.Tanh, scale=0.5), s, "tanh")

            def expertT(ph, it, s, bank):
                u, e = s[1], 0 if s[0] == "xvT" else 1
                at = VEC["self_w" if ph.index == 1 else "mlp_w"]
                wait(act, ph, it, s, "mm")
                for c in range(DC):
                    t = act.activation(xT[u][:, e, c, :], bank[:, c * TOK:(c + 1) * TOK], ACT.Copy,
                                       scale=vec[:, at + c:at + c + 1])
                done(t, s, "copied")

            def v1(ph, it, s, bank):
                copy(ph, it, s, v_view("self", s[1])[:, :, :, 0:HD1],
                     bank[:, :].rearrange("p (b h d) -> p b h d", b=ROWS, h=HEADS))

            def qT(ph, it, s, bank):
                copy(ph, it, s, views[s[1]].qT1, bank[:, :].rearrange("p (b c t) -> p b c t", b=ROWS, c=DC), HD1 ** -0.5)

            def scores(ph, it, s, bank):
                i = s[2]
                wait(act, ph, it, s, "max")
                before, back = ph.earlier(("turn",) + s[1:], P_RING)
                wait(act, ph, it, before, "copied", back)
                for j in range(QUAD):
                    part = slice(j * P, (j + 1) * P)
                    t = act.activation(p_ring[i % P_RING][:, part], bank[:, part], ACT.Exp,
                                       bias=nmax[:, i % (P_RING + 1), j:j + 1])
                done(t, s, "exp")

            def maskedT(ph, it, s, bank):
                u, b = s[1:]
                copy(ph, it, s, views[u].oT1[:, b, :, :, :],
                     bank[:, :].rearrange("p (e c t) -> p e c t", e=EXPERTS, c=DC))

            def nT(ph, it, s, bank):
                u = s[1]
                wait(act, ph, it, s, "mm")
                for c in range(DC):
                    if ph.index == 1:
                        at = VEC["cross_w"] + c
                        t = act.activation(xT[u][:, 0, c, :], bank[:, c * TOK:(c + 1) * TOK], ACT.Copy,
                                           scale=vec[:, at:at + 1])
                    else:
                        name = "q" if ph.index in (3, 5) else "ff"
                        g, a = (VEC[f"{name}_{x}{ph.layer}"] + c for x in "gb")
                        t = act.activation(xT[u][:, 0, c, :], bank[:, c * TOK:(c + 1) * TOK], ACT.Identity,
                                           scale=vec[:, g:g + 1], bias=vec[:, a:a + 1])
                done(t, s, "copied")

            def cq(ph, it, s, bank):
                copy(ph, it, s, views[s[1]].cqT, bank[:, 0:TOK], HDC ** -0.5)

            def cv(ph, it, s, bank):
                copy(ph, it, s, v_view("cross", s[1])[:, :, :, 0:HDC],
                     bank[:, 0:TOK].rearrange("p (b h d) -> p b h d", b=ROWS, h=HEADS))

            def coT(ph, it, s, bank):
                copy(ph, it, s, views[s[1]].coT, bank[:, 0:TOK])

            def gate1(ph, it, s, bank):
                before, back = ph.earlier(s, 2)
                wait(act, ph, it, ("up1",) + before[1:], "h", back)
                copy(ph, it, s, silu[ph.place[s] % 2], bank[:, :], event="silu", func=ACT.Silu)

            def q2(ph, it, s, bank):
                u, j = s[1:]
                copy(ph, it, s, views[u].qT2[:, 2 * j:2 * j + 2, :], bank[:, :].rearrange("p (m t) -> p m t", m=2),
                     HD2 ** -0.5)

            def v2(ph, it, s, bank):
                u, b, j = s[1:]
                copy(ph, it, s, v_view("media", u)[:, b, j * 8:(j + 1) * 8, 0:HD2],
                     bank[:, :].rearrange("p (h d) -> p h d", d=HD2))

            def oT2(ph, it, s, bank):
                u, b, j = s[1:]
                copy(ph, it, s, views[u].oT2[:, 4 * j:4 * j + 4, b * P:(b + 1) * P],
                     bank[:, :].rearrange("p (m t) -> p m t", m=4))

            def w1(ph, it, s, bank):
                u, j = s[1:]
                copy(ph, it, s, views[u].h2[:, 2 * j:2 * j + 2, :], bank[:, :].rearrange("p (f t) -> p f t", f=2),
                     event="gelu", func=ACT.Gelu)

            stages = dict(memT=memT, score0=score0, turn0=turn0, mixT=mixT, out0=out0, xvT=expertT, xlT=expertT,
                          v1=v1, qT=qT, scores=scores, maskedT=maskedT, nT=nT, cq=cq, cv=cv, coT=coT, gate1=gate1,
                          q2=q2, v2=v2, oT2=oT2, w1=w1)

            act.wait_ge(consts_in, 16 * 11)
            act.activation(tgates[:, :], gates[:, :], ACT.Tanh).then_inc(setup_a, 1)
            for ph in PHASES:
                phase_start(act, ph)
                if ph.index in (1, 3):
                    act.wait_ge(zeroed, 1 if ph.index == 1 else 2)
                with act.Fori(0, ITERS) as it:
                    for s in ph.steps:
                        if s[0] in stages:
                            stages[s[0]](ph, it, s, ps[ph.bank[s]] if s in ph.bank else None)

        @block.gpsimd
        def _(pool):
            def done(ins, s, event):
                ins.then_inc(sems[s[0], event], 1)

            def to_rstd(ph, it, s, bank):
                u = s[1]
                rms = s[0] in ("out0", "norm_self", "norm_mlp", "norm_cross")
                experts = s[0] in ("norm_self", "norm_mlp")
                mean, var = aggr[:, u, :, 0], aggr[:, u, :, 1]
                wait(pool, ph, it, s, "aggr")
                if rms:
                    done(pool.tensor_tensor(ms[:, u, 0, :], mean, mean, ALU.mult), s, "square")
                    wait(pool, ph, it, s, "square")
                    done(pool.tensor_tensor(ms[:, u, 1, :], ms[:, u, 0, :], var, ALU.add), s, "mean")
                    wait(pool, ph, it, s, "mean")
                    var = ms[:, u, 1, :]
                done(pool.tensor_tensor(ms[:, u, 2, :], var, eps[:, 0 if rms else 1, :], ALU.add), s, "eps")
                if experts:
                    pool.tensor_copy(vm_here[:, u, :, :], vm[:, rows(it, u), :])
                wait(pool, ph, it, s, "eps")
                r = ms[:, u, 3, :] if experts else rstd[:, u, :, 0]
                done(pool.tensor_tensor(r, ms[:, u, 2, :], minus_half[:, :], ALU.pow), s, "pow" if experts else "rstd")
                if experts:
                    wait(pool, ph, it, s, "pow")
                    done(pool.tensor_tensor(rstd[:, u, :, :], ms[:, u, 3, :].unsqueeze(2).broadcast_to([P, ROWS, EXPERTS]),
                                            vm_here[:, u, :, :], ALU.mult), s, "rstd")

            def qk(ph, it, s, bank):
                u, b = s[1:]
                wait(pool, ph, it, s, "halves")
                done(pool.tensor_tensor(qk_of(u, b), *rot_of(u, b), ALU.add), s, "sum")

            def maskedT(ph, it, s, bank):
                u, b = s[1:]
                i = (u * ROWS + b) * GROUPS + GROUPS - 1
                wait(pool, ph, it, ("values", "self", i, u, b, GROUPS - 1), "normed")
                done(pool.tensor_tensor(xn[u][:, b, :, :],
                                        o[u][:, 1024 + b * D:1024 + (b + 1) * D].unsqueeze(1).broadcast_to([P, EXPERTS, D]),
                                        vm_here[:, u, b, :].unsqueeze(2).broadcast_to([P, EXPERTS, D]), ALU.mult),
                     s, "masked")

            stages = dict(out0=to_rstd, norm_self=to_rstd, norm_mlp=to_rstd, norm_cross=to_rstd, norm_q=to_rstd,
                          norm_ff=to_rstd, qk=qk, maskedT=maskedT)

            pool.wait_ge(setup_v, VECTOR_SETUP)
            for ph in PHASES:
                phase_start(pool, ph)
                if ph.index in (1, 3):
                    for u in range(UNITS):
                        for kind in (("self", "cross") if ph.index == 1 else ("media",)):
                            t = pool.memset(v_view(kind, u)[:, :, :, head_width(kind)], 1.0)
                        if ph.index == 3:
                            t = pool.memset(kbd[u][:, :], 0.0)
                    t.then_inc(zeroed, 1)
                with pool.Fori(0, ITERS) as it:
                    for s in ph.steps:
                        if s[0] in stages:
                            stages[s[0]](ph, it, s, None)



def by_chunk(w, rows_to=None):
    k, n = w.shape
    rows_to = rows_to or k
    if rows_to > k:
        w = np.concatenate([w, np.zeros((rows_to - k, n), w.dtype)])
    return w.reshape(rows_to // P, P, n).transpose(1, 0, 2).reshape(P, -1)


def wide(w, cols):
    return np.concatenate([w, np.zeros((w.shape[0], cols - w.shape[1]), w.dtype)], axis=1)


def kernel(**inputs):
    import concourse.bacc as bacc
    from concourse.bass_utils import run_bass_kernel_spmd

    a = {k: np.asarray(v) for k, v in inputs.items()}
    l0 = lambda n: a["L0_xattn_" + n]
    l1 = lambda n: a["L1_xattn_" + n]
    arrays = {
        "x": a["x"].transpose(1, 0, 2),
        "xT": a["x"].transpose(2, 0, 1).reshape(DC, P, B * P).transpose(1, 0, 2),
        "ctxT": a["ctx_1024"].transpose(2, 0, 1),
        "w0": np.concatenate([l0("W_mem").T, by_chunk(l0("W_gate").T)], axis=1),
        "rows0": np.broadcast_to(np.stack([l0("b_gate"), l0("norm_w")]), (P, 2, D)),
        "w1a": np.concatenate(
            [by_chunk(l1(n)) for n in ("v_qkv", "l_qkv", "v_dense", "l_dense", "cq_w", "ckv_w", "cdense_w")], axis=1),
        "w1b": np.concatenate(
            [by_chunk(wide(l1(n), F1C * P)) for n in ("v_gate", "v_up", "l_gate", "l_up")]
            + [by_chunk(l1(n), F1C * P) for n in ("v_down", "l_down")], axis=1),
    }
    for n in (2, 3):
        ln = lambda name: a[f"L{n}_xattn_{name}"]
        arrays[f"w{n}a"] = np.concatenate([by_chunk(ln("Wq")), ln("Wkv"), by_chunk(ln("Wo"))], axis=1)
        arrays[f"w{n}b"] = np.concatenate([by_chunk(ln("W1")), by_chunk(ln("W2"))], axis=1)
    vecs = [l1("ln_in_w"), l1("ln_post_cross_w"), l1("ln_post_attn_w")]
    for n in (2, 3):
        vecs += [a[f"L{n}_xattn_ln_{x}"] for x in ("q_g", "q_b", "ff_g", "ff_b")]
    arrays["vec"] = np.stack(vecs).reshape(-1, DC, P).transpose(2, 0, 1).reshape(P, -1)
    arrays["gates"] = np.broadcast_to(
        np.concatenate([a["L2_xattn_attn_gate"], a["L2_xattn_ff_gate"], a["L3_xattn_attn_gate"], a["L3_xattn_ff_gate"]]),
        (P, 4))
    kinds = a["mask_BxS_ik0"].T
    arrays["tt"] = np.stack([kinds, np.concatenate([kinds[1:], np.zeros((1, B), kinds.dtype)])], axis=1)
    arrays["media"] = a["mask_BxS2_bk0"].reshape(1, B * P)
    arrays["pos"] = np.broadcast_to(a["pos_1xS"], (P, P))
    f = np.float32
    inv = f(1.0) / f(ROPE_BASE) ** (np.arange(0, HD1, 2, dtype=f) / f(HD1))
    freq = np.outer(np.arange(P, dtype=f), inv).astype(f)
    arrays["rope_tab"] = np.concatenate([np.cos(freq), np.cos(freq), -np.sin(freq), np.sin(freq)], axis=1).astype(f)
    arrays["token"] = np.arange(P, dtype=f).reshape(P, 1)
    arrays["ident"] = np.eye(P, dtype=f)
    arrays["causal"] = np.where(np.tril(np.ones((P, P), bool)), f(0), f(MASKED))
    part = np.arange(P)[:, None]
    arrays["head_rows"] = np.concatenate(
        [part // HD1 == np.arange(P // HD1), part // HDC == np.arange(P // HDC)], axis=1).astype(f)

    nc = bacc.Bacc("TRN2", target_bir_lowering=False, num_devices=1)
    given, dram = {}, {}
    for name, array in arrays.items():
        array = np.ascontiguousarray(array)
        given[f"in_{name}"] = array
        dram[name] = nc.dram_tensor(f"in_{name}", array.shape, mybir.dt.from_np(array.dtype), kind="ExternalInput").ap()
    out = nc.dram_tensor("out", (P, B, D), F32, kind="ExternalOutput").ap()
    build(nc, dram, out)
    result = run_bass_kernel_spmd(nc, [given], core_ids=[0])
    return result.results[0]["out"].transpose(1, 0, 2)
```

```python
from contextlib import ExitStack

import numpy as np

import concourse.bass as bass
from concourse import mybir

F32 = mybir.dt.float32
BF16 = mybir.dt.bfloat16
I32 = mybir.dt.int32
U8 = mybir.dt.uint8
ALU = mybir.AluOpType
ACT = mybir.ActivationFunctionType
AX_X = mybir.AxisListType.X

P = 128
B = 16
D = 256
DC = D // P
ROWS = 2
UNITS = 2
ITERS = B // (ROWS * UNITS)
TOK = ROWS * P
BANKS = 8
BANK = 512

HEADS = 16
QUAD = 4
GROUPS = HEADS // QUAD
HD1 = D // HEADS
HDC = P // HEADS
HD2 = 64
INNER = HEADS * HD2
IC = INNER // P
EXPERTS = 2
FF1 = 688
F1C = -(-FF1 // P)
FF2 = 1024
F2C = FF2 // P
ROPE_BASE = 10000.0
EPS_RMS = 1e-6
EPS_LN = 1e-5
MASKED = -(2.0 ** 100)

P_RING = 4
PT_RING = 2
SKEW_T = 2
SKEW_O = 3



def layout(parts):
    table, at = {}, 0
    for name, chunks, width in parts:
        table[name] = (at, chunks, width)
        at += chunks * width
    return table, at


W0, W0_COLS = layout([("mem", 1, D), ("gate", 2 * DC, D)])
W1A, W1A_COLS = layout([("qkv0", DC, 3 * D), ("qkv1", DC, 3 * D), ("dense0", DC, D), ("dense1", DC, D),
                        ("cq", DC, P), ("ckv", 1, 2 * P), ("cdense", 1, D)])
W1B, W1B_COLS = layout([("gate0", DC, F1C * P), ("up0", DC, F1C * P), ("gate1", DC, F1C * P),
                        ("up1", DC, F1C * P), ("down0", F1C, D), ("down1", F1C, D)])
W2A, W2A_COLS = layout([("q", DC, INNER), ("kv", 1, 2 * INNER), ("o", IC, D)])
W2B, W2B_COLS = layout([("w1", DC, FF2), ("w2", F2C, D)])
WA_COLS = max(W1A_COLS, W2A_COLS)
WF_COLS = max(W0_COLS, W1B_COLS, W2B_COLS)

VEC = {n: DC * i for i, n in enumerate(
    ["self_w", "cross_w", "mlp_w", "q_g2", "q_b2", "ff_g2", "ff_b2", "q_g3", "q_b3", "ff_g3", "ff_b3"])}



A_, B_ = range(UNITS)


def here(*steps):
    return [(s, 0) for s in steps]


def ahead(*steps):
    return [(s, 1) for s in steps]


def attention(streams):
    groups = [(kind, u, b, g) for kind, u in streams for b in range(ROWS) for g in range(GROUPS)]
    slots = []
    for i in range(len(groups) + SKEW_O):
        slot = []
        if i < len(groups):
            slot += here(("scores",) + groups[i])
        if 0 <= i - SKEW_T < len(groups):
            slot += here(("turn",) + groups[i - SKEW_T])
        if 0 <= i - SKEW_O < len(groups):
            slot += here(("values",) + groups[i - SKEW_O])
        slots.append(slot)
    return slots


def weave(slots, *sides):
    filled = [list(slot) for slot in slots]
    for steps, first, last in sides:
        n = last - first + 1
        for i, s in enumerate(steps):
            if s[0]:
                filled[first + i * n // len(steps)].append(s)
    return [s for slot in filled for s in slot]


def pre_memory(u):
    return [(k, u) for k in ("memT", "mem", "score0", "turn0", "mix0")]


def pre_self(u):
    return [("xvT", u), ("xlT", u), ("qk", u, 0), ("qk", u, 1), ("kT", u), ("v1", u), ("qT", u)] + spreads("self", u)


def spreads(kind, u):
    return [("spread", kind, u, b, half) for b in range(ROWS) for half in range(2)]


def pre_mlp1(u):
    return [("xvT", u), ("xlT", u)]


def pre_attn2(u):
    return ([("nT", u)] + [("k2", u, j) for j in range(IC // 2)]
            + [("v2", u, b, j) for b in range(ROWS) for j in range(2)] + [("q2", u, j) for j in range(IC // 2)])


def pre_ff2(u):
    return [("nT", u)]




def steps_memory(norms, pre):
    def half(u, first):
        second = here(("mixT", u), ("gate0", u), ("out0", u), ("end", u))
        return [s for s in first[0:1] + second[0:1] + first[1:3] + second[1:2] + first[3:] + second[2:] if s[0]]

    return half(A_, here(*pre_memory(B_))) + half(B_, ahead(*norms) + ahead(*pre))


def steps_self(norms, pre):
    n = ROWS * GROUPS
    sides = []
    for u in range(UNITS):
        keys = spreads("cross", u)
        for slot, steps in ((0, [("ck", u), ("cv", u), ("mask", u, 0), keys[0]]), (1, [keys[1], ("maskedT", u, 0)]),
                            (2, [("mask", u, 1)]), (3, [keys[2], ("maskedT", u, 1)]),
                            (4, [("dense", u), ("norm_cross", u)]), (5, [("scale", "cross", u), keys[3]]),
                            (6, [("nT", u)]), (7, [("cq", u)])):
            sides.append((here(*steps), (u + 1) * n + slot, (u + 1) * n + slot))
    pre_b = pre_self(B_)
    return weave(attention([("self", A_), ("self", B_), ("cross", A_), ("cross", B_)]),
                 (here(*pre_b), 0, 6),
                 *sides,
                 (ahead(*norms), 3 * n - 3, 3 * n),
                 (ahead(*pre), 3 * n, 4 * n),
                 (here(("coT", A_), ("cdense", A_), ("end", A_)), 3 * n + SKEW_O, 3 * n + SKEW_O + 1),
                 (here(("coT", B_), ("cdense", B_), ("end", B_)), 4 * n + SKEW_O - 1, 4 * n + SKEW_O - 1))


def steps_mlp1(norms, pre):
    def hidden(u):
        return [(k, u, e, j) for e in range(EXPERTS) for j in range(F1C // 2) for k in ("gate1", "up1")]

    h = len(hidden(A_))
    return weave([here(s) for s in hidden(A_) + hidden(B_) + [("down", A_), ("down", B_)]],
                 (here(*pre_mlp1(B_)), 0, h - 4),
                 (ahead(*norms), h, h + 2),
                 (ahead(*pre), 2 * h, 2 * h + 1),
                 (here(("end", A_)), 2 * h + 1, 2 * h + 1),
                 (here(("end", B_)), 2 * h + 1, 2 * h + 1))


def steps_attn2(norms, pre):
    def tail(u):
        return [("oT2", u, b, j) for b in range(ROWS) for j in range(2)] + [("wo", u), ("end", u)]

    n = ROWS * GROUPS
    return weave(attention([("media", A_), ("media", B_)]),
                 (here(*pre_attn2(B_)), 0, n - 2),
                 (here(*tail(A_)), n + SKEW_O, n + SKEW_O + 2),
                 (ahead(*norms), n, n + 1),
                 (ahead(*pre), n + SKEW_O + 2, 2 * n + SKEW_O - 1),
                 (here(*tail(B_)), 2 * n + SKEW_O - 1, 2 * n + SKEW_O - 1))


def steps_ff2(norms, pre):
    def hidden(u):
        return [("w1", u, j) for j in range(F2C // 2)]

    h = F2C // 2
    return weave([here(s) for s in hidden(A_) + hidden(B_) + [("w2", A_), ("w2", B_)]],
                 (here(*pre_ff2(B_)), 0, 0),
                 (ahead(*norms), 1, h - 1),
                 (ahead(*pre), 2 * h - 1, 2 * h + 1),
                 (here(("end", A_), ("end", B_)), 2 * h + 1, 2 * h + 1))


PLAN = [(0, steps_memory, None, pre_memory), (1, steps_self, "self", pre_self),
        (1, steps_mlp1, "mlp", pre_mlp1), (2, steps_attn2, "q", pre_attn2),
        (2, steps_ff2, "ff", pre_ff2), (3, steps_attn2, "q", pre_attn2), (3, steps_ff2, "ff", pre_ff2)]

EVENTS = {
    "memT": "mm copied", "mem": "mm copied", "score0": "mm max exp", "turn0": "mm copied",
    "mix0": "mm rinv normed", "mixT": "mm copied", "gate0": "mm biased",
    "out0": "tanh gated fused stats aggr square mean eps rstd",
    "norm_self": "stats aggr square mean eps pow rstd", "norm_mlp": "stats aggr square mean eps pow rstd",
    "norm_cross": "stats aggr square mean eps rstd", "norm_q": "stats aggr eps rstd",
    "norm_ff": "stats aggr eps rstd", "scale": "xn", "spread": "done",
    "xvT": "mm copied", "xlT": "mm copied", "qk": "mm halves sum", "v1": "mm copied", "qT": "mm copied",
    "kT": "mm flat", "scores": "mm max exp", "turn": "mm copied", "values": "mm rinv normed",
    "mask": "done", "maskedT": "mm copied", "dense": "mm added", "nT": "mm copied", "cq": "mm copied", "ck": "mm flat",
    "cv": "mm copied", "coT": "mm copied", "cdense": "mm", "gate1": "mm silu", "up1": "mm h",
    "down": "mm", "q2": "mm copied", "k2": "mm copied", "v2": "mm copied", "oT2": "mm copied",
    "wo": "mm", "w1": "mm gelu", "w2": "mm", "end": "done",
}
EVENTS = {kind: events.split() for kind, events in EVENTS.items()}
EMPTIED = {k: e[-1] for k, e in EVENTS.items()} | {"qk": "halves"}
LAST = {"cdense", "down", "wo", "w2"}


class Phase:

    def __init__(self, index, before):
        self.index = index
        self.layer, self.weave, norm, pre = PLAN[index]
        self.norms = [(f"norm_{norm}", u) for u in range(UNITS)] + [("scale", norm, u) for u in range(UNITS)] if norm else []
        self.pre = pre(A_)
        body = self.body = self.weave(self.norms, self.pre)
        self.prologue = [s for s, early in body if early]
        self.own = [s for s, early in body if not early]
        self.of_kind, self.place = {}, {}
        for s in self.prologue + self.own:
            n = self.of_kind.get(s[0], 0)
            self.place[s] = n
            self.of_kind[s[0]] = n + 1
        self.base = dict(before)
        self.after = {k: before.get(k, 0) + ITERS * self.of_kind.get(k, 0) for k in {*before, *self.of_kind}}
        jobs = [s for s, _ in body if "mm" in EVENTS[s[0]]]
        self.bank = {s: i % BANKS for i, s in enumerate(jobs)}

    def count(self, step, event, it):
        kind = step[0]
        before = PRIME.get((kind, event), 0) + self.base.get(kind, 0)
        return it * self.of_kind[kind] + (before + self.place[step] + 1)

    def earlier(self, step, n):
        same = sorted((s for s in self.place if s[0] == step[0]), key=self.place.get)
        at = self.place[step] - n
        return same[at % len(same)], -(at // len(same))


PHASES = []
for _i in range(len(PLAN)):
    PHASES.append(Phase(_i, PHASES[-1].after if PHASES else {}))


def between(ph):
    if ph is PHASES[0]:
        return [(ph, 0, s) for s in ph.norms + ph.pre]
    old = PHASES[ph.index - 1] if ph else PHASES[-1]
    return [(ph, 0, s) if early else (old, ITERS - 1, s)
            for s, early in (old.weave(ph.norms, ph.pre) if ph else old.weave([], []))]


PRIME = {(k, EMPTIED[k]): max(ph.of_kind.get(k, 0) for ph in PHASES) for k in EVENTS}
for _k in LAST:
    del PRIME[_k, "mm"]
for _k, _e in (("cv", "mm"), ("v2", "mm"), ("mem", "mm"), ("gate0", "mm"), ("out0", "fused"), ("qk", "sum"), ("nT", "mm"), ("xlT", "mm")):
    PRIME[_k, _e] = max(ph.of_kind.get(_k, 0) for ph in PHASES)


def build(nc, dram, out):
    with ExitStack() as ctx:
        def sb(name, shape, dt=F32):
            return ctx.enter_context(nc.sbuf_tensor(name, shape, dt))

        sems = {}
        for kind, events in EVENTS.items():
            for e in events:
                sems[kind, e] = ctx.enter_context(nc.semaphore(f"{kind}_{e}"))

        def sem(name):
            return ctx.enter_context(nc.semaphore(name))

        consts_in = sem("consts_in")
        weights_att = sem("weights_att")
        weights_ff = sem("weights_ff")
        x_in = [sem(f"x_in{u}") for u in range(UNITS)]
        xT_in = [sem(f"xT_in{u}") for u in range(UNITS)]
        ctx_in = [sem(f"ctx_in{u}") for u in range(UNITS)]
        setup_v = sem("setup_vector")
        setup_p = sem("setup_pool")
        setup_pe = sem("setup_tensor")
        setup_a = sem("setup_scalar")
        zeroed = sem("zeroed")
        primed = sem("primed")
        out_done = sem("out_done")
        settled = {n: sem(f"settled_{n}") for n in ("vector", "tensor")}

        x_all = sb("x_all", [P, B, D])
        w_att = sb("w_att", [P, WA_COLS])
        w_ff = sb("w_ff", [P, WF_COLS])
        ctxT = [sb(f"ctxT{u}", [P, TOK]) for u in range(UNITS)]
        xn = [sb(f"xn{u}", [P, ROWS, EXPERTS, D]) for u in range(UNITS)]
        xT = [sb(f"xT{u}", [P, EXPERTS, DC, TOK]) for u in range(UNITS)]
        hT = [sb(f"hT{u}", [P, EXPERTS * F1C * TOK]) for u in range(UNITS)]
        kbd = [sb(f"kbd{u}", [P, IC * ROWS * 2 * P]) for u in range(UNITS)]
        v = [sb(f"v{u}", [P, ROWS * HEADS * (HD2 + 1)]) for u in range(UNITS)]
        o = [sb(f"o{u}", [P, ROWS * INNER]) for u in range(UNITS)]
        p_ring = [sb(f"p{i}", [P, BANK]) for i in range(P_RING)]
        pT_ring = [sb(f"pT{i}", [P, BANK]) for i in range(PT_RING)]
        nmax = sb("nmax", [P, P_RING, QUAD])
        rinv = sb("rinv", [P, 2, QUAD])
        rsum0 = sb("rsum0", [P, UNITS, ROWS])
        rinv0 = sb("rinv0", [P, UNITS, ROWS])
        stats = sb("stats", [P, UNITS, ROWS, 6])
        aggr = sb("aggr", [P, UNITS, ROWS, 2])
        ms = sb("ms", [P, UNITS, 4, ROWS])
        rstd = sb("rstd", [P, UNITS, ROWS, EXPERTS])
        vm_here = sb("vm_here", [P, UNITS, ROWS, EXPERTS])
        minus_half = sb("minus_half", [P, ROWS])
        eps = sb("eps", [P, 2, ROWS])
        ident = sb("ident", [P, P])
        ident16 = sb("ident16", [P, P], BF16)
        causal = p_ring[1][:, 0:P]
        causal16 = sb("causal16", [P, P], BF16)
        head_rows = sb("head_rows", [P, 8 + HEADS])
        rope_tab = sb("rope_tab", [P, 2 * HD1])
        rope = sb("rope", [P, 2, HD1])
        vec = sb("vec", [P, DC * 11])
        rows0 = sb("rows0", [P, 2, D])
        gates = sb("gates", [P, 4])
        tgates = sb("tgates", [P, 4])
        tt = sb("tt", [P, 2, B], I32)
        vm = sb("vm", [P, B, EXPERTS])
        media = p_ring[2][0:1, :].bitcast(U8)
        media16 = sb("media16", [1, B, P], BF16)
        ones16 = sb("ones16", [1, P], BF16)
        pos_i = pT_ring[0][:, 0:P].bitcast(I32)
        pos_f = pT_ring[1][:, 0:2 * P].rearrange("p (a t) -> p a t", a=2)
        pos_hot = p_ring[0][:, 0:P]
        token = sb("token", [P, 1])
        ps = [ctx.enter_context(nc.psum_tensor(f"bank{k}", [P, BANK], F32)) for k in range(BANKS)]

        silu = [o[i][:, 0:BANK] for i in range(2)]

        def rot_of(u, b):
            both_ = (hT[u][:, 2048:3072], xn[u][:, :, :, :].rearrange("p b e d -> p (b e d)"))[b]
            return both_[:, 0:BANK], both_[:, BANK:2 * BANK]

        def qk_of(u, b):
            return o[u][:, b * BANK:(b + 1) * BANK]

        def weight(buf, table, name):
            at, chunks, width = table[name]
            return buf[:, at:at + chunks * width].rearrange("p (c n) -> p c n", c=chunks)

        def head_width(kind):
            return {"self": HD1, "cross": HDC, "media": HD2}[kind]

        def v_view(kind, u):
            w = head_width(kind) + 1
            at = ROWS * HEADS * (HD1 + 1) if kind == "cross" else 0
            return v[u][:, at:at + ROWS * HEADS * w].rearrange("p (b h w) -> p b h w", b=ROWS, h=HEADS)

        class View:
            pass

        views = []
        for u in range(UNITS):
            w = View()
            h = hT[u]
            w.qT1 = h[:, 0:512].rearrange("p (b c t) -> p b c t", b=ROWS, c=DC)
            w.oT1 = h[:, 512:1536].rearrange("p (b e c t) -> p b e c t", b=ROWS, e=EXPERTS, c=DC)
            w.cqT = h[:, 1536:1792]
            w.coT = h[:, 1792:2048]
            w.qT2 = h[:, 0:IC * TOK].rearrange("p (m t) -> p m t", m=IC)
            w.oT2 = w.qT2
            w.h1 = h[:, :].rearrange("p (e f t) -> p e f t", e=EXPERTS, f=F1C)
            w.h2 = h[:, 0:F2C * TOK].rearrange("p (f t) -> p f t", f=F2C)
            w.k_flat = h[:, 512:1024]
            w.ck_flat = h[:, 2048:2304]
            w.k1 = kbd[u][:, :].rearrange("p (b h t) -> p b h t", b=ROWS, h=HEADS)
            w.k2 = kbd[u][:, :].rearrange("p (m b s t) -> p m b s t", m=IC, b=ROWS, s=2)
            w.x0 = o[u][:, 0:512].rearrange("p (b d) -> p b d", b=ROWS)
            w.mix = o[u][:, 512:1024].rearrange("p (b d) -> p b d", b=ROWS)
            w.z = o[u][:, 1024:1536].rearrange("p (b d) -> p b d", b=ROWS)
            w.fused = o[u][:, 1536:2048].rearrange("p (b d) -> p b d", b=ROWS)
            w.xT0 = h[:, 0:512].rearrange("p (c t) -> p c t", c=DC)
            w.memT = h[:, 512:1024].rearrange("p (c t) -> p c t", c=DC)
            w.mixT = h[:, 1024:1536].rearrange("p (b c t) -> p b c t", b=ROWS, c=DC)
            w.mem = kbd[u][:, 0:512].rearrange("p (b d) -> p b d", b=ROWS)
            views.append(w)

        def out_of(kind, u, b, g):
            w = head_width(kind)
            at = {"self": b * D, "cross": 512 + b * P, "media": b * INNER}[kind] + (1024 if kind != "media" else 0)
            return o[u][:, at + g * QUAD * w:at + (g + 1) * QUAD * w].rearrange("p (h w) -> p h w", w=w)

        def rows(it, u):
            return bass.ds(it * (UNITS * ROWS) + u * ROWS, ROWS)

        def row(it, u, b):
            return bass.ds(it * (UNITS * ROWS) + (u * ROWS + b), 1)

        def wait(eng, ph, it, step, event, back=0):
            eng.wait_ge(sems[step[0], event], ph.count(step, event, it - back))

        def settle(eng, name):
            eng.sem_inc(settled[name], 1)

        def final(ph, u):
            return [s for s in ph.own if s[0] in LAST and s[1] == u][0]

        def run(eng, stages, ready=None):
            for ph in PHASES:
                if ready:
                    ready(ph)
                for p, it, s in between(ph):
                    if s[0] in stages:
                        stages[s[0]](p, it, s, ps[p.bank[s]] if s in p.bank else None)
                with eng.Fori(0, ITERS - 1) as it:
                    for s, early in ph.body:
                        if s[0] in stages:
                            stages[s[0]](ph, it + early, s, ps[ph.bank[s]] if s in ph.bank else None)
            for p, it, s in between(None):
                if s[0] in stages:
                    stages[s[0]](p, it, s, ps[p.bank[s]] if s in p.bank else None)

        VECTOR_SETUP = 17
        SCALAR_SETUP = 1
        ATT_LOADS = {1: 1, 3: 2, 5: 3}
        FF_LOADS = {0: 1, 2: 2, 4: 3, 6: 4}
        CTX_BEFORE = {0: 0, 1: ITERS, 3: 2 * ITERS, 5: 3 * ITERS}

        block = ctx.enter_context(nc.Block())

        @block.sync
        def _(sp):
            for dst, src in ((rope_tab, "rope_tab"), (token, "token"), (pos_i, "pos"), (tt, "tt"), (media, "media"),
                             (gates, "gates"), (ident, "ident"), (causal, "causal"), (head_rows, "head_rows"),
                             (vec, "vec"), (rows0, "rows0")):
                sp.dma_start(dst[:, :] if len(dst.shape) == 2 else dst[:, :, :], dram[src]).then_inc(consts_in, 16)
            sp.dma_start(w_ff[:, 0:W0_COLS], dram["w0"]).then_inc(weights_ff, 16)
            sp.dma_start(w_att[:, 0:W1A_COLS], dram["w1a"]).then_inc(weights_att, 16)
            for (kind, event), n in PRIME.items():
                if n:
                    sp.sem_inc(sems[kind, event], n)
            sp.sem_inc(primed, 1)

            def load_ctx(ph, it, u, reader):
                wait(sp, ph, it, reader, "mm", back=1)
                sp.dma_start(ctxT[u][:, :].rearrange("p (b t) -> p b t", b=ROWS),
                             dram["ctxT"][:, rows(it, u), :]).then_inc(ctx_in[u], 16)

            def ended(ph):
                wait(sp, ph, ITERS - 1, ("end", B_), "done")

            for ph in PHASES:
                if ph.index == 0:
                    with sp.Fori(0, ITERS) as it:
                        for u in range(UNITS):
                            wait(sp, ph, it, ("gate0", u), "mm", back=1)
                            sp.dma_start(views[u].xT0, dram["xT"][:, :, bass.ds(it * (UNITS * TOK) + u * TOK, TOK)])\
                              .then_inc(xT_in[u], 16)
                            load_ctx(ph, it, u, ("mem", u))
                            wait(sp, ph, it, ("out0", u), "fused", back=1)
                            sp.dma_start(views[u].x0, dram["x"][:, rows(it, u), :]).then_inc(x_in[u], 16)
                if ph.index == 1:
                    for u in range(UNITS):
                        wait(sp, PHASES[0], ITERS - 1, ("mem", u), "mm")
                        load_ctx(ph, 0, u, ("cv", u))
                    ended(PHASES[0])
                    sp.dma_start(w_ff[:, 0:W1B_COLS], dram["w1b"]).then_inc(weights_ff, 16)
                    with sp.Fori(1, ITERS) as it:
                        for u in range(UNITS):
                            load_ctx(ph, it, u, ("cv", u))
                    ended(ph)
                    sp.dma_start(w_att[:, 0:W2A_COLS], dram["w2a"]).then_inc(weights_att, 16)
                if ph.index in (3, 5):
                    reader = lambda u: ("v2", u, ROWS - 1, 1)
                    for u in range(UNITS):
                        before, last = (PHASES[1], ("cv", u)) if ph.index == 3 else (PHASES[3], reader(u))
                        wait(sp, before, ITERS - 1, last, "mm")
                        load_ctx(ph, 0, u, reader(u))
                    ended(PHASES[ph.index - 1])
                    sp.dma_start(w_ff[:, 0:W2B_COLS], dram["w2b" if ph.index == 3 else "w3b"])\
                      .then_inc(weights_ff, 16)
                    with sp.Fori(1, ITERS) as it:
                        for u in range(UNITS):
                            load_ctx(ph, it, u, reader(u))
                    if ph.index == 3:
                        ended(ph)
                        sp.dma_start(w_att[:, 0:W2A_COLS], dram["w3a"]).then_inc(weights_att, 16)
                if ph.index == 6:
                    with sp.Fori(0, ITERS) as it:
                        for u in range(UNITS):
                            wait(sp, ph, it, ("end", u), "done")
                            sp.dma_start(out[:, rows(it, u), :], x_all[:, rows(it, u), :]).then_inc(out_done, 16)
            sp.wait_ge(out_done, 16 * ITERS * UNITS)

        @block.tensor
        def _(pe):
            def mm(dst, lhsT, rhs, first, last):
                return pe.matmul(dst, lhsT, rhs, start=first, stop=last)

            def done(ins, s):
                ins.then_inc(sems[s[0], "mm"], 1)

            def turn(s, dst_of, blocks):
                bank = ps[dst_of]
                for i, src in enumerate(blocks):
                    t = pe.transpose(bank[:, i * P:(i + 1) * P], src, ident[:])
                done(t, s)

            def memT(ph, it, s, bank):
                u = s[1]
                pe.wait_ge(ctx_in[u], it * 16 + 16)
                w = weight(w_ff, W0, "mem")
                for c in range(DC):
                    t = mm(bank[:, c * TOK:(c + 1) * TOK], w[:, 0, c * P:(c + 1) * P], ctxT[u][:, :], True, True)
                done(t, s)

            def mem(ph, it, s, bank):
                u = s[1]
                w = weight(w_ff, W0, "mem")
                for b in range(ROWS):
                    t = mm(bank[:, b * D:(b + 1) * D], ctxT[u][:, b * P:(b + 1) * P], w[:, 0, :], True, True)
                done(t, s)

            def score0(ph, it, s, bank):
                u = s[1]
                w = views[u]
                pe.wait_ge(xT_in[u], it * 16 + 16)
                wait(pe, ph, it, ("memT", u), "copied")
                for b in range(ROWS):
                    for c in range(DC):
                        t = mm(bank[:, b * P:(b + 1) * P], w.xT0[:, c, b * P:(b + 1) * P],
                               w.memT[:, c, b * P:(b + 1) * P], c == 0, c == DC - 1)
                done(t, s)

            def turn0(ph, it, s, bank):
                wait(pe, ph, it, ("score0", s[1]), "exp")
                turn(s, ph.bank[s], [p_ring[s[1]][:, b * P:(b + 1) * P] for b in range(ROWS)])

            def mix0(ph, it, s, bank):
                u = s[1]
                wait(pe, ph, it, ("turn0", u), "copied")
                wait(pe, ph, it, ("mem", u), "copied")
                for b in range(ROWS):
                    t = mm(bank[:, b * D:(b + 1) * D], pT_ring[u][:, b * P:(b + 1) * P], views[u].mem[:, b, :], True, True)
                done(t, s)

            def mixT(ph, it, s, bank):
                u = s[1]
                wait(pe, ph, it, ("mix0", u), "normed")
                turn(s, ph.bank[s], [views[u].mix[:, b, c * P:(c + 1) * P] for b in range(ROWS) for c in range(DC)])

            def gate0(ph, it, s, bank):
                u = s[1]
                wg = weight(w_ff, W0, "gate")
                wait(pe, ph, it, ("mixT", u), "copied")
                for b in range(ROWS):
                    for c in range(2 * DC):
                        lhsT = views[u].xT0[:, c, b * P:(b + 1) * P] if c < DC else views[u].mixT[:, b, c - DC, :]
                        t = mm(bank[:, b * D:(b + 1) * D], lhsT, wg[:, c, :], c == 0, c == 2 * DC - 1)
                done(t, s)

            def expertT(ph, it, s, bank):
                u, e = s[1], 0 if s[0] == "xvT" else 1
                wait(pe, ph, it, ("scale", "self" if ph.index == 1 else "mlp", u), "xn")
                turn(s, ph.bank[s], [xn[u][:, b, e, c * P:(c + 1) * P] for c in range(DC) for b in range(ROWS)])

            def qk(ph, it, s, bank):
                u, b = s[1:]
                wait(pe, ph, it, ("xvT", u), "copied")
                wait(pe, ph, it, ("xlT", u), "copied")
                for e in range(EXPERTS):
                    for c in range(DC):
                        t = mm(bank[:, :], xT[u][:, e, c, b * P:(b + 1) * P],
                               weight(w_att, W1A, f"qkv{e}")[:, c, 0:2 * D], e + c == 0, e + c == 2)
                done(t, s)

            def v1(ph, it, s, bank):
                u = s[1]
                for b in range(ROWS):
                    for e in range(EXPERTS):
                        for c in range(DC):
                            t = mm(bank[:, b * D:(b + 1) * D], xT[u][:, e, c, b * P:(b + 1) * P],
                                   weight(w_att, W1A, f"qkv{e}")[:, c, 2 * D:3 * D], e + c == 0, e + c == 2)
                done(t, s)

            def qkT(ph, it, s, bank):
                u, at = s[1], 0 if s[0] == "qT" else D
                wait(pe, ph, it, ("qk", u, ROWS - 1), "sum")
                turn(s, ph.bank[s], [qk_of(u, b)[:, at + c * P:at + (c + 1) * P] for b in range(ROWS) for c in range(DC)])

            def scores(ph, it, s, bank):
                kind, u, b, g = s[1:]
                w = views[u]
                heads = slice(g * QUAD, (g + 1) * QUAD)
                if kind == "self":
                    wait(pe, ph, it, ("qT", u), "copied")
                    wait(pe, ph, it, ("spread", kind, u, b, g // 2), "done")
                    mm(bank[:, :], ident16[:, :], causal16[:, :].unsqueeze(1).broadcast_to([P, QUAD, P]), True, False)
                    t = mm(bank[:, :], w.qT1[:, b, g // 2, :], w.k1[:, b, heads, :], False, True)
                elif kind == "cross":
                    wait(pe, ph, it, ("cq", u), "copied")
                    wait(pe, ph, it, ("spread", kind, u, b, g // 2), "done")
                    t = mm(bank[:, :], w.cqT[:, b * P:(b + 1) * P], w.k1[:, b, heads, :], True, True)
                else:
                    wait(pe, ph, it, ("q2", u, g), "copied")
                    wait(pe, ph, it, ("k2", u, g), "copied")
                    settle(pe, "tensor")
                    mm(bank[:, :], ones16[0:1, :], media16[0:1, row(it, u, b), :].broadcast_to([1, QUAD, P]), True, False)
                    for m in (2 * g, 2 * g + 1):
                        half = (m % 2) * 2 * P
                        t = mm(bank[:, half:half + 2 * P], w.qT2[:, m, b * P:(b + 1) * P], w.k2[:, m, b, :, :],
                               False, m % 2 == 1)
                done(t, s)

            def turn_p(ph, it, s, bank):
                wait(pe, ph, it, ("scores",) + s[1:], "exp")
                turn(s, ph.bank[s], [p_ring[ph.place[s] % P_RING][:, j * P:(j + 1) * P] for j in range(QUAD)])

            def values(ph, it, s, bank):
                kind, u, b, g = s[1:]
                wait(pe, ph, it, ("turn",) + s[1:], "copied")
                if (b, g) == (0, 0):
                    wait(pe, ph, it, {"self": ("v1", u), "cross": ("cv", u), "media": ("v2", u, ROWS - 1, 1)}[kind], "copied")
                w = head_width(kind) + 1
                for j in range(QUAD):
                    t = mm(bank[:, j * w:(j + 1) * w], pT_ring[ph.place[s] % PT_RING][:, j * P:(j + 1) * P],
                           v_view(kind, u)[:, b, g * QUAD + j, :], True, True)
                done(t, s)

            def maskedT(ph, it, s, bank):
                u, b = s[1:]
                wait(pe, ph, it, ("mask", u, b), "done")
                turn(s, ph.bank[s], [xn[u][:, b, e, c * P:(c + 1) * P] for e in range(EXPERTS) for c in range(DC)])

            def dense(ph, it, s, bank):
                u = s[1]
                for b in range(ROWS):
                    wait(pe, ph, it, ("maskedT", u, b), "copied")
                    for e in range(EXPERTS):
                        for c in range(DC):
                            t = mm(bank[:, b * D:(b + 1) * D], views[u].oT1[:, b, e, c, :],
                                   weight(w_att, W1A, f"dense{e}")[:, c, :], e + c == 0, e + c == 2)
                done(t, s)

            def nT(ph, it, s, bank):
                u = s[1]
                wait(pe, ph, it, ("scale", {1: "cross", 3: "q", 5: "q", 4: "ff", 6: "ff"}[ph.index], u), "xn")
                turn(s, ph.bank[s], [xn[u][:, b, 0, c * P:(c + 1) * P] for c in range(DC) for b in range(ROWS)])

            def cq(ph, it, s, bank):
                u = s[1]
                wait(pe, ph, it, ("nT", u), "copied")
                for c in range(DC):
                    t = mm(bank[:, 0:TOK], weight(w_att, W1A, "cq")[:, c, :], xT[u][:, 0, c, :], c == 0, c == DC - 1)
                done(t, s)

            def ctx_here(ph, it, u):
                pe.wait_ge(ctx_in[u], it * 16 + 16 * (CTX_BEFORE[ph.index] + 1))

            def ck(ph, it, s, bank):
                u = s[1]
                ctx_here(ph, it, u)
                done(mm(bank[:, 0:TOK], weight(w_att, W1A, "ckv")[:, 0, 0:P], ctxT[u][:, :], True, True), s)

            def cv(ph, it, s, bank):
                u = s[1]
                for b in range(ROWS):
                    t = mm(bank[:, b * P:(b + 1) * P], ctxT[u][:, b * P:(b + 1) * P],
                           weight(w_att, W1A, "ckv")[:, 0, P:2 * P], True, True)
                done(t, s)

            def coT(ph, it, s, bank):
                u = s[1]
                wait(pe, ph, it, ("values", "cross", u, ROWS - 1, GROUPS - 1), "normed")
                turn(s, ph.bank[s], [o[u][:, 1536 + b * P:1536 + (b + 1) * P] for b in range(ROWS)])

            def cdense(ph, it, s, bank):
                u = s[1]
                wait(pe, ph, it, ("coT", u), "copied")
                for b in range(ROWS):
                    t = mm(bank[:, b * D:(b + 1) * D], views[u].coT[:, b * P:(b + 1) * P],
                           weight(w_att, W1A, "cdense")[:, 0, :], True, True)
                done(t, s)

            def hidden1(ph, it, s, bank):
                u, e, j = s[1:]
                wait(pe, ph, it, ("xvT" if e == 0 else "xlT", u), "copied")
                w = weight(w_ff, W1B, ("gate" if s[0] == "gate1" else "up") + str(e))
                for k in range(2):
                    f = 2 * j + k
                    for c in range(DC):
                        t = mm(bank[:, k * TOK:(k + 1) * TOK], w[:, c, f * P:(f + 1) * P], xT[u][:, e, c, :],
                               c == 0, c == DC - 1)
                done(t, s)

            def down(ph, it, s, bank):
                u = s[1]
                wait(pe, ph, it, ("up1", u, EXPERTS - 1, F1C // 2 - 1), "h")
                for b in range(ROWS):
                    for e in range(EXPERTS):
                        for f in range(F1C):
                            t = mm(bank[:, b * D:(b + 1) * D], views[u].h1[:, e, f, b * P:(b + 1) * P],
                                   weight(w_ff, W1B, f"down{e}")[:, f, :], e + f == 0, e == 1 and f == F1C - 1)
                done(t, s)

            def q2(ph, it, s, bank):
                u, j = s[1:]
                wait(pe, ph, it, ("nT", u), "copied")
                for k in range(2):
                    m = 2 * j + k
                    for c in range(DC):
                        t = mm(bank[:, k * TOK:(k + 1) * TOK], weight(w_att, W2A, "q")[:, c, m * P:(m + 1) * P],
                               xT[u][:, 0, c, :], c == 0, c == DC - 1)
                done(t, s)

            def k2(ph, it, s, bank):
                u, j = s[1:]
                if j == 0:
                    ctx_here(ph, it, u)
                for k in range(2):
                    m = 2 * j + k
                    t = mm(bank[:, k * TOK:(k + 1) * TOK], weight(w_att, W2A, "kv")[:, 0, m * P:(m + 1) * P],
                           ctxT[u][:, :], True, True)
                done(t, s)

            def v2(ph, it, s, bank):
                u, b, j = s[1:]
                at = INNER + j * BANK
                done(mm(bank[:, :], ctxT[u][:, b * P:(b + 1) * P], weight(w_att, W2A, "kv")[:, 0, at:at + BANK],
                        True, True), s)

            def oT2(ph, it, s, bank):
                u, b, j = s[1:]
                wait(pe, ph, it, ("values", "media", u, b, GROUPS - 1), "normed")
                turn(s, ph.bank[s], [o[u][:, b * INNER + m * P:b * INNER + (m + 1) * P] for m in range(4 * j, 4 * j + 4)])

            def wo(ph, it, s, bank):
                u = s[1]
                wait(pe, ph, it, ("oT2", u, ROWS - 1, 1), "copied")
                for b in range(ROWS):
                    for m in range(IC):
                        t = mm(bank[:, b * D:(b + 1) * D], views[u].oT2[:, m, b * P:(b + 1) * P],
                               weight(w_att, W2A, "o")[:, m, :], m == 0, m == IC - 1)
                done(t, s)

            def w1(ph, it, s, bank):
                u, j = s[1:]
                wait(pe, ph, it, ("nT", u), "copied")
                for k in range(2):
                    f = 2 * j + k
                    for c in range(DC):
                        t = mm(bank[:, k * TOK:(k + 1) * TOK], weight(w_ff, W2B, "w1")[:, c, f * P:(f + 1) * P],
                               xT[u][:, 0, c, :], c == 0, c == DC - 1)
                done(t, s)

            def w2(ph, it, s, bank):
                u = s[1]
                wait(pe, ph, it, ("w1", u, F2C // 2 - 1), "gelu")
                for b in range(ROWS):
                    for f in range(F2C):
                        t = mm(bank[:, b * D:(b + 1) * D], views[u].h2[:, f, b * P:(b + 1) * P],
                               weight(w_ff, W2B, "w2")[:, f, :], f == 0, f == F2C - 1)
                done(t, s)

            stages = dict(memT=memT, mem=mem, score0=score0, turn0=turn0, mix0=mix0, mixT=mixT, gate0=gate0,
                          xvT=expertT, xlT=expertT, qk=qk, v1=v1, qT=qkT, kT=qkT, scores=scores, turn=turn_p,
                          values=values, maskedT=maskedT, dense=dense, nT=nT, cq=cq, ck=ck, cv=cv, coT=coT,
                          cdense=cdense, gate1=hidden1, up1=hidden1, down=down, q2=q2, k2=k2, v2=v2, oT2=oT2,
                          wo=wo, w1=w1, w2=w2)

            pe.wait_ge(consts_in, 16 * 11)
            pe.wait_ge(setup_v, 5)
            pe.matmul(ps[0][:, 0:2 * HD1], pos_hot, rope_tab[:], start=True, stop=True).then_inc(setup_pe, 1)
            pe.wait_ge(setup_v, VECTOR_SETUP)
            pe.wait_ge(primed, 1)

            holder = {}

            def job(ph, it, s):
                k = ph.bank[s]
                if k in holder:
                    p, when, held = holder[k]
                    if held[0] in LAST:
                        held = ("end", held[1])
                    wait(pe, p, when, held, EMPTIED[held[0]])
                    if s[0] == "scores" and held[0] in ("q2", "k2"):
                        settle(pe, "tensor")
                stages[s[0]](ph, it, s, ps[k])
                holder[k] = (ph, it, s)

            def apart(ph, it, s):
                if s not in ph.bank:
                    return
                if s in ph.prologue and it == 0 and s == [t for t in ph.prologue if t in ph.bank][0]:
                    if ph.index in ATT_LOADS:
                        pe.wait_ge(weights_att, 16 * ATT_LOADS[ph.index])
                        pe.wait_ge(zeroed, 1 if ph.index == 1 else 2)
                    else:
                        pe.wait_ge(weights_ff, 16 * FF_LOADS[ph.index])
                job(ph, it, s)

            for ph in PHASES:
                for p, when, s in between(ph):
                    apart(p, when, s)
                for k, (p, when, s) in holder.items():
                    if s[0] in LAST:
                        s = ("end", s[1])
                        if (s, 0) in p.body and p is ph:
                            continue
                    wait(pe, p, when, s, EMPTIED[s[0]])
                left = {ph.bank[s]: (s, early) for s, early in ph.body if s in ph.bank}
                with pe.Fori(0, ITERS - 1) as it:
                    holder = {k: (ph, it + (early - 1), s) for k, (s, early) in left.items()}
                    for s, early in ph.body:
                        if s in ph.bank:
                            job(ph, it + early, s)
                holder = {k: (ph, ITERS - 2 + early, s) for k, (s, early) in left.items()}
            for p, when, s in between(None):
                apart(p, when, s)

        @block.vector
        def _(dve):
            def done(ins, s, event):
                ins.then_inc(sems[s[0], event], 1)

            def copy(ph, it, s, dst, src):
                wait(dve, ph, it, s, "mm")
                done(dve.tensor_copy(dst, src), s, "copied")

            def mem(ph, it, s, bank):
                copy(ph, it, s, views[s[1]].mem, bank[:, :].rearrange("p (b d) -> p b d", b=ROWS))

            def score0(ph, it, s, bank):
                u = s[1]
                wait(dve, ph, it, s, "mm")
                done(dve.tensor_reduce(nmax[:, u, 0:ROWS], bank[:, 0:TOK].rearrange("p (b t) -> p b t", b=ROWS),
                                       AX_X, ALU.max, negate=True), s, "max")

            def mix0(ph, it, s, bank):
                u = s[1]
                wait(dve, ph, it, ("score0", u), "exp")
                done(dve.reciprocal(rinv0[:, u, :], rsum0[:, u, :]), s, "rinv")
                wait(dve, ph, it, s, "mm")
                wait(dve, ph, it, s, "rinv")
                done(dve.tensor_tensor(views[u].mix, bank[:, :].rearrange("p (b d) -> p b d", b=ROWS),
                                       rinv0[:, u, :].unsqueeze(2).broadcast_to([P, ROWS, D]), ALU.mult), s, "normed")

            def gate0(ph, it, s, bank):
                wait(dve, ph, it, s, "mm")
                done(dve.tensor_tensor(views[s[1]].z, bank[:, :].rearrange("p (b d) -> p b d", b=ROWS),
                                       rows0[:, 0:1, :].broadcast_to([P, ROWS, D]), ALU.add), s, "biased")

            def spread(ph, it, s, of):
                u = s[1]
                settle(dve, "vector")
                for b in range(ROWS):
                    t = dve.bn_stats(stats[:, u, b, :], of(b))
                done(t, s, "stats")
                wait(dve, ph, it, s, "stats")
                settle(dve, "vector")
                for b in range(ROWS):
                    t = dve.bn_aggr(aggr[:, u, b, :], stats[:, u, b, :])
                done(t, s, "aggr")

            def out0(ph, it, s, bank):
                u = s[1]
                w = views[u]
                wait(dve, ph, it, s, "tanh")
                done(dve.scalar_tensor_tensor(out=w.z, in0=w.z, scalar=1.0, in1=w.mix, op0=ALU.add, op1=ALU.mult),
                     s, "gated")
                wait(dve, ph, it, s, "gated")
                dve.wait_ge(x_in[u], it * 16 + 16)
                done(dve.scalar_tensor_tensor(out=w.fused, in0=w.z, scalar=0.5, in1=w.x0, op0=ALU.mult, op1=ALU.add),
                     s, "fused")
                wait(dve, ph, it, s, "fused")
                spread(ph, it, s, lambda b: w.fused[:, b, :])

            def norm(ph, it, s, bank):
                u = s[1]
                if s[0] == "norm_cross":
                    wait(dve, ph, it, ("dense", u), "added")
                else:
                    wait(dve, PHASES[ph.index - 1], it, ("end", u), "done")
                spread(ph, it, s, lambda b: x_all[:, row(it, u, b), :])

            def scale(ph, it, s, bank):
                which, u = s[1:]
                wait(dve, ph, it, ("norm_" + which, u), "rstd")
                if which == "mlp":
                    wait(dve, ph, it, ("xlT", u), "mm", back=1)
                elif which == "cross":
                    wait(dve, ph, it, ("maskedT", u, ROWS - 1), "mm")
                else:
                    wait(dve, ph, it, ("nT", u), "mm", back=1)
                for b in range(ROWS):
                    x_b = x_all[:, row(it, u, b), :]
                    if which in ("self", "mlp"):
                        for e in range(EXPERTS):
                            t = dve.tensor_scalar(xn[u][:, b, e:e + 1, :], x_b, rstd[:, u, b, e:e + 1], None, ALU.mult)
                    elif which == "cross":
                        t = dve.tensor_scalar(xn[u][:, b, 0:1, :], x_b, rstd[:, u, b, 0:1], None, ALU.mult)
                    else:
                        t = dve.tensor_scalar(xn[u][:, b, 0:1, :], x_b, aggr[:, u, b, 0:1], rstd[:, u, b, 0:1],
                                              ALU.subtract, ALU.mult)
                done(t, s, "xn")

            def qk(ph, it, s, bank):
                u, b = s[1:]
                r = rot_of(u, b)
                wait(dve, ph, it, s, "mm")
                heads = bank[:, :].rearrange("p (h d) -> p h d", d=HD1)
                half = HD1 // 2
                by_cos = r[0][:, :].rearrange("p (h d) -> p h d", d=HD1)
                by_sin = r[1][:, :].rearrange("p (h d) -> p h d", d=HD1)
                n = 2 * HEADS
                dve.tensor_tensor(by_cos, heads, rope[:, 0:1, :].broadcast_to([P, n, HD1]), ALU.mult)
                dve.tensor_tensor(by_sin[:, :, 0:half], heads[:, :, half:HD1],
                                  rope[:, 1:2, 0:half].broadcast_to([P, n, half]), ALU.mult)
                done(dve.tensor_tensor(by_sin[:, :, half:HD1], heads[:, :, 0:half],
                                       rope[:, 1:2, half:HD1].broadcast_to([P, n, half]), ALU.mult), s, "halves")

            def scores(ph, it, s, bank):
                wait(dve, ph, it, s, "mm")
                done(dve.tensor_reduce(nmax[:, ph.place[s] % P_RING, :], bank[:, :].rearrange("p (h t) -> p h t", h=QUAD),
                                       AX_X, ALU.max, negate=True), s, "max")

            def turn(ph, it, s, bank):
                copy(ph, it, s, pT_ring[ph.place[s] % PT_RING][:, :], bank[:, :])

            def values(ph, it, s, bank):
                kind, u, b, g = s[1:]
                i = ph.place[s]
                w = head_width(kind) + 1
                r = bank[:, 0:QUAD * w].rearrange("p (h w) -> p h w", w=w)
                wait(dve, ph, it, s, "mm")
                done(dve.reciprocal(rinv[:, i % 2, :], r[:, :, w - 1]), s, "rinv")
                wait(dve, ph, it, s, "rinv")
                done(dve.tensor_tensor(out_of(kind, u, b, g), r[:, :, 0:w - 1],
                                       rinv[:, i % 2, :].unsqueeze(2).broadcast_to([P, QUAD, w - 1]), ALU.mult),
                     s, "normed")

            def dense(ph, it, s, bank):
                u = s[1]
                wait(dve, ph, it, s, "mm")
                x_u = x_all[:, rows(it, u), :]
                done(dve.tensor_tensor(x_u, bank[:, :].rearrange("p (b d) -> p b d", b=ROWS), x_u, ALU.add), s, "added")

            def up1(ph, it, s, bank):
                u, e, j = s[1:]
                wait(dve, ph, it, ("gate1", u, e, j), "silu")
                wait(dve, ph, it, s, "mm")
                done(dve.tensor_tensor(views[u].h1[:, e, 2 * j:2 * j + 2, :], bank[:, :].rearrange("p (f t) -> p f t", f=2),
                                       silu[ph.place[s] % 2].rearrange("p (f t) -> p f t", f=2), ALU.mult), s, "h")

            def k2(ph, it, s, bank):
                u, j = s[1:]
                wait(dve, ph, it, s, "mm")
                for h in range(2):
                    part = slice(h * HD2, (h + 1) * HD2)
                    t = dve.tensor_copy(views[u].k2[part, 2 * j:2 * j + 2, :, h, :],
                                        bank[part, :].rearrange("p (m b t) -> p m b t", m=2, b=ROWS))
                done(t, s, "copied")

            def end(ph, it, s, bank):
                u = s[1]
                x_u = x_all[:, rows(it, u), :]
                if ph.index == 0:
                    wait(dve, ph, it, ("out0", u), "rstd")
                    for b in range(ROWS):
                        t = dve.scalar_tensor_tensor(out=x_all[:, row(it, u, b), :], in0=views[u].fused[:, b:b + 1, :],
                                                     scalar=rstd[:, u, b, 0:1], in1=rows0[:, 1:2, :],
                                                     op0=ALU.mult, op1=ALU.mult)
                    return done(t, s, "done")
                job = final(ph, u)
                wait(dve, ph, it, job, "mm")
                r = ps[ph.bank[job]][:, :].rearrange("p (b d) -> p b d", b=ROWS)
                if ph.layer == 1:
                    t = dve.tensor_tensor(x_u, r, x_u, ALU.add)
                else:
                    n = {("wo", 2): 0, ("w2", 2): 1, ("wo", 3): 2, ("w2", 3): 3}[job[0], ph.layer]
                    t = dve.scalar_tensor_tensor(out=x_u, in0=r, scalar=tgates[:, n:n + 1], in1=x_u,
                                                 op0=ALU.mult, op1=ALU.add)
                done(t, s, "done")

            stages = dict(mem=mem, score0=score0, mix0=mix0, gate0=gate0, out0=out0, norm_self=norm, norm_cross=norm,
                          norm_mlp=norm, norm_q=norm, norm_ff=norm, scale=scale, qk=qk, scores=scores, turn=turn,
                          values=values, dense=dense, up1=up1, k2=k2, end=end)

            dve.wait_ge(consts_in, 16 * 11)
            dve.tensor_copy(pos_f[:, 0, :], pos_i[:, :]).then_inc(setup_v, 1)
            dve.wait_ge(setup_v, 1)
            dve.tensor_scalar(pos_f[:, 1, :], pos_f[:, 0, :], 0.0, float(P), ALU.is_lt, ALU.mult).then_inc(setup_v, 1)
            dve.wait_ge(setup_v, 2)
            dve.tensor_tensor(pos_f[:, 0, :], pos_f[:, 0, :], pos_f[:, 1, :], ALU.add).then_inc(setup_v, 1)
            dve.wait_ge(setup_v, 3)
            dve.tensor_scalar(pos_f[:, 1, :], pos_f[:, 0, :], 0.0, float(P - 1), ALU.max, ALU.min).then_inc(setup_v, 1)
            dve.wait_ge(setup_v, 4)
            dve.tensor_scalar(pos_hot, pos_f[:, 1, :], token[:, 0:1], None, ALU.is_equal).then_inc(setup_v, 1)
            dve.tensor_scalar(vm[:, :, 0], tt[:, 0, :], 1.0, None, ALU.is_equal).then_inc(setup_v, 1)
            dve.tensor_scalar(vm[:, :, 1], tt[:, 1, :], 1.0, None, ALU.is_equal).then_inc(setup_v, 1)
            dve.wait_ge(setup_v, 7)
            dve.tensor_tensor(vm[:, :, 0], vm[:, :, 0], vm[:, :, 1], ALU.mult).then_inc(setup_v, 1)
            dve.wait_ge(setup_v, 8)
            dve.tensor_scalar(vm[:, :, 1], vm[:, :, 0], -1.0, 1.0, ALU.mult, ALU.add).then_inc(setup_v, 1)
            dve.tensor_scalar(media16[:, :, :], media[:, :].rearrange("p (b t) -> p b t", b=B), 0.0, MASKED,
                              ALU.is_equal, ALU.mult).then_inc(setup_v, 1)
            dve.memset(ones16[:, :], 1.0).then_inc(setup_v, 1)
            dve.tensor_copy(ident16[:, :], ident[:, :]).then_inc(setup_v, 1)
            dve.tensor_copy(causal16[:, :], causal[:, :]).then_inc(setup_v, 1)
            dve.memset(minus_half[:, :], -0.5).then_inc(setup_v, 1)
            dve.memset(eps[:, 0, :], EPS_RMS).then_inc(setup_v, 1)
            dve.memset(eps[:, 1, :], EPS_LN).then_inc(setup_v, 1)
            dve.wait_ge(setup_pe, 1)
            dve.tensor_copy(rope[:, :, :], ps[0][:, 0:2 * HD1].rearrange("p (a d) -> p a d", a=2)).then_inc(setup_v, 1)
            dve.wait_ge(setup_v, VECTOR_SETUP)
            dve.wait_ge(setup_a, SCALAR_SETUP)
            dve.wait_ge(primed, 1)

            def ready(ph):
                if ph.index in (1, 3):
                    dve.wait_ge(zeroed, 1 if ph.index == 1 else 2)

            run(dve, stages, ready)

        @block.scalar
        def _(act):
            def done(ins, s, event):
                ins.then_inc(sems[s[0], event], 1)

            def copy(ph, it, s, dst, src, scale=1.0, event="copied", func=ACT.Copy):
                wait(act, ph, it, s, "mm")
                done(act.activation(dst, src, func, scale=scale), s, event)

            def memT(ph, it, s, bank):
                copy(ph, it, s, views[s[1]].memT, bank[:, :].rearrange("p (c t) -> p c t", c=DC), D ** -0.5)

            def score0(ph, it, s, bank):
                u = s[1]
                wait(act, ph, it, s, "max")
                for b in range(ROWS):
                    t = act.activation(p_ring[u][:, b * P:(b + 1) * P], bank[:, b * P:(b + 1) * P], ACT.Exp,
                                       bias=nmax[:, u, b:b + 1], accum_out=rsum0[:, u, b:b + 1])
                done(t, s, "exp")

            def turn0(ph, it, s, bank):
                copy(ph, it, s, pT_ring[s[1]][:, 0:TOK], bank[:, 0:TOK])

            def mixT(ph, it, s, bank):
                copy(ph, it, s, hT[s[1]][:, 1024:1536], bank[:, :])

            def out0(ph, it, s, bank):
                w = views[s[1]]
                wait(act, ph, it, ("gate0", s[1]), "biased")
                done(act.activation(w.z, w.z, ACT.Tanh, scale=0.5), s, "tanh")

            def expertT(ph, it, s, bank):
                u, e = s[1], 0 if s[0] == "xvT" else 1
                at = VEC["self_w" if ph.index == 1 else "mlp_w"]
                wait(act, ph, it, s, "mm")
                for c in range(DC):
                    t = act.activation(xT[u][:, e, c, :], bank[:, c * TOK:(c + 1) * TOK], ACT.Copy,
                                       scale=vec[:, at + c:at + c + 1])
                done(t, s, "copied")

            def v1(ph, it, s, bank):
                copy(ph, it, s, v_view("self", s[1])[:, :, :, 0:HD1],
                     bank[:, :].rearrange("p (b h d) -> p b h d", b=ROWS, h=HEADS))

            def qT(ph, it, s, bank):
                copy(ph, it, s, views[s[1]].qT1, bank[:, :].rearrange("p (b c t) -> p b c t", b=ROWS, c=DC), HD1 ** -0.5)

            def scores(ph, it, s, bank):
                i = ph.place[s]
                wait(act, ph, it, s, "max")
                before, back = ph.earlier(("turn",) + s[1:], P_RING)
                wait(act, ph, it, before, "copied", back)
                for j in range(QUAD):
                    part = slice(j * P, (j + 1) * P)
                    t = act.activation(p_ring[i % P_RING][:, part], bank[:, part], ACT.Exp,
                                       bias=nmax[:, i % P_RING, j:j + 1])
                done(t, s, "exp")

            def kT(ph, it, s, bank):
                wait(act, ph, it, spreads("self", s[1])[-1], "done", back=1)
                copy(ph, it, s, views[s[1]].k_flat, bank[:, :], event="flat")

            def ck(ph, it, s, bank):
                wait(act, ph, it, spreads("cross", s[1])[-1], "done", back=1)
                copy(ph, it, s, views[s[1]].ck_flat, bank[:, 0:TOK], event="flat")

            def maskedT(ph, it, s, bank):
                u, b = s[1:]
                copy(ph, it, s, views[u].oT1[:, b, :, :, :],
                     bank[:, :].rearrange("p (e c t) -> p e c t", e=EXPERTS, c=DC))

            def nT(ph, it, s, bank):
                u = s[1]
                wait(act, ph, it, s, "mm")
                for c in range(DC):
                    if ph.index == 1:
                        at = VEC["cross_w"] + c
                        t = act.activation(xT[u][:, 0, c, :], bank[:, c * TOK:(c + 1) * TOK], ACT.Copy,
                                           scale=vec[:, at:at + 1])
                    else:
                        name = "q" if ph.index in (3, 5) else "ff"
                        g, a = (VEC[f"{name}_{x}{ph.layer}"] + c for x in "gb")
                        t = act.activation(xT[u][:, 0, c, :], bank[:, c * TOK:(c + 1) * TOK], ACT.Identity,
                                           scale=vec[:, g:g + 1], bias=vec[:, a:a + 1])
                done(t, s, "copied")

            def cq(ph, it, s, bank):
                copy(ph, it, s, views[s[1]].cqT, bank[:, 0:TOK], HDC ** -0.5)

            def cv(ph, it, s, bank):
                copy(ph, it, s, v_view("cross", s[1])[:, :, :, 0:HDC],
                     bank[:, 0:TOK].rearrange("p (b h d) -> p b h d", b=ROWS, h=HEADS))

            def coT(ph, it, s, bank):
                copy(ph, it, s, views[s[1]].coT, bank[:, 0:TOK])

            def gate1(ph, it, s, bank):
                before, back = ph.earlier(s, 2)
                wait(act, ph, it, ("up1",) + before[1:], "h", back)
                copy(ph, it, s, silu[ph.place[s] % 2], bank[:, :], event="silu", func=ACT.Silu)

            def q2(ph, it, s, bank):
                u, j = s[1:]
                copy(ph, it, s, views[u].qT2[:, 2 * j:2 * j + 2, :], bank[:, :].rearrange("p (m t) -> p m t", m=2),
                     HD2 ** -0.5)

            def v2(ph, it, s, bank):
                u, b, j = s[1:]
                copy(ph, it, s, v_view("media", u)[:, b, j * 8:(j + 1) * 8, 0:HD2],
                     bank[:, :].rearrange("p (h d) -> p h d", d=HD2))

            def oT2(ph, it, s, bank):
                u, b, j = s[1:]
                copy(ph, it, s, views[u].oT2[:, 4 * j:4 * j + 4, b * P:(b + 1) * P],
                     bank[:, :].rearrange("p (m t) -> p m t", m=4))

            def w1(ph, it, s, bank):
                u, j = s[1:]
                copy(ph, it, s, views[u].h2[:, 2 * j:2 * j + 2, :], bank[:, :].rearrange("p (f t) -> p f t", f=2),
                     event="gelu", func=ACT.Gelu)

            stages = dict(memT=memT, score0=score0, turn0=turn0, mixT=mixT, out0=out0, xvT=expertT, xlT=expertT,
                          v1=v1, qT=qT, kT=kT, ck=ck, scores=scores, maskedT=maskedT, nT=nT, cq=cq, cv=cv, coT=coT, gate1=gate1,
                          q2=q2, v2=v2, oT2=oT2, w1=w1)

            act.wait_ge(consts_in, 16 * 11)
            act.activation(tgates[:, :], gates[:, :], ACT.Tanh).then_inc(setup_a, 1)
            act.wait_ge(primed, 1)

            def ready(ph):
                if ph.index in (1, 3):
                    act.wait_ge(zeroed, 1 if ph.index == 1 else 2)

            run(act, stages, ready)

        @block.gpsimd
        def _(pool):
            def done(ins, s, event):
                ins.then_inc(sems[s[0], event], 1)

            def to_rstd(ph, it, s, bank):
                u = s[1]
                rms = ph.layer < 2
                experts = s[0] in ("norm_self", "norm_mlp")
                mean, var = aggr[:, u, :, 0], aggr[:, u, :, 1]
                wait(pool, ph, it, s, "aggr")
                if rms:
                    done(pool.tensor_tensor(ms[:, u, 0, :], mean, mean, ALU.mult), s, "square")
                    wait(pool, ph, it, s, "square")
                    done(pool.tensor_tensor(ms[:, u, 1, :], ms[:, u, 0, :], var, ALU.add), s, "mean")
                    wait(pool, ph, it, s, "mean")
                    var = ms[:, u, 1, :]
                done(pool.tensor_tensor(ms[:, u, 2, :], var, eps[:, 0 if rms else 1, :], ALU.add), s, "eps")
                if experts:
                    pool.tensor_copy(vm_here[:, u, :, :], vm[:, rows(it, u), :])
                wait(pool, ph, it, s, "eps")
                r = ms[:, u, 3, :] if experts else rstd[:, u, :, 0]
                done(pool.tensor_tensor(r, ms[:, u, 2, :], minus_half[:, :], ALU.pow), s, "pow" if experts else "rstd")
                if experts:
                    wait(pool, ph, it, s, "pow")
                    done(pool.tensor_tensor(rstd[:, u, :, :], ms[:, u, 3, :].unsqueeze(2).broadcast_to([P, ROWS, EXPERTS]),
                                            vm_here[:, u, :, :], ALU.mult), s, "rstd")

            def qk(ph, it, s, bank):
                u, b = s[1:]
                wait(pool, ph, it, s, "halves")
                done(pool.tensor_tensor(qk_of(u, b), *rot_of(u, b), ALU.add), s, "sum")

            def mask(ph, it, s, bank):
                u, b = s[1:]
                wait(pool, ph, it, ("values", "self", u, b, GROUPS - 1), "normed")
                done(pool.tensor_tensor(xn[u][:, b, :, :],
                                        o[u][:, 1024 + b * D:1024 + (b + 1) * D].unsqueeze(1).broadcast_to([P, EXPERTS, D]),
                                        vm_here[:, u, b, :].unsqueeze(2).broadcast_to([P, EXPERTS, D]), ALU.mult),
                     s, "done")

            def spread_keys(ph, it, s, bank):
                kind, u, b, half = s[1:]
                w = views[u]
                wait(pool, ph, it, ({"self": "kT", "cross": "ck"}[kind], u), "flat")
                if (b, half) == (0, 0):
                    other, back = ("cross", 1) if kind == "self" else ("self", 0)
                    wait(pool, ph, it, ("scores", other, u, ROWS - 1, GROUPS - 1), "exp", back)
                n = HEADS // 2
                if kind == "self":
                    src, rows_of = w.k_flat[:, (2 * b + half) * P:(2 * b + half + 1) * P], head_rows[:, 0:n]
                else:
                    src, rows_of = w.ck_flat[:, b * P:(b + 1) * P], head_rows[:, (half + 1) * n:(half + 2) * n]
                done(pool.tensor_tensor(w.k1[:, b, half * n:(half + 1) * n, :], src.unsqueeze(1).broadcast_to([P, n, P]),
                                        rows_of.unsqueeze(2).broadcast_to([P, n, P]), ALU.mult), s, "done")

            stages = dict(spread=spread_keys, out0=to_rstd, norm_self=to_rstd, norm_mlp=to_rstd,
                          norm_cross=to_rstd, norm_q=to_rstd, norm_ff=to_rstd, qk=qk, mask=mask)

            pool.wait_ge(setup_v, VECTOR_SETUP)
            pool.wait_ge(primed, 1)
            def ready(ph):
                if ph.index == 0:
                    for u in range(UNITS):
                        for kind in ("self", "cross"):
                            t = pool.memset(v_view(kind, u)[:, :, :, head_width(kind)], 1.0)
                    t.then_inc(zeroed, 1)
                if ph.index == 3:
                    wait(pool, PHASES[1], ITERS - 1, ("end", B_), "done")
                    for u in range(UNITS):
                        pool.memset(v_view("media", u)[:, :, :, HD2], 1.0)
                        t = pool.memset(kbd[u][:, :], 0.0)
                    t.then_inc(zeroed, 1)

            run(pool, stages, ready)



def by_chunk(w, rows_to=None):
    k, n = w.shape
    rows_to = rows_to or k
    if rows_to > k:
        w = np.concatenate([w, np.zeros((rows_to - k, n), w.dtype)])
    return w.reshape(rows_to // P, P, n).transpose(1, 0, 2).reshape(P, -1)


def wide(w, cols):
    return np.concatenate([w, np.zeros((w.shape[0], cols - w.shape[1]), w.dtype)], axis=1)


def kernel(**inputs):
    import concourse.bacc as bacc
    from concourse.bass_utils import run_bass_kernel_spmd

    a = {k: np.asarray(v) for k, v in inputs.items()}
    l0 = lambda n: a["L0_xattn_" + n]
    l1 = lambda n: a["L1_xattn_" + n]
    arrays = {
        "x": a["x"].transpose(1, 0, 2),
        "xT": a["x"].transpose(2, 0, 1).reshape(DC, P, B * P).transpose(1, 0, 2),
        "ctxT": a["ctx_1024"].transpose(2, 0, 1),
        "w0": np.concatenate([l0("W_mem").T, by_chunk(l0("W_gate").T)], axis=1),
        "rows0": np.broadcast_to(np.stack([l0("b_gate"), l0("norm_w")]), (P, 2, D)),
        "w1a": np.concatenate(
            [by_chunk(l1(n)) for n in ("v_qkv", "l_qkv", "v_dense", "l_dense", "cq_w", "ckv_w", "cdense_w")], axis=1),
        "w1b": np.concatenate(
            [by_chunk(wide(l1(n), F1C * P)) for n in ("v_gate", "v_up", "l_gate", "l_up")]
            + [by_chunk(l1(n), F1C * P) for n in ("v_down", "l_down")], axis=1),
    }
    for n in (2, 3):
        ln = lambda name: a[f"L{n}_xattn_{name}"]
        arrays[f"w{n}a"] = np.concatenate([by_chunk(ln("Wq")), ln("Wkv"), by_chunk(ln("Wo"))], axis=1)
        arrays[f"w{n}b"] = np.concatenate([by_chunk(ln("W1")), by_chunk(ln("W2"))], axis=1)
    vecs = [l1("ln_in_w"), l1("ln_post_cross_w"), l1("ln_post_attn_w")]
    for n in (2, 3):
        vecs += [a[f"L{n}_xattn_ln_{x}"] for x in ("q_g", "q_b", "ff_g", "ff_b")]
    arrays["vec"] = np.stack(vecs).reshape(-1, DC, P).transpose(2, 0, 1).reshape(P, -1)
    arrays["gates"] = np.broadcast_to(
        np.concatenate([a["L2_xattn_attn_gate"], a["L2_xattn_ff_gate"], a["L3_xattn_attn_gate"], a["L3_xattn_ff_gate"]]),
        (P, 4))
    kinds = a["mask_BxS_ik0"].T
    arrays["tt"] = np.stack([kinds, np.concatenate([kinds[1:], np.zeros((1, B), kinds.dtype)])], axis=1)
    arrays["media"] = a["mask_BxS2_bk0"].reshape(1, B * P)
    arrays["pos"] = np.broadcast_to(a["pos_1xS"], (P, P))
    f = np.float32
    inv = f(1.0) / f(ROPE_BASE) ** (np.arange(0, HD1, 2, dtype=f) / f(HD1))
    freq = np.outer(np.arange(P, dtype=f), inv).astype(f)
    arrays["rope_tab"] = np.concatenate([np.cos(freq), np.cos(freq), -np.sin(freq), np.sin(freq)], axis=1).astype(f)
    arrays["token"] = np.arange(P, dtype=f).reshape(P, 1)
    arrays["ident"] = np.eye(P, dtype=f)
    arrays["causal"] = np.where(np.tril(np.ones((P, P), bool)), f(0), f(MASKED))
    part = np.arange(P)[:, None]
    arrays["head_rows"] = np.concatenate(
        [part // HD1 == np.arange(P // HD1), part // HDC == np.arange(P // HDC)], axis=1).astype(f)

    nc = bacc.Bacc("TRN2", target_bir_lowering=False, num_devices=1)
    given, dram = {}, {}
    for name, array in arrays.items():
        array = np.ascontiguousarray(array)
        given[f"in_{name}"] = array
        dram[name] = nc.dram_tensor(f"in_{name}", array.shape, mybir.dt.from_np(array.dtype), kind="ExternalInput").ap()
    out = nc.dram_tensor("out", (P, B, D), F32, kind="ExternalOutput").ap()
    build(nc, dram, out)
    result = run_bass_kernel_spmd(nc, [given], core_ids=[0])
    return result.results[0]["out"].transpose(1, 0, 2)
```

```python
from contextlib import ExitStack

import numpy as np

import concourse.bass as bass
from concourse import mybir

F32 = mybir.dt.float32
F32R = mybir.dt.float32r
BF16 = mybir.dt.bfloat16
I32 = mybir.dt.int32
U8 = mybir.dt.uint8
ALU = mybir.AluOpType
ACT = mybir.ActivationFunctionType
AX_X = mybir.AxisListType.X

P = 128
B = 16
D = 256
DC = D // P
ROWS = 2
UNITS = 2
ITERS = B // (ROWS * UNITS)
TOK = ROWS * P
BANKS = 8
BANK = 512

HEADS = 16
QUAD = 4
GROUPS = HEADS // QUAD
HD1 = D // HEADS
HDC = P // HEADS
HD2 = 64
INNER = HEADS * HD2
IC = INNER // P
EXPERTS = 2
FF1 = 688
F1C = -(-FF1 // P)
FF2 = 1024
F2C = FF2 // P
ROPE_BASE = 10000.0
EPS_RMS = 1e-6
EPS_LN = 1e-5
MASKED = -(2.0 ** 100)

P_RING = 4
PT_RING = 2
SKEW_T = 2
SKEW_O = 3



def layout(parts):
    table, at = {}, 0
    for name, chunks, width in parts:
        table[name] = (at, chunks, width)
        at += chunks * width
    return table, at


CONSTS, CONSTS_COLS = layout([("ident", 1, P), ("causal", 1, P), ("head_rows", 1, 8 + HEADS), ("rope_tab", 1, 2 * HD1),
                              ("token", 1, 1), ("gates", 1, 4), ("vec", 1, DC * 11), ("rows0", 2, D)])
W0, W0_COLS = layout([("mem", 1, D), ("gate", 2 * DC, D)])
W1A, W1A_COLS = layout([("qkv0", DC, 3 * D), ("qkv1", DC, 3 * D), ("dense0", DC, D), ("dense1", DC, D),
                        ("cq", DC, P), ("ckv", 1, 2 * P), ("cdense", 1, D)])
W1B, W1B_COLS = layout([("gate0", DC, F1C * P), ("up0", DC, F1C * P), ("gate1", DC, F1C * P),
                        ("up1", DC, F1C * P), ("down0", F1C, D), ("down1", F1C, D)])
W2A, W2A_COLS = layout([("q", DC, INNER), ("kv", 1, 2 * INNER), ("o", IC, D)])
W2B, W2B_COLS = layout([("w1", DC, FF2), ("w2", F2C, D)])
WA_COLS = max(W1A_COLS, W2A_COLS)
WF_COLS = max(W0_COLS, W1B_COLS, 2 * W2B_COLS + IC * D)
PIECE = 512

VEC = {n: DC * i for i, n in enumerate(
    ["self_w", "cross_w", "mlp_w", "q_g2", "q_b2", "ff_g2", "ff_b2", "q_g3", "q_b3", "ff_g3", "ff_b3"])}



A_, B_ = range(UNITS)


def here(*steps):
    return [(s, 0) for s in steps]


def ahead(*steps):
    return [(s, 1) for s in steps]


def attention(streams):
    groups = [(kind, u, b, g) for kind, u in streams for b in range(ROWS) for g in range(GROUPS)]
    slots = []
    for i in range(len(groups) + SKEW_O):
        slot = []
        if i < len(groups):
            slot += here(("scores",) + groups[i])
        if 0 <= i - SKEW_T < len(groups):
            slot += here(("turn",) + groups[i - SKEW_T])
        if 0 <= i - SKEW_O < len(groups):
            slot += here(("values",) + groups[i - SKEW_O])
        slots.append(slot)
    return slots


def weave(slots, *sides):
    filled = [list(slot) for slot in slots]
    for steps, first, last in sides:
        n = last - first + 1
        for i, s in enumerate(steps):
            if s[0]:
                filled[first + i * n // len(steps)].append(s)
    return [s for slot in filled for s in slot]


def pre_memory(u):
    return [(k, u) for k in ("memT", "mem", "score0", "turn0", "mix0")]


def pre_self(u):
    return [("xvT", u), ("xlT", u), ("qk", u, 0), ("qk", u, 1), ("v1", u), ("kT", u), ("qT", u)] + spreads("self", u)


def spreads(kind, u):
    return [("spread", kind, u, b, half) for b in range(ROWS) for half in range(2)]


def pre_mlp1(u):
    return [("xvT2", u), ("xlT2", u)]


def pre_attn2(u):
    keys_and_values = [s for j in range(IC // 2) for s in (("k2", u, j), ("v2", u, j // 2, j % 2))]
    return [("nT2", u)] + keys_and_values + [("q2", u, j) for j in range(IC // 2)]


def pre_ff2(u):
    return [("nT2", u)]




def steps_memory(norms, pre):
    def half(u, first, end):
        return (first[0:1] + here(("mixT", u)) + first[1:3] + end + here(("gate0", u)) + first[3:]
                + here(("out0", u)))

    of_a, end_a, end_b = half(A_, here(*pre_memory(B_)), []), here(("end", A_)), here(("end", B_))
    if norms:
        return of_a + end_a + half(B_, ahead(*norms) + ahead(*pre), []) + end_b
    return of_a + half(B_, ahead(*pre), end_a) + end_b


def steps_self(norms, pre):
    n = ROWS * GROUPS
    sides = []
    for u in range(UNITS):
        keys = spreads("cross", u)
        for slot, steps in ((0, [("ck", u), ("cv", u), ("mask", u, 0), keys[0]]), (1, [keys[1], ("maskedT", u, 0)]),
                            (2, [("mask", u, 1)]), (3, [keys[2], ("maskedT", u, 1)]),
                            (4, [("dense", u), ("norm_cross", u)]), (5, [("scale_cross", u), keys[3]]),
                            (6, [("nT", u)]), (7, [("cq", u)])):
            sides.append((here(*steps), (u + 1) * n + slot, (u + 1) * n + slot))
    end = 4 * n + SKEW_O - 1
    return weave(attention([("self", A_), ("self", B_), ("cross", A_), ("cross", B_)]),
                 (here(*pre_self(B_)[2:]), 0, n - 1),
                 *sides,
                 (ahead(*norms[0:2]), 2 * n + 1, 2 * n + 2),
                 (ahead(*norms[2:]), 3 * n, 3 * n + 1),
                 (ahead(*pre[0:2]), 3 * n, 3 * n),
                 (ahead(*pre[2:-2]), 3 * n + 2, 4 * n),
                 (here(("coT", A_)), 3 * n + SKEW_O, 3 * n + SKEW_O),
                 (here(("cdense", A_), ("end", A_)), 3 * n + SKEW_O + 1, 3 * n + SKEW_O + 1),
                 (ahead(*pre[2:][-2:-1]), end, end),
                 (here(("coT", B_)), end, end),
                 (ahead(*pre[2:][-1:]), end, end),
                 (here(("cdense", B_), ("end", B_)), end, end))


def steps_mlp1(norms, pre):
    def hidden(u):
        return [(k, u, e, j) for e in range(EXPERTS) for j in range(F1C // 2) for k in ("gate1", "up1")]

    h = len(hidden(A_))
    return weave([here(s) for s in hidden(A_) + hidden(B_) + [("down", A_), ("down", B_)]],
                 (here(*pre_mlp1(B_)), 3, 4),
                 (ahead(*norms[0:2]), h, h + 4),
                 (ahead(*norms[2:3]), 2 * h, 2 * h),
                 (here(("end", A_), ("end", B_)), 2 * h, 2 * h + 1),
                 (ahead(*pre[:2]), 2 * h, 2 * h),
                 (ahead(*pre[2:]), 2 * h, 2 * h + 1),
                 (ahead(*norms[3:]), 2 * h + 1, 2 * h + 1))


def steps_attn2(norms, pre):
    def low(u):
        return here(*[("oT2_low", u, b, j) for b in range(ROWS) for j in range(2)])

    n = ROWS * GROUPS
    end = 2 * n + SKEW_O - 1
    a, b = (here(*[("oT2", u, b, j) for b in range(ROWS) for j in range(2)]) for u in range(UNITS))
    return weave(attention([("media", A_), ("media", B_)]),
                 (here(*pre_attn2(B_)), 0, n - 2),
                 (a, n, n + SKEW_O),
                 (low(A_), n + 1, n + SKEW_O + 1),
                 (here(("wo", A_), ("end", A_)), n + SKEW_O + 2, n + SKEW_O + 2),
                 (ahead(*norms), n, n + 3),
                 (b[0:3], end - 3, end - 1),
                 (low(B_)[0:2], end - 2, end - 1),
                 (ahead(*pre[:-3]), n + SKEW_O + 1, end - 1),
                 (ahead(*pre[-3:-2]), end, end),
                 (b[3:], end, end),
                 (ahead(*pre[-2:]), end, end),
                 (low(B_)[2:], end, end),
                 (here(("wo", B_), ("end", B_)), end, end))


def steps_ff2(norms, pre):
    def hidden(u):
        return [("w1", u, j) for j in range(F2C // 2)]

    h = F2C // 2
    return weave([here(s) for s in hidden(A_) + hidden(B_) + [("w2", A_), ("w2", B_)]],
                 (here(*pre_ff2(B_)), 0, 0),
                 (ahead(*norms), 1, 2 * h - 2),
                 (here(("end", A_), ("end", B_)), 2 * h, 2 * h + 1),
                 (ahead(*pre), 2 * h, 2 * h + 1))


PLAN = [(0, steps_memory, None, pre_memory), (1, steps_self, "self", pre_self),
        (1, steps_mlp1, "mlp", pre_mlp1), (2, steps_attn2, "q", pre_attn2),
        (2, steps_ff2, "ff", pre_ff2), (3, steps_attn2, "q", pre_attn2), (3, steps_ff2, "ff", pre_ff2)]

EVENTS = {
    "memT": "mm copied", "mem": "mm copied", "score0": "mm max exp", "turn0": "mm copied",
    "mix0": "mm rinv normed", "mixT": "mm copied", "gate0": "mm biased",
    "out0": "tanh gated fused stats aggr square mean eps rstd",
    "norm_self": "stats aggr square mean eps pow rstd", "norm_mlp": "stats aggr square mean eps pow rstd",
    "norm_cross": "stats aggr square mean eps rstd", "norm_q": "stats aggr eps rstd",
    "norm_ff": "stats aggr eps rstd", "scale_self": "xn", "scale_cross": "xn", "scale_mlp": "xn",
    "scale_q": "xn", "scale_ff": "xn", "spread": "done",
    "xvT": "mm copied", "xlT": "mm copied", "qk": "mm halves sum", "v1": "mm copied", "qT": "mm copied",
    "kT": "mm flat", "scores": "mm max exp", "turn": "mm copied", "values": "mm rinv normed",
    "mask": "done", "maskedT": "mm copied", "dense": "mm added", "nT": "mm copied",
    "nT2": "mm wide hi lo", "round": "done", "split": "lo", "finish": "hi", "cq": "mm copied", "ck": "mm flat",
    "cv": "mm copied", "coT": "mm copied", "cdense": "mm", "gate1": "mm silu", "up1": "mm product hi h",
    "xvT2": "mm hi lo", "xlT2": "mm hi lo", "zero": "done",
    "down": "mm", "q2": "mm copied", "k2": "mm copied", "v2": "mm copied", "oT2": "mm hi lo", "oT2_low": "",
    "wo": "mm", "w1": "mm gelu hi lo", "w2": "mm", "end": "done",
}
EVENTS = {kind: events.split() for kind, events in EVENTS.items()}
EMPTIED = {k: e[-1] for k, e in EVENTS.items() if e} | {"qk": "halves", "nT2": "wide", "w1": "gelu", "up1": "product"}
LAST = {"cdense", "down", "wo", "w2"}


class Phase:

    def __init__(self, index, before):
        self.index = index
        self.layer, self.weave, norm, pre = PLAN[index]
        self.norms = [(f"{kind}_{norm}", u) for u in range(UNITS) for kind in ("norm", "scale")] if norm else []
        self.pre = pre(A_)
        self.pre += pre(B_)[0:2] if index == 1 else []
        body = self.body = self.weave(self.norms, self.pre)
        self.prologue = [s for s, early in body if early]
        self.own = [s for s, early in body if not early]
        self.of_kind, self.place = {}, {}
        for s in self.prologue + self.own:
            n = self.of_kind.get(s[0], 0)
            self.place[s] = n
            self.of_kind[s[0]] = n + 1
        self.base = dict(before)
        self.after = {k: before.get(k, 0) + ITERS * self.of_kind.get(k, 0) for k in {*before, *self.of_kind}}
        pieces = {2: [("experts", i) for i in range(W1B_COLS // PIECE)]}
        pieces |= {p: [(name, i) for name in ("q", "o") for i in range(DC * INNER // PIECE)] for p in (3, 5)}
        pieces |= {p: [("w", i) for i in range(W2B_COLS // PIECE)] for p in (4, 6)}
        pieces = pieces.get(index, [])
        kinds = ("round", "split", "finish")
        for kind in kinds:
            self.place |= {(kind,) + piece: i for i, piece in enumerate(pieces)}
            self.of_kind[kind] = 0
            self.after[kind] = before.get(kind, 0) + len(pieces)
        self.once = [(kind,) + pieces[i - late] for i in range(len(pieces) + 2)
                     for late, kind in enumerate(kinds) if 0 <= i - late < len(pieces)]
        self.place |= {("zero", n): n for n in range(3)}
        self.of_kind["zero"] = 0
        jobs = [s for s, _ in body if "mm" in EVENTS[s[0]]]
        self.bank = {s: i % BANKS for i, s in enumerate(jobs)}

    def count(self, step, event, it):
        kind = step[0]
        before = PRIME.get((kind, event), 0) + self.base.get(kind, 0)
        return it * self.of_kind[kind] + (before + self.place[step] + 1)

    def earlier(self, step, n):
        same = sorted((s for s in self.place if s[0] == step[0]), key=self.place.get)
        at = self.place[step] - n
        return same[at % len(same)], -(at // len(same))


PHASES = []
for _i in range(len(PLAN)):
    PHASES.append(Phase(_i, PHASES[-1].after if PHASES else {}))


def between(ph):
    if ph is PHASES[0]:
        return [(ph, 0, s) for s in ph.pre]
    if ph is None:
        return [(PHASES[-1], ITERS - 1, s) for s, _ in PHASES[-1].weave([], [])]
    old = PHASES[ph.index - 1]
    steps = [(ph, 0, s) if early else (old, ITERS - 1, s) for s, early in old.weave(ph.norms, ph.pre)]
    once = [(ph, 0, s) for s in ph.once]
    if ph.index == 2:
        of_a, of_b = (steps.index((old, ITERS - 1, ("scores", "cross", u, ROWS - 1, GROUPS - 1))) for u in range(UNITS))
        thirds = [[s for s in once if s[2][2] // 6 == n] for n in range(3)]
        return (steps[:of_a + 1] + spread(steps[of_a + 1:of_b + 1], thirds[0])
                + spread(steps[of_b + 1:], thirds[1]) + thirds[2])
    if ph.index in (3, 5):
        if ph.index == 3:
            last = [(old, ITERS - 1, (kind, B_)) for kind in ("down", "end")]
            steps = [s for s in steps if s not in last]
            at = steps.index((ph, 0, ("v2", A_, 0, 0)))
            steps[at:at] = last + [(ph, 0, ("zero", 2))]
            for e in reversed(range(EXPERTS)):
                at = steps.index((old, ITERS - 1, ("up1", B_, e, F1C // 2 - 1)))
                steps[at + 1:at + 1] = [(ph, 0, ("zero", e))]
        at = steps.index((ph, 0, ("q2", A_, 0)))
        q, o = ([s for s in once if s[2][1] == name] for name in "qo")
        return (steps[:at] + q if ph.index == 3 else spread(steps[:at], q)) + spread(steps[at:], o)
    return spread(steps, once)


def spread(steps, more):
    out, done = [], 0
    for i, s in enumerate(steps):
        n = len(more) * (i + 1) // len(steps)
        out += [s] + more[done:n]
        done = n
    return out


PRIME = {(k, EMPTIED[k]): max(ph.of_kind.get(k, 0) for ph in PHASES) for k in EMPTIED}
for _k in LAST:
    del PRIME[_k, "mm"]
for _k, _e in (("cv", "mm"), ("v2", "mm"), ("mem", "mm"), ("gate0", "mm"), ("out0", "fused"), ("qk", "sum"),
               ("nT2", "mm"), ("nT", "mm"), ("up1", "mm"), ("up1", "h")):
    PRIME[_k, _e] = max(ph.of_kind.get(_k, 0) for ph in PHASES)


def build(nc, dram, out):
    with ExitStack() as ctx:
        def sb(name, shape, dt=F32):
            return ctx.enter_context(nc.sbuf_tensor(name, shape, dt))

        twins = {}

        def sb_twin(name, shape):
            with nc.sbuf_tensor(name, shape, F32) as buf:
                pass
            twins[name] = ctx.enter_context(nc.sbuf_tensor(f"{name}_rounded", shape, F32R))
            return buf

        sems = {}
        for kind, events in EVENTS.items():
            for e in events:
                sems[kind, e] = ctx.enter_context(nc.semaphore(f"{kind}_{e}"))

        def sem(name):
            return ctx.enter_context(nc.semaphore(name))

        consts_in = sem("consts_in")
        weights_att = sem("weights_att")
        weights_ff = sem("weights_ff")
        x_in = [sem(f"x_in{u}") for u in range(UNITS)]
        xT_in = [sem(f"xT_in{u}") for u in range(UNITS)]
        ctx_in = [sem(f"ctx_in{u}") for u in range(UNITS)]
        setup_v = sem("setup_vector")
        setup_pe = sem("setup_tensor")
        setup_a = sem("setup_scalar")
        ones_beside = sem("ones_beside")
        primed = sem("primed")
        out_done = sem("out_done")
        settled = {n: sem(f"settled_{n}") for n in ("vector", "tensor")}

        x_all = sb("x_all", [P, B, D])
        w_att = sb_twin("w_att", [P, WA_COLS])
        w_ff = sb_twin("w_ff", [P, WF_COLS])
        ctxT = [sb(f"ctxT{u}", [P, TOK]) for u in range(UNITS)]
        xn = [sb_twin(f"xn{u}", [P, ROWS, EXPERTS, D]) for u in range(UNITS)]
        xT = [sb_twin(f"xT{u}", [P, EXPERTS, DC, TOK]) for u in range(UNITS)]
        hT = [sb_twin(f"hT{u}", [P, EXPERTS * F1C * TOK]) for u in range(UNITS)]
        kbd = [sb_twin(f"kbd{u}", [P, IC * ROWS * 2 * P]) for u in range(UNITS)]
        v = [sb_twin(f"v{u}", [P, ROWS * HEADS * (HD2 + 1)]) for u in range(UNITS)]
        o = [sb_twin(f"o{u}", [P, ROWS * INNER]) for u in range(UNITS)]
        p_ring = [sb_twin(f"p{i}", [P, BANK]) for i in range(P_RING)]
        pT_ring = [sb_twin(f"pT{i}", [P, BANK]) for i in range(PT_RING)]
        nmax = sb("nmax", [P, P_RING, QUAD])
        rinv = sb("rinv", [P, 2, QUAD])
        rsum0 = sb("rsum0", [P, UNITS, ROWS])
        rinv0 = sb("rinv0", [P, UNITS, ROWS])
        stats = sb("stats", [P, UNITS, ROWS, 6])
        aggr = sb("aggr", [P, UNITS, ROWS, 2])
        ms = sb("ms", [P, UNITS, 4, ROWS])
        rstd = sb("rstd", [P, UNITS, ROWS, EXPERTS])
        vm_here = sb("vm_here", [P, UNITS, ROWS, EXPERTS])
        minus_half = sb("minus_half", [P, ROWS])
        eps = sb("eps", [P, 2, ROWS])
        consts = sb("consts", [P, CONSTS_COLS])
        const = {n: consts[:, at:at + chunks * w] for n, (at, chunks, w) in CONSTS.items()}
        ident, causal, head_rows, rope_tab = (const[n] for n in ("ident", "causal", "head_rows", "rope_tab"))
        vec, gates = const["vec"], const["gates"]
        token = const["token"]
        rows0 = const["rows0"].rearrange("p (a d) -> p a d", a=2)
        ident16 = sb("ident16", [P, P], BF16)
        causal16 = sb("causal16", [P, P], BF16)
        rope = sb("rope", [P, 2, HD1])
        tgates = sb("tgates", [P, 4])
        tt = sb("tt", [P, 2, B], I32)
        vm = sb("vm", [P, B, EXPERTS])
        media = p_ring[2][0:1, :].bitcast(U8)
        media16 = sb("media16", [1, B, P], BF16)
        ones16 = sb("ones16", [1, P], BF16)
        pos_i = pT_ring[0][:, 0:P].bitcast(I32)
        pos_f = pT_ring[1][:, 0:2 * P].rearrange("p (a t) -> p a t", a=2)
        pos_hot = p_ring[0][:, 0:P]
        ps = [ctx.enter_context(nc.psum_tensor(f"bank{k}", [P, BANK], F32)) for k in range(BANKS)]

        silu = [o[i][:, 0:BANK] for i in range(2)]

        def rot_of(u, b):
            both_ = (hT[u][:, 2048:3072], xn[u][:, :, :, :].rearrange("p b e d -> p (b e d)"))[b]
            return both_[:, 0:BANK], both_[:, BANK:2 * BANK]

        def qk_of(u, b):
            return o[u][:, b * BANK:(b + 1) * BANK]

        def weight(buf, table, name):
            at, chunks, width = table[name]
            return buf[:, at:at + chunks * width].rearrange("p (c n) -> p c n", c=chunks)

        def rounded(ap):
            return bass.AP(twins[ap.tensor.name], ap.offset, ap.ap)

        def piece(s):
            name, i = s[1:]
            part = slice(i * PIECE, (i + 1) * PIECE)
            if name == "experts":
                third, at = divmod(i, 6)
                low = kbd[third][:, at * PIECE:(at + 1) * PIECE] if third < 2 else \
                    v[at // 3][:, at % 3 * PIECE:(at % 3 + 1) * PIECE]
                return w_ff[:, part], low
            if name == "w":
                return w_ff[:, part], w_ff[:, W2B_COLS:][:, part]
            if name == "o":
                return w_att[:, W2A["o"][0]:][:, part], o_low[:, part]
            return w_att[:, part], q_low(i // 2)[:, (i % 2) * PIECE:(i % 2 + 1) * PIECE]

        ff_low = w_ff[:, W2B_COLS:2 * W2B_COLS]
        o_low = w_ff[:, 2 * W2B_COLS:2 * W2B_COLS + IC * D]

        def q_low(c):
            return hT[c][:, IC * TOK:IC * TOK + INNER]

        def expert_low(name, e):
            if name == "down":
                return v[e][:, 0:F1C * D].rearrange("p (c n) -> p c n", c=F1C)
            at = 0 if name == "gate" else DC * F1C * P
            return kbd[e][:, at:at + DC * F1C * P].rearrange("p (c n) -> p c n", c=DC)

        def x_low1(u, e):
            return xn[u][:, :, :, :].rearrange("p b e d -> p (b e) d")[:, e * DC:(e + 1) * DC, :]

        def h_low1(u, e, j):
            i = 3 * e + j
            rings = (p_ring[2 * u], p_ring[2 * u + 1], pT_ring[u])
            low = o[u][:, (i + 1) * BANK:(i + 2) * BANK] if i < 3 else rings[i - 3][:, :]
            return low.rearrange("p (f t) -> p f t", f=2)

        def x_low(u, c):
            return xn[u][:, c, 1, :]

        def head_width(kind):
            return {"self": HD1, "cross": HDC, "media": HD2}[kind]

        def v_view(kind, u):
            w = head_width(kind) + 1
            at = ROWS * HEADS * (HD1 + 1) if kind == "cross" else 0
            return v[u][:, at:at + ROWS * HEADS * w].rearrange("p (b h w) -> p b h w", b=ROWS, h=HEADS)

        class View:
            pass

        views = []
        for u in range(UNITS):
            w = View()
            h = hT[u]
            w.qT1 = h[:, 0:512].rearrange("p (b c t) -> p b c t", b=ROWS, c=DC)
            w.oT1 = h[:, 512:1536].rearrange("p (b e c t) -> p b e c t", b=ROWS, e=EXPERTS, c=DC)
            w.cqT = h[:, 1536:1792]
            w.coT = h[:, 1792:2048]
            w.qT2 = h[:, 0:IC * TOK].rearrange("p (m t) -> p m t", m=IC)
            w.oT2 = w.qT2
            w.h1 = h[:, :].rearrange("p (e f t) -> p e f t", e=EXPERTS, f=F1C)
            w.h2 = h[:, 0:F2C * TOK].rearrange("p (f t) -> p f t", f=F2C)
            w.h2_low = o[u][:, :].rearrange("p (f t) -> p f t", f=F2C)
            w.k_flat = h[:, 512:1024]
            w.ck_flat = h[:, 2048:2304]
            w.k1 = kbd[u][:, :].rearrange("p (b h t) -> p b h t", b=ROWS, h=HEADS)
            w.k2 = kbd[u][:, :].rearrange("p (m b s t) -> p m b s t", m=IC, b=ROWS, s=2)
            w.x0 = o[u][:, 0:512].rearrange("p (b d) -> p b d", b=ROWS)
            w.mix = o[u][:, 512:1024].rearrange("p (b d) -> p b d", b=ROWS)
            w.z = o[u][:, 1024:1536].rearrange("p (b d) -> p b d", b=ROWS)
            w.fused = o[u][:, 1536:2048].rearrange("p (b d) -> p b d", b=ROWS)
            w.xT0 = h[:, 0:512].rearrange("p (c t) -> p c t", c=DC)
            w.memT = h[:, 512:1024].rearrange("p (c t) -> p c t", c=DC)
            w.mixT = h[:, 1024:1536].rearrange("p (b c t) -> p b c t", b=ROWS, c=DC)
            w.mem = kbd[u][:, 0:512].rearrange("p (b d) -> p b d", b=ROWS)
            views.append(w)

        def out_of(kind, u, b, g):
            w = head_width(kind)
            at = {"self": b * D, "cross": 512 + b * P, "media": b * INNER}[kind] + (1024 if kind != "media" else 0)
            return o[u][:, at + g * QUAD * w:at + (g + 1) * QUAD * w].rearrange("p (h w) -> p h w", w=w)

        def rows(it, u):
            return bass.ds(it * (UNITS * ROWS) + u * ROWS, ROWS)

        def row(it, u, b):
            return bass.ds(it * (UNITS * ROWS) + (u * ROWS + b), 1)

        def after(ph, it, step, event, back=0):
            return sems[step[0], event], ph.count(step, event, it - back)

        def split(ph, name, i):
            return sems["finish", "hi"], ph.count(("finish", name, i), "hi", 0)

        def settle(eng, name):
            eng.sem_inc(settled[name], 1)

        def final(ph, u):
            return [s for s in ph.own if s[0] in LAST and s[1] == u][0]

        def run(eng, stages):
            for ph in PHASES:
                for p, it, s in between(ph):
                    if s[0] in stages:
                        stages[s[0]](p, it, s, ps[p.bank[s]] if s in p.bank else None)
                with eng.Fori(0, ITERS - 1) as it:
                    for s, early in ph.body:
                        if s[0] in stages:
                            stages[s[0]](ph, it + early, s, ps[ph.bank[s]] if s in ph.bank else None)
            for p, it, s in between(None):
                if s[0] in stages:
                    stages[s[0]](p, it, s, ps[p.bank[s]] if s in p.bank else None)

        VECTOR_SETUP = 17
        SCALAR_SETUP = 1
        ATT_LOADS = {1: 1, 3: 2, 5: 3}
        FF_LOADS = {0: 1, 2: 2, 4: 3, 6: 4}
        CTX_BEFORE = {1: ITERS, 3: 2 * ITERS, 5: 3 * ITERS}

        block = ctx.enter_context(nc.Block())

        @block.sync
        def _(sp):
            def load_memory(it, u):
                sp.dma_start(ctxT[u][:, :].rearrange("p (b t) -> p b t", b=ROWS),
                             dram["ctxT"][:, rows(it, u), :]).then_inc(ctx_in[u], 16)

            def load_xT(it, u):
                sp.dma_start(views[u].xT0, dram["xT"][:, :, bass.ds(it * (UNITS * TOK) + u * TOK, TOK)])\
                  .then_inc(xT_in[u], 16)

            def load_x(it, u):
                sp.dma_start(views[u].x0, dram["x"][:, rows(it, u), :]).then_inc(x_in[u], 16)

            sp.dma_start(w_ff[:, 0:W0_COLS], dram["w0"]).then_inc(weights_ff, 16)
            for u in range(UNITS):
                load_memory(0, u)
                load_xT(0, u)
            for dst, src in ((consts, "consts"), (pos_i, "pos"), (tt, "tt"), (media, "media")):
                sp.dma_start(dst[:, :] if len(dst.shape) == 2 else dst[:, :, :], dram[src]).then_inc(consts_in, 16)
            for u in range(UNITS):
                load_x(0, u)
            sp.dma_start(w_att[:, 0:W1A_COLS], dram["w1a"]).then_inc(weights_att, 16)
            sp.wait_ge(primed, 1)

            def load_ctx(ph, it, u, reader):
                sp.wait_ge(*after(ph, it, reader, "mm", back=1))
                load_memory(it, u)

            def ended(ph):
                sp.wait_ge(*after(ph, ITERS - 1, ("end", B_), "done"))

            for ph in PHASES:
                if ph.index == 0:
                    with sp.Fori(1, ITERS) as it:
                        for u in range(UNITS):
                            load_ctx(ph, it, u, ("mem", u))
                        for u in range(UNITS):
                            sp.wait_ge(*after(ph, it, ("gate0", u), "mm", back=1))
                            load_xT(it, u)
                            sp.wait_ge(*after(ph, it, ("out0", u), "fused", back=1))
                            load_x(it, u)
                if ph.index == 1:
                    for u in range(UNITS):
                        sp.wait_ge(*after(PHASES[0], ITERS - 1, ("mem", u), "mm"))
                        load_ctx(ph, 0, u, ("cv", u))
                    ended(PHASES[0])
                    sp.dma_start(w_ff[:, 0:W1B_COLS], dram["w1b"]).then_inc(weights_ff, 16)
                    with sp.Fori(1, ITERS) as it:
                        for u in range(UNITS):
                            load_ctx(ph, it, u, ("cv", u))
                    ended(ph)
                    sp.dma_start(w_att[:, 0:W2A_COLS], dram["w2a"]).then_inc(weights_att, 16)
                if ph.index in (3, 5):
                    reader = lambda u: ("v2", u, ROWS - 1, 1)
                    for u in range(UNITS):
                        before, last = (PHASES[1], ("cv", u)) if ph.index == 3 else (PHASES[3], reader(u))
                        sp.wait_ge(*after(before, ITERS - 1, last, "mm"))
                        load_ctx(ph, 0, u, reader(u))
                    ended(PHASES[ph.index - 1])
                    sp.dma_start(w_ff[:, 0:W2B_COLS], dram["w2b" if ph.index == 3 else "w3b"])\
                      .then_inc(weights_ff, 16)
                    with sp.Fori(1, ITERS) as it:
                        for u in range(UNITS):
                            load_ctx(ph, it, u, reader(u))
                    if ph.index == 3:
                        ended(ph)
                        sp.dma_start(w_att[:, 0:W2A_COLS], dram["w3a"]).then_inc(weights_att, 16)
                if ph.index == 6:
                    with sp.Fori(0, ITERS) as it:
                        for u in range(UNITS):
                            sp.wait_ge(*after(ph, it, ("end", u), "done"))
                            sp.dma_start(out[:, rows(it, u), :], x_all[:, rows(it, u), :]).then_inc(out_done, 16)
            sp.wait_ge(out_done, 16 * ITERS * UNITS)

        @block.tensor
        def _(pe):
            def mm(dst, lhsT, rhs, first, last):
                return pe.matmul(dst, lhsT, rhs, start=first, stop=last)

            def mm3(dst, lhsT, rhs, first, last):
                mm(dst, rounded(lhsT[0]), rounded(rhs[0]), first, False)
                mm(dst, rounded(lhsT[0]), rounded(rhs[1]), False, False)
                return mm(dst, rounded(lhsT[1]), rounded(rhs[0]), False, last)

            def turn(s, dst_of, blocks):
                bank = ps[dst_of]
                for i, src in enumerate(blocks):
                    t = pe.transpose(bank[:, i * P:(i + 1) * P], src, ident[:])
                t.then_inc(sems[s[0], "mm"], 1)

            def memT(ph, it, s, bank):
                u = s[1]
                pe.wait_ge(ctx_in[u], it * 16 + 16)
                w = weight(w_ff, W0, "mem")
                for c in range(DC):
                    t = mm(bank[:, c * TOK:(c + 1) * TOK], w[:, 0, c * P:(c + 1) * P], ctxT[u][:, :], True, True)
                t.then_inc(sems[s[0], "mm"], 1)

            def mem(ph, it, s, bank):
                u = s[1]
                w = weight(w_ff, W0, "mem")
                for b in range(ROWS):
                    t = mm(bank[:, b * D:(b + 1) * D], ctxT[u][:, b * P:(b + 1) * P], w[:, 0, :], True, True)
                t.then_inc(sems[s[0], "mm"], 1)

            def score0(ph, it, s, bank):
                u = s[1]
                w = views[u]
                pe.wait_ge(xT_in[u], it * 16 + 16)
                pe.wait_ge(*after(ph, it, ("memT", u), "copied"))
                for b in range(ROWS):
                    for c in range(DC):
                        t = mm(bank[:, b * P:(b + 1) * P], w.xT0[:, c, b * P:(b + 1) * P],
                               w.memT[:, c, b * P:(b + 1) * P], c == 0, c == DC - 1)
                t.then_inc(sems[s[0], "mm"], 1)

            def turn0(ph, it, s, bank):
                pe.wait_ge(*after(ph, it, ("score0", s[1]), "exp"))
                turn(s, ph.bank[s], [p_ring[s[1]][:, b * P:(b + 1) * P] for b in range(ROWS)])

            def mix0(ph, it, s, bank):
                u = s[1]
                pe.wait_ge(*after(ph, it, ("turn0", u), "copied"))
                pe.wait_ge(*after(ph, it, ("mem", u), "copied"))
                for b in range(ROWS):
                    t = mm(bank[:, b * D:(b + 1) * D], pT_ring[u][:, b * P:(b + 1) * P], views[u].mem[:, b, :], True,
                           True)
                t.then_inc(sems[s[0], "mm"], 1)

            def mixT(ph, it, s, bank):
                u = s[1]
                pe.wait_ge(*after(ph, it, ("mix0", u), "normed"))
                turn(s, ph.bank[s], [views[u].mix[:, b, c * P:(c + 1) * P] for b in range(ROWS) for c in range(DC)])

            def gate0(ph, it, s, bank):
                u = s[1]
                wg = weight(w_ff, W0, "gate")
                pe.wait_ge(*after(ph, it, ("mixT", u), "copied"))
                for b in range(ROWS):
                    for c in range(2 * DC):
                        lhsT = views[u].xT0[:, c, b * P:(b + 1) * P] if c < DC else views[u].mixT[:, b, c - DC, :]
                        t = mm(bank[:, b * D:(b + 1) * D], lhsT, wg[:, c, :], c == 0, c == 2 * DC - 1)
                t.then_inc(sems[s[0], "mm"], 1)

            def expertT(ph, it, s, bank):
                u, e = s[1], 0 if s[0] in ("xvT", "xvT2") else 1
                pe.wait_ge(*after(ph, it, ("scale_self" if ph.index == 1 else "scale_mlp", u), "xn"))
                turn(s, ph.bank[s], [xn[u][:, b, e, c * P:(c + 1) * P] for c in range(DC) for b in range(ROWS)])

            def qk(ph, it, s, bank):
                u, b = s[1:]
                pe.wait_ge(*after(ph, it, ("xvT", u), "copied"))
                pe.wait_ge(*after(ph, it, ("xlT", u), "copied"))
                for e in range(EXPERTS):
                    for c in range(DC):
                        t = mm(bank[:, :], xT[u][:, e, c, b * P:(b + 1) * P],
                               weight(w_att, W1A, f"qkv{e}")[:, c, 0:2 * D], e + c == 0, e + c == 2)
                t.then_inc(sems[s[0], "mm"], 1)

            def v1(ph, it, s, bank):
                u = s[1]
                for b in range(ROWS):
                    for e in range(EXPERTS):
                        for c in range(DC):
                            t = mm(bank[:, b * D:(b + 1) * D], xT[u][:, e, c, b * P:(b + 1) * P],
                                   weight(w_att, W1A, f"qkv{e}")[:, c, 2 * D:3 * D], e + c == 0, e + c == 2)
                t.then_inc(sems[s[0], "mm"], 1)

            def qkT(ph, it, s, bank):
                u, at = s[1], 0 if s[0] == "qT" else D
                pe.wait_ge(*after(ph, it, ("qk", u, ROWS - 1), "sum"))
                turn(s, ph.bank[s], [qk_of(u, b)[:,
                     at + c * P:at + (c + 1) * P] for b in range(ROWS) for c in range(DC)])

            def scores(ph, it, s, bank):
                kind, u, b, g = s[1:]
                w = views[u]
                heads = slice(g * QUAD, (g + 1) * QUAD)
                if kind == "self":
                    pe.wait_ge(*after(ph, it, ("qT", u), "copied"))
                    pe.wait_ge(*after(ph, it, ("spread", kind, u, b, g // 2), "done"))
                    mm(bank[:, :], ident16[:, :], causal16[:, :].unsqueeze(1).broadcast_to([P, QUAD, P]), True, False)
                    t = mm(bank[:, :], w.qT1[:, b, g // 2, :], w.k1[:, b, heads, :], False, True)
                elif kind == "cross":
                    pe.wait_ge(*after(ph, it, ("cq", u), "copied"))
                    pe.wait_ge(*after(ph, it, ("spread", kind, u, b, g // 2), "done"))
                    t = mm(bank[:, :], w.cqT[:, b * P:(b + 1) * P], w.k1[:, b, heads, :], True, True)
                else:
                    pe.wait_ge(*after(ph, it, ("q2", u, g), "copied"))
                    pe.wait_ge(*after(ph, it, ("k2", u, g), "copied"))
                    settle(pe, "tensor")
                    mm(bank[:, :], ones16[0:1, :], media16[0:1, row(it, u, b), :].broadcast_to([1, QUAD, P]), True,
                       False)
                    for m in (2 * g, 2 * g + 1):
                        half = (m % 2) * 2 * P
                        t = mm(bank[:, half:half + 2 * P], w.qT2[:, m, b * P:(b + 1) * P], w.k2[:, m, b, :, :],
                               False, m % 2 == 1)
                t.then_inc(sems[s[0], "mm"], 1)

            def turn_p(ph, it, s, bank):
                pe.wait_ge(*after(ph, it, ("scores",) + s[1:], "exp"))
                turn(s, ph.bank[s], [p_ring[ph.place[s] % P_RING][:, j * P:(j + 1) * P] for j in range(QUAD)])

            def values(ph, it, s, bank):
                kind, u, b, g = s[1:]
                pe.wait_ge(*after(ph, it, ("turn",) + s[1:], "copied"))
                if (b, g) == (0, 0) and kind == "media":
                    if ph.index == 3:
                        pe.wait_ge(sems["zero", "done"], 2 + 1)
                if (b, g) == (0, 0):
                    of_values = {"self": ("v1", u), "cross": ("cv", u), "media": ("v2", u, ROWS - 1, 1)}[kind]
                    pe.wait_ge(*after(ph, it, of_values, "copied"))
                w = head_width(kind) + 1
                for j in range(QUAD):
                    t = mm(bank[:, j * w:(j + 1) * w], pT_ring[ph.place[s] % PT_RING][:, j * P:(j + 1) * P],
                           v_view(kind, u)[:, b, g * QUAD + j, :], True, True)
                t.then_inc(sems[s[0], "mm"], 1)

            def maskedT(ph, it, s, bank):
                u, b = s[1:]
                pe.wait_ge(*after(ph, it, ("mask", u, b), "done"))
                turn(s, ph.bank[s], [xn[u][:, b, e, c * P:(c + 1) * P] for e in range(EXPERTS) for c in range(DC)])

            def dense(ph, it, s, bank):
                u = s[1]
                for b in range(ROWS):
                    pe.wait_ge(*after(ph, it, ("maskedT", u, b), "copied"))
                    for e in range(EXPERTS):
                        for c in range(DC):
                            t = mm(bank[:, b * D:(b + 1) * D], views[u].oT1[:, b, e, c, :],
                                   weight(w_att, W1A, f"dense{e}")[:, c, :], e + c == 0, e + c == 2)
                t.then_inc(sems[s[0], "mm"], 1)

            def nT(ph, it, s, bank):
                u = s[1]
                scaled = {1: "scale_cross", 3: "scale_q", 5: "scale_q", 4: "scale_ff", 6: "scale_ff"}[ph.index]
                pe.wait_ge(*after(ph, it, (scaled, u), "xn"))
                turn(s, ph.bank[s], [xn[u][:, b, 0, c * P:(c + 1) * P] for c in range(DC) for b in range(ROWS)])

            def cq(ph, it, s, bank):
                u = s[1]
                pe.wait_ge(*after(ph, it, ("nT", u), "copied"))
                for c in range(DC):
                    t = mm(bank[:, 0:TOK], weight(w_att, W1A, "cq")[:, c, :], xT[u][:, 0, c, :], c == 0, c == DC - 1)
                t.then_inc(sems[s[0], "mm"], 1)

            def ctx_here(ph, it, u):
                pe.wait_ge(ctx_in[u], it * 16 + 16 * (CTX_BEFORE[ph.index] + 1))

            def ck(ph, it, s, bank):
                u = s[1]
                ctx_here(ph, it, u)
                mm(bank[:, 0:TOK], weight(w_att, W1A, "ckv")[:, 0, 0:P], ctxT[u][:, :], True, True)\
                  .then_inc(sems[s[0], "mm"], 1)

            def cv(ph, it, s, bank):
                u = s[1]
                for b in range(ROWS):
                    t = mm(bank[:, b * P:(b + 1) * P], ctxT[u][:, b * P:(b + 1) * P],
                           weight(w_att, W1A, "ckv")[:, 0, P:2 * P], True, True)
                t.then_inc(sems[s[0], "mm"], 1)

            def coT(ph, it, s, bank):
                u = s[1]
                pe.wait_ge(*after(ph, it, ("values", "cross", u, ROWS - 1, GROUPS - 1), "normed"))
                turn(s, ph.bank[s], [o[u][:, 1536 + b * P:1536 + (b + 1) * P] for b in range(ROWS)])

            def cdense(ph, it, s, bank):
                u = s[1]
                pe.wait_ge(*after(ph, it, ("coT", u), "copied"))
                for b in range(ROWS):
                    t = mm(bank[:, b * D:(b + 1) * D], views[u].coT[:, b * P:(b + 1) * P],
                           weight(w_att, W1A, "cdense")[:, 0, :], True, True)
                t.then_inc(sems[s[0], "mm"], 1)

            def hidden1(ph, it, s, bank):
                u, e, j = s[1:]
                pe.wait_ge(*after(ph, it, ("xvT2" if e == 0 else "xlT2", u), "lo"))
                name = "gate" if s[0] == "gate1" else "up"
                if u == A_ and j == 0:
                    pe.wait_ge(*split(ph, "experts", 6 * e + (2 if name == "gate" else 5)))
                w, low = weight(w_ff, W1B, f"{name}{e}"), expert_low(name, e)
                for k in range(2):
                    part = slice((2 * j + k) * P, (2 * j + k + 1) * P)
                    for c in range(DC):
                        t = mm3(bank[:, k * TOK:(k + 1) * TOK], (w[:, c, part], low[:, c, part]),
                                (xT[u][:, e, c, :], x_low1(u, e)[:, c, :]), c == 0, c == DC - 1)
                t.then_inc(sems[s[0], "mm"], 1)

            def down(ph, it, s, bank):
                u = s[1]
                pe.wait_ge(*after(ph, it, ("up1", u, EXPERTS - 1, F1C // 2 - 1), "h"))
                pe.wait_ge(*split(ph, "experts", 17))
                for b in range(ROWS):
                    part = slice(b * P, (b + 1) * P)
                    for e in range(EXPERTS):
                        for f in range(F1C):
                            t = mm3(bank[:, b * D:(b + 1) * D],
                                    (views[u].h1[:, e, f, part], h_low1(u, e, f // 2)[:, f % 2, part]),
                                    (weight(w_ff, W1B, f"down{e}")[:, f, :], expert_low("down", e)[:, f, :]),
                                    e + f == 0, e == 1 and f == F1C - 1)
                t.then_inc(sems[s[0], "mm"], 1)

            def q2(ph, it, s, bank):
                u, j = s[1:]
                pe.wait_ge(*after(ph, it, ("nT2", u), "lo"))
                if j == 0:
                    pe.wait_ge(*split(ph, "q", 3))
                for k in range(2):
                    part = slice((2 * j + k) * P, (2 * j + k + 1) * P)
                    for c in range(DC):
                        t = mm3(bank[:, k * TOK:(k + 1) * TOK],
                                (weight(w_att, W2A, "q")[:, c, part], q_low(c)[:, part]),
                                (xT[u][:, 0, c, :], x_low(u, c)), c == 0, c == DC - 1)
                t.then_inc(sems[s[0], "mm"], 1)

            def k2(ph, it, s, bank):
                u, j = s[1:]
                if j == 0:
                    ctx_here(ph, it, u)
                for k in range(2):
                    m = 2 * j + k
                    t = mm(bank[:, k * TOK:(k + 1) * TOK], weight(w_att, W2A, "kv")[:, 0, m * P:(m + 1) * P],
                           ctxT[u][:, :], True, True)
                t.then_inc(sems[s[0], "mm"], 1)

            def v2(ph, it, s, bank):
                u, b, j = s[1:]
                at = INNER + j * BANK
                mm(bank[:, :], ctxT[u][:, b * P:(b + 1) * P], weight(w_att, W2A, "kv")[:, 0, at:at + BANK],
                        True, True).then_inc(sems[s[0], "mm"], 1)

            def oT2(ph, it, s, bank):
                u, b, j = s[1:]
                pe.wait_ge(*after(ph, it, ("values", "media", u, b, 2 * j + 1), "normed"))
                turn(s, ph.bank[s], [o[u][:, b * INNER + m * P:b * INNER + (m + 1) * P] for m in range(4 * j,
                     4 * j + 4)])

            def wo(ph, it, s, bank):
                u = s[1]
                pe.wait_ge(*after(ph, it, ("oT2", u, ROWS - 1, 1), "lo"))
                pe.wait_ge(*split(ph, "o", 3))
                for b in range(ROWS):
                    for m in range(IC):
                        low = b * INNER + m * P
                        t = mm3(bank[:, b * D:(b + 1) * D],
                                (views[u].oT2[:, m, b * P:(b + 1) * P], o[u][:, low:low + P]),
                                (weight(w_att, W2A, "o")[:, m, :], o_low[:, m * D:(m + 1) * D]), m == 0, m == IC - 1)
                t.then_inc(sems[s[0], "mm"], 1)

            def w1(ph, it, s, bank):
                u, j = s[1:]
                pe.wait_ge(*after(ph, it, ("nT2", u), "lo"))
                if j == 0:
                    pe.wait_ge(*split(ph, "w", 3))
                for k in range(2):
                    part = slice((2 * j + k) * P, (2 * j + k + 1) * P)
                    for c in range(DC):
                        t = mm3(bank[:, k * TOK:(k + 1) * TOK],
                                (weight(w_ff, W2B, "w1")[:, c, part], weight(ff_low, W2B, "w1")[:, c, part]),
                                (xT[u][:, 0, c, :], x_low(u, c)), c == 0, c == DC - 1)
                t.then_inc(sems[s[0], "mm"], 1)

            def w2(ph, it, s, bank):
                u = s[1]
                pe.wait_ge(*after(ph, it, ("w1", u, F2C // 2 - 1), "lo"))
                pe.wait_ge(*split(ph, "w", 7))
                for b in range(ROWS):
                    for f in range(F2C):
                        part = slice(b * P, (b + 1) * P)
                        t = mm3(bank[:, b * D:(b + 1) * D], (views[u].h2[:, f, part], views[u].h2_low[:, f, part]),
                                (weight(w_ff, W2B, "w2")[:, f, :], weight(ff_low, W2B, "w2")[:, f, :]),
                                f == 0, f == F2C - 1)
                t.then_inc(sems[s[0], "mm"], 1)

            stages = dict(memT=memT, mem=mem, score0=score0, turn0=turn0, mix0=mix0, mixT=mixT, gate0=gate0,
                          xvT=expertT, xlT=expertT, xvT2=expertT,
                          xlT2=expertT, qk=qk, v1=v1, qT=qkT, kT=qkT, scores=scores, turn=turn_p,
                          values=values, maskedT=maskedT, dense=dense, nT=nT, nT2=nT, cq=cq, ck=ck, cv=cv, coT=coT,
                          cdense=cdense, gate1=hidden1, up1=hidden1, down=down, q2=q2, k2=k2, v2=v2, oT2=oT2,
                          wo=wo, w1=w1, w2=w2)

            pe.wait_ge(consts_in, 16 * 4)
            pe.wait_ge(setup_v, 5)
            pe.matmul(ps[0][:, 0:2 * HD1], pos_hot, rope_tab[:], start=True, stop=True).then_inc(setup_pe, 1)
            pe.wait_ge(setup_v, VECTOR_SETUP)
            pe.wait_ge(primed, 1)

            holder = {}

            def job(ph, it, s):
                k = ph.bank[s]
                if k in holder:
                    p, when, held = holder[k]
                    if held[0] in LAST:
                        held = ("end", held[1])
                    pe.wait_ge(*after(p, when, held, EMPTIED[held[0]]))
                    if s[0] == "scores" and held[0] in ("q2", "k2"):
                        settle(pe, "tensor")
                stages[s[0]](ph, it, s, ps[k])
                holder[k] = (ph, it, s)

            def apart(ph, it, s):
                if s not in ph.bank:
                    return
                if s in ph.prologue and it == 0 and s == [t for t in ph.prologue if t in ph.bank][0]:
                    if ph.index in ATT_LOADS:
                        pe.wait_ge(weights_att, 16 * ATT_LOADS[ph.index])
                        pe.wait_ge(ones_beside, 1)
                    else:
                        pe.wait_ge(weights_ff, 16 * FF_LOADS[ph.index])
                job(ph, it, s)

            for ph in PHASES:
                for p, when, s in between(ph):
                    apart(p, when, s)
                for k, (p, when, s) in holder.items():
                    if s[0] in LAST:
                        s = ("end", s[1])
                        if (s, 0) in p.body and p is ph:
                            continue
                    pe.wait_ge(*after(p, when, s, EMPTIED[s[0]]))
                left = {ph.bank[s]: (s, early) for s, early in ph.body if s in ph.bank}
                with pe.Fori(0, ITERS - 1) as it:
                    holder = {k: (ph, it + (early - 1), s) for k, (s, early) in left.items()}
                    for s, early in ph.body:
                        if s in ph.bank:
                            job(ph, it + early, s)
                holder = {k: (ph, ITERS - 2 + early, s) for k, (s, early) in left.items()}
            for p, when, s in between(None):
                apart(p, when, s)

        @block.vector
        def _(dve):
            def copy(ph, it, s, dst, src):
                dve.wait_ge(*after(ph, it, s, "mm"))
                dve.tensor_copy(dst, src).then_inc(sems[s[0], "copied"], 1)

            def mem(ph, it, s, bank):
                copy(ph, it, s, views[s[1]].mem, bank[:, :].rearrange("p (b d) -> p b d", b=ROWS))

            def score0(ph, it, s, bank):
                u = s[1]
                dve.wait_ge(*after(ph, it, s, "mm"))
                dve.tensor_reduce(nmax[:, u, 0:ROWS], bank[:, 0:TOK].rearrange("p (b t) -> p b t", b=ROWS),
                                       AX_X, ALU.max, negate=True).then_inc(sems[s[0], "max"], 1)

            def mix0(ph, it, s, bank):
                u = s[1]
                dve.wait_ge(*after(ph, it, ("score0", u), "exp"))
                dve.reciprocal(rinv0[:, u, :], rsum0[:, u, :]).then_inc(sems[s[0], "rinv"], 1)
                dve.wait_ge(*after(ph, it, s, "mm"))
                dve.wait_ge(*after(ph, it, s, "rinv"))
                dve.tensor_tensor(views[u].mix, bank[:, :].rearrange("p (b d) -> p b d", b=ROWS),
                                       rinv0[:, u, :].unsqueeze(2).broadcast_to([P, ROWS, D]), ALU.mult)\
                  .then_inc(sems[s[0], "normed"], 1)

            def gate0(ph, it, s, bank):
                dve.wait_ge(*after(ph, it, s, "mm"))
                dve.tensor_tensor(views[s[1]].z, bank[:, :].rearrange("p (b d) -> p b d", b=ROWS),
                                       rows0[:, 0:1, :].broadcast_to([P, ROWS, D]), ALU.add)\
                  .then_inc(sems[s[0], "biased"], 1)

            def spread(ph, it, s, of):
                u = s[1]
                settle(dve, "vector")
                for b in range(ROWS):
                    t = dve.bn_stats(stats[:, u, b, :], of(b))
                t.then_inc(sems[s[0], "stats"], 1)
                dve.wait_ge(*after(ph, it, s, "stats"))
                settle(dve, "vector")
                for b in range(ROWS):
                    t = dve.bn_aggr(aggr[:, u, b, :], stats[:, u, b, :])
                t.then_inc(sems[s[0], "aggr"], 1)

            def out0(ph, it, s, bank):
                u = s[1]
                w = views[u]
                dve.wait_ge(*after(ph, it, s, "tanh"))
                dve.scalar_tensor_tensor(out=w.z, in0=w.z, scalar=1.0, in1=w.mix, op0=ALU.add, op1=ALU.mult)\
                  .then_inc(sems[s[0], "gated"], 1)
                dve.wait_ge(*after(ph, it, s, "gated"))
                dve.wait_ge(x_in[u], it * 16 + 16)
                dve.scalar_tensor_tensor(out=w.fused, in0=w.z, scalar=0.5, in1=w.x0, op0=ALU.mult, op1=ALU.add)\
                  .then_inc(sems[s[0], "fused"], 1)
                dve.wait_ge(*after(ph, it, s, "fused"))
                spread(ph, it, s, lambda b: w.fused[:, b, :])

            def norm(ph, it, s, bank):
                u = s[1]
                if s[0] == "norm_cross":
                    dve.wait_ge(*after(ph, it, ("dense", u), "added"))
                else:
                    dve.wait_ge(*after(PHASES[ph.index - 1], it, ("end", u), "done"))
                spread(ph, it, s, lambda b: x_all[:, row(it, u, b), :])

            def scale(ph, it, s, bank):
                which, u = s[0][len("scale_"):], s[1]
                dve.wait_ge(*after(ph, it, ("norm_" + which, u), "rstd"))
                if which == "mlp":
                    dve.wait_ge(*after(ph, it, ("up1", u, EXPERTS - 1, F1C // 2 - 1), "mm", back=1))
                elif which == "cross":
                    dve.wait_ge(*after(ph, it, ("maskedT", u, ROWS - 1), "mm"))
                else:
                    dve.wait_ge(*after(ph, it, ("nT" if which == "self" else "nT2", u), "mm", back=1))
                if ph.index == 3 and isinstance(it, int) and it == 0:
                    dve.wait_ge(*after(PHASES[2], ITERS - 1, ("up1", u, EXPERTS - 1, F1C // 2 - 1), "mm"))
                for b in range(ROWS):
                    x_b = x_all[:, row(it, u, b), :]
                    if which in ("self", "mlp"):
                        for e in range(EXPERTS):
                            t = dve.tensor_scalar(xn[u][:, b, e:e + 1, :], x_b, rstd[:, u, b, e:e + 1], None, ALU.mult)
                    elif which == "cross":
                        t = dve.tensor_scalar(xn[u][:, b, 0:1, :], x_b, rstd[:, u, b, 0:1], None, ALU.mult)
                    else:
                        t = dve.tensor_scalar(xn[u][:, b, 0:1, :], x_b, aggr[:, u, b, 0:1], rstd[:, u, b, 0:1],
                                              ALU.subtract, ALU.mult)
                t.then_inc(sems[s[0], "xn"], 1)

            def qk(ph, it, s, bank):
                u, b = s[1:]
                r = rot_of(u, b)
                dve.wait_ge(*after(ph, it, s, "mm"))
                heads = bank[:, :].rearrange("p (h d) -> p h d", d=HD1)
                half = HD1 // 2
                by_cos = r[0][:, :].rearrange("p (h d) -> p h d", d=HD1)
                by_sin = r[1][:, :].rearrange("p (h d) -> p h d", d=HD1)
                n = 2 * HEADS
                dve.tensor_tensor(by_cos, heads, rope[:, 0:1, :].broadcast_to([P, n, HD1]), ALU.mult)
                dve.tensor_tensor(by_sin[:, :, 0:half], heads[:, :, half:HD1],
                                  rope[:, 1:2, 0:half].broadcast_to([P, n, half]), ALU.mult)
                dve.tensor_tensor(by_sin[:, :, half:HD1], heads[:, :, 0:half],
                                       rope[:, 1:2, half:HD1].broadcast_to([P, n, half]), ALU.mult)\
                  .then_inc(sems[s[0], "halves"], 1)

            def scores(ph, it, s, bank):
                dve.wait_ge(*after(ph, it, s, "mm"))
                dve.tensor_reduce(nmax[:, ph.place[s] % P_RING, :], bank[:, :].rearrange("p (h t) -> p h t", h=QUAD),
                                       AX_X, ALU.max, negate=True).then_inc(sems[s[0], "max"], 1)

            def turn(ph, it, s, bank):
                copy(ph, it, s, pT_ring[ph.place[s] % PT_RING][:, :], bank[:, :])

            def values(ph, it, s, bank):
                kind, u, b, g = s[1:]
                i = ph.place[s]
                w = head_width(kind) + 1
                r = bank[:, 0:QUAD * w].rearrange("p (h w) -> p h w", w=w)
                dve.wait_ge(*after(ph, it, s, "mm"))
                dve.reciprocal(rinv[:, i % 2, :], r[:, :, w - 1]).then_inc(sems[s[0], "rinv"], 1)
                dve.wait_ge(*after(ph, it, s, "rinv"))
                dve.tensor_tensor(out_of(kind, u, b, g), r[:, :, 0:w - 1],
                                       rinv[:, i % 2, :].unsqueeze(2).broadcast_to([P, QUAD, w - 1]), ALU.mult)\
                  .then_inc(sems[s[0], "normed"], 1)

            def dense(ph, it, s, bank):
                u = s[1]
                dve.wait_ge(*after(ph, it, s, "mm"))
                x_u = x_all[:, rows(it, u), :]
                dve.tensor_tensor(x_u, bank[:, :].rearrange("p (b d) -> p b d", b=ROWS), x_u, ALU.add)\
                  .then_inc(sems[s[0], "added"], 1)

            def up1(ph, it, s, bank):
                u, e, j = s[1:]
                dve.wait_ge(*after(ph, it, ("gate1", u, e, j), "silu"))
                dve.wait_ge(*after(ph, it, s, "mm"))
                product = silu[ph.place[s] % 2].rearrange("p (f t) -> p f t", f=2)
                high = views[u].h1[:, e, 2 * j:2 * j + 2, :]
                dve.tensor_tensor(product, bank[:, :].rearrange("p (f t) -> p f t", f=2), product, ALU.mult)\
                  .then_inc(sems[s[0], "product"], 1)
                dve.wait_ge(*after(ph, it, s, "product"))
                dve.tensor_copy(rounded(high), product).then_inc(sems[s[0], "hi"], 1)
                dve.wait_ge(*after(ph, it, s, "hi"))
                dve.tensor_tensor(rounded(h_low1(u, e, j)), product, rounded(high), ALU.subtract)\
                  .then_inc(sems[s[0], "h"], 1)

            def expertT2(ph, it, s, bank):
                u, e = s[1], 0 if s[0] == "xvT2" else 1
                dve.wait_ge(*after(ph, it, ("xlT2", u), "mm"))
                dve.wait_ge(*after(ph, it, s, "hi"))
                for c in range(DC):
                    at = VEC["mlp_w"] + c
                    t = dve.scalar_tensor_tensor(out=rounded(x_low1(u, e)[:, c, :]), in0=bank[:, c * TOK:(c + 1) * TOK],
                                                 scalar=vec[:, at:at + 1], in1=rounded(xT[u][:, e, c, :]),
                                                 op0=ALU.mult, op1=ALU.subtract)
                t.then_inc(sems[s[0], "lo"], 1)

            def k2(ph, it, s, bank):
                u, j = s[1:]
                dve.wait_ge(*after(ph, it, s, "mm"))
                if ph.index == 3:
                    dve.wait_ge(sems["zero", "done"], u + 1)
                for h in range(2):
                    part = slice(h * HD2, (h + 1) * HD2)
                    t = dve.tensor_copy(views[u].k2[part, 2 * j:2 * j + 2, :, h, :],
                                        bank[part, :].rearrange("p (m b t) -> p m b t", m=2, b=ROWS))
                t.then_inc(sems[s[0], "copied"], 1)

            def split_piece(ph, it, s, bank):
                high, low = piece(s)
                dve.wait_ge(*after(ph, it, ("round",) + s[1:], "done"))
                dve.tensor_tensor(rounded(low), high, rounded(low), ALU.subtract).then_inc(sems[s[0], "lo"], 1)

            def nT2(ph, it, s, bank):
                u = s[1]
                dve.wait_ge(*after(ph, it, s, "hi"))
                low = xn[u][:, :, 1, :]
                dve.tensor_tensor(rounded(low), low, rounded(xT[u][:, 0, :, :]), ALU.subtract)\
                  .then_inc(sems[s[0], "lo"], 1)

            def oT2_low(ph, it, s, bank):
                u, b, j = s[1:]
                s = ("oT2", u, b, j)
                bank = ps[ph.bank[s]]
                low = o[u][:, b * INNER + j * BANK:b * INNER + (j + 1) * BANK].rearrange("p (m t) -> p m t", m=4)
                dve.wait_ge(*after(ph, it, s, "hi"))
                dve.tensor_tensor(rounded(low), bank[:, :].rearrange("p (m t) -> p m t", m=4),
                                       rounded(views[u].oT2[:, 4 * j:4 * j + 4, b * P:(b + 1) * P]), ALU.subtract)\
                  .then_inc(sems[s[0], "lo"], 1)

            def w1(ph, it, s, bank):
                u, j = s[1:]
                high, low = (h[:, 2 * j:2 * j + 2, :] for h in (views[u].h2, views[u].h2_low))
                dve.wait_ge(*after(ph, it, s, "gelu"))
                dve.tensor_copy(rounded(high), low).then_inc(sems[s[0], "hi"], 1)
                dve.wait_ge(*after(ph, it, s, "hi"))
                dve.tensor_tensor(rounded(low), low, rounded(high), ALU.subtract).then_inc(sems[s[0], "lo"], 1)

            def end(ph, it, s, bank):
                u = s[1]
                x_u = x_all[:, rows(it, u), :]
                if ph.index == 0:
                    dve.wait_ge(*after(ph, it, ("out0", u), "rstd"))
                    for b in range(ROWS):
                        t = dve.scalar_tensor_tensor(out=x_all[:, row(it, u, b), :], in0=views[u].fused[:, b:b + 1, :],
                                                     scalar=rstd[:, u, b, 0:1], in1=rows0[:, 1:2, :],
                                                     op0=ALU.mult, op1=ALU.mult)
                    return t.then_inc(sems[s[0], "done"], 1)
                job = final(ph, u)
                dve.wait_ge(*after(ph, it, job, "mm"))
                r = ps[ph.bank[job]][:, :].rearrange("p (b d) -> p b d", b=ROWS)
                if ph.layer == 1:
                    t = dve.tensor_tensor(x_u, r, x_u, ALU.add)
                else:
                    n = {("wo", 2): 0, ("w2", 2): 1, ("wo", 3): 2, ("w2", 3): 3}[job[0], ph.layer]
                    t = dve.scalar_tensor_tensor(out=x_u, in0=r, scalar=tgates[:, n:n + 1], in1=x_u,
                                                 op0=ALU.mult, op1=ALU.add)
                t.then_inc(sems[s[0], "done"], 1)

            stages = dict(mem=mem, score0=score0, mix0=mix0, gate0=gate0, out0=out0, norm_self=norm, norm_cross=norm,
                          norm_mlp=norm, norm_q=norm, norm_ff=norm, scale_self=scale, scale_cross=scale,
                          scale_mlp=scale, scale_q=scale, scale_ff=scale, qk=qk, scores=scores, turn=turn,
                          values=values, dense=dense, up1=up1, k2=k2, end=end, split=split_piece, nT2=nT2,
                          oT2_low=oT2_low, w1=w1, xvT2=expertT2, xlT2=expertT2)

            dve.wait_ge(consts_in, 16 * 4)
            dve.tensor_copy(pos_f[:, 0, :], pos_i[:, :]).then_inc(setup_v, 1)
            dve.wait_ge(setup_v, 1)
            dve.tensor_scalar(pos_f[:, 1, :], pos_f[:, 0, :], 0.0, float(P), ALU.is_lt, ALU.mult).then_inc(setup_v, 1)
            dve.wait_ge(setup_v, 2)
            dve.tensor_tensor(pos_f[:, 0, :], pos_f[:, 0, :], pos_f[:, 1, :], ALU.add).then_inc(setup_v, 1)
            dve.wait_ge(setup_v, 3)
            dve.tensor_scalar(pos_f[:, 1, :], pos_f[:, 0, :], 0.0, float(P - 1), ALU.max, ALU.min).then_inc(setup_v, 1)
            dve.wait_ge(setup_v, 4)
            dve.tensor_scalar(pos_hot, pos_f[:, 1, :], token[:, 0:1], None, ALU.is_equal).then_inc(setup_v, 1)
            dve.tensor_scalar(vm[:, :, 0], tt[:, 0, :], 1.0, None, ALU.is_equal).then_inc(setup_v, 1)
            dve.tensor_scalar(vm[:, :, 1], tt[:, 1, :], 1.0, None, ALU.is_equal).then_inc(setup_v, 1)
            dve.wait_ge(setup_v, 7)
            dve.tensor_tensor(vm[:, :, 0], vm[:, :, 0], vm[:, :, 1], ALU.mult).then_inc(setup_v, 1)
            dve.wait_ge(setup_v, 8)
            dve.tensor_scalar(vm[:, :, 1], vm[:, :, 0], -1.0, 1.0, ALU.mult, ALU.add).then_inc(setup_v, 1)
            dve.tensor_scalar(media16[:, :, :], media[:, :].rearrange("p (b t) -> p b t", b=B), 0.0, MASKED,
                              ALU.is_equal, ALU.mult).then_inc(setup_v, 1)
            dve.memset(ones16[:, :], 1.0).then_inc(setup_v, 1)
            dve.tensor_copy(ident16[:, :], ident[:, :]).then_inc(setup_v, 1)
            dve.tensor_copy(causal16[:, :], causal[:, :]).then_inc(setup_v, 1)
            dve.memset(minus_half[:, :], -0.5).then_inc(setup_v, 1)
            dve.memset(eps[:, 0, :], EPS_RMS).then_inc(setup_v, 1)
            dve.memset(eps[:, 1, :], EPS_LN).then_inc(setup_v, 1)
            dve.wait_ge(setup_pe, 1)
            dve.tensor_copy(rope[:, :, :], ps[0][:, 0:2 * HD1].rearrange("p (a d) -> p a d", a=2)).then_inc(setup_v, 1)
            dve.wait_ge(setup_v, VECTOR_SETUP)
            dve.wait_ge(setup_a, SCALAR_SETUP)
            dve.wait_ge(primed, 1)

            run(dve, stages)

        @block.scalar
        def _(act):
            def copy(ph, it, s, dst, src, scale=1.0, event="copied", func=ACT.Copy):
                act.wait_ge(*after(ph, it, s, "mm"))
                act.activation(dst, src, func, scale=scale).then_inc(sems[s[0], event], 1)

            def memT(ph, it, s, bank):
                copy(ph, it, s, views[s[1]].memT, bank[:, :].rearrange("p (c t) -> p c t", c=DC), D ** -0.5)

            def score0(ph, it, s, bank):
                u = s[1]
                act.wait_ge(*after(ph, it, s, "max"))
                for b in range(ROWS):
                    t = act.activation(p_ring[u][:, b * P:(b + 1) * P], bank[:, b * P:(b + 1) * P], ACT.Exp,
                                       bias=nmax[:, u, b:b + 1], accum_out=rsum0[:, u, b:b + 1])
                t.then_inc(sems[s[0], "exp"], 1)

            def turn0(ph, it, s, bank):
                copy(ph, it, s, pT_ring[s[1]][:, 0:TOK], bank[:, 0:TOK])

            def mixT(ph, it, s, bank):
                copy(ph, it, s, hT[s[1]][:, 1024:1536], bank[:, :])

            def out0(ph, it, s, bank):
                w = views[s[1]]
                act.wait_ge(*after(ph, it, ("gate0", s[1]), "biased"))
                act.activation(w.z, w.z, ACT.Tanh, scale=0.5).then_inc(sems[s[0], "tanh"], 1)

            def expertT(ph, it, s, bank):
                u, e = s[1], 0 if s[0] in ("xvT", "xvT2") else 1
                at = VEC["self_w" if ph.index == 1 else "mlp_w"]
                act.wait_ge(*after(ph, it, s, "mm"))
                for c in range(DC):
                    to = xT[u][:, e, c, :]
                    t = act.activation(to if ph.index == 1 else rounded(to), bank[:, c * TOK:(c + 1) * TOK], ACT.Copy,
                                       scale=vec[:, at + c:at + c + 1])
                t.then_inc(sems[s[0], "copied" if ph.index == 1 else "hi"], 1)

            def v1(ph, it, s, bank):
                copy(ph, it, s, v_view("self", s[1])[:, :, :, 0:HD1],
                     bank[:, :].rearrange("p (b h d) -> p b h d", b=ROWS, h=HEADS))

            def qT(ph, it, s, bank):
                copy(ph, it, s, views[s[1]].qT1, bank[:, :].rearrange("p (b c t) -> p b c t", b=ROWS, c=DC),
                     HD1 ** -0.5)

            def scores(ph, it, s, bank):
                i = ph.place[s]
                act.wait_ge(*after(ph, it, s, "max"))
                before, back = ph.earlier(("turn",) + s[1:], P_RING)
                act.wait_ge(*after(ph, it, before, "copied", back))
                for j in range(QUAD):
                    part = slice(j * P, (j + 1) * P)
                    t = act.activation(p_ring[i % P_RING][:, part], bank[:, part], ACT.Exp,
                                       bias=nmax[:, i % P_RING, j:j + 1])
                t.then_inc(sems[s[0], "exp"], 1)

            def kT(ph, it, s, bank):
                act.wait_ge(*after(ph, it, spreads("self", s[1])[-1], "done", back=1))
                copy(ph, it, s, views[s[1]].k_flat, bank[:, :], event="flat")

            def ck(ph, it, s, bank):
                act.wait_ge(*after(ph, it, spreads("cross", s[1])[-1], "done", back=1))
                copy(ph, it, s, views[s[1]].ck_flat, bank[:, 0:TOK], event="flat")

            def maskedT(ph, it, s, bank):
                u, b = s[1:]
                copy(ph, it, s, views[u].oT1[:, b, :, :, :],
                     bank[:, :].rearrange("p (e c t) -> p e c t", e=EXPERTS, c=DC))

            def nT(ph, it, s, bank):
                u = s[1]
                act.wait_ge(*after(ph, it, s, "mm"))
                for c in range(DC):
                    at = VEC["cross_w"] + c
                    t = act.activation(xT[u][:, 0, c, :], bank[:, c * TOK:(c + 1) * TOK], ACT.Copy,
                                       scale=vec[:, at:at + 1])
                t.then_inc(sems[s[0], "copied"], 1)

            def nT2(ph, it, s, bank):
                u = s[1]
                name = "q" if ph.index in (3, 5) else "ff"
                act.wait_ge(*after(ph, it, s, "mm"))
                for c in range(DC):
                    g, a = (VEC[f"{name}_{x}{ph.layer}"] + c for x in "gb")
                    t = act.activation(x_low(u, c), bank[:, c * TOK:(c + 1) * TOK], ACT.Identity,
                                       scale=vec[:, g:g + 1], bias=vec[:, a:a + 1])
                t.then_inc(sems[s[0], "wide"], 1)
                act.wait_ge(*after(ph, it, s, "wide"))
                act.activation(rounded(xT[u][:, 0, :, :]), xn[u][:, :, 1, :], ACT.Copy).then_inc(sems[s[0], "hi"], 1)

            def cq(ph, it, s, bank):
                copy(ph, it, s, views[s[1]].cqT, bank[:, 0:TOK], HDC ** -0.5)

            def cv(ph, it, s, bank):
                copy(ph, it, s, v_view("cross", s[1])[:, :, :, 0:HDC],
                     bank[:, 0:TOK].rearrange("p (b h d) -> p b h d", b=ROWS, h=HEADS))

            def coT(ph, it, s, bank):
                copy(ph, it, s, views[s[1]].coT, bank[:, 0:TOK])

            def gate1(ph, it, s, bank):
                before, back = ph.earlier(s, 2)
                act.wait_ge(*after(ph, it, ("up1",) + before[1:], "h", back))
                copy(ph, it, s, silu[ph.place[s] % 2], bank[:, :], event="silu", func=ACT.Silu)

            def q2(ph, it, s, bank):
                u, j = s[1:]
                copy(ph, it, s, views[u].qT2[:, 2 * j:2 * j + 2, :], bank[:, :].rearrange("p (m t) -> p m t", m=2),
                     HD2 ** -0.5)

            def v2(ph, it, s, bank):
                u, b, j = s[1:]
                if ph.index == 3:
                    act.wait_ge(sems["zero", "done"], 2 + 1)
                copy(ph, it, s, v_view("media", u)[:, b, j * 8:(j + 1) * 8, 0:HD2],
                     bank[:, :].rearrange("p (h d) -> p h d", d=HD2))

            def oT2(ph, it, s, bank):
                u, b, j = s[1:]
                copy(ph, it, s, rounded(views[u].oT2[:, 4 * j:4 * j + 4, b * P:(b + 1) * P]),
                     bank[:, :].rearrange("p (m t) -> p m t", m=4), event="hi")

            def w1(ph, it, s, bank):
                u, j = s[1:]
                copy(ph, it, s, views[u].h2_low[:, 2 * j:2 * j + 2, :], bank[:, :].rearrange("p (f t) -> p f t", f=2),
                     event="gelu", func=ACT.Gelu)

            def round_piece(ph, it, s, bank):
                high, low = piece(s)
                if ph.index in ATT_LOADS:
                    act.wait_ge(weights_att, 16 * ATT_LOADS[ph.index])
                else:
                    act.wait_ge(weights_ff, 16 * FF_LOADS[ph.index])
                if ph.index == 2:
                    third, at = divmod(s[2], 6)
                    last = ("scores", "cross", third) if third < 2 else ("values", "cross", at // 3)
                    act.wait_ge(*after(PHASES[1], ITERS - 1, last + (ROWS - 1, GROUPS - 1), "mm"))
                if ph.index == 3:
                    act.wait_ge(*after(PHASES[2], ITERS - 1, ("down", s[2] // 2 if s[1] == "q" else B_), "mm"))
                act.activation(rounded(low), high, ACT.Copy).then_inc(sems[s[0], "done"], 1)

            def finish(ph, it, s, bank):
                high, _ = piece(s)
                act.wait_ge(*after(ph, it, ("split",) + s[1:], "lo"))
                act.activation(rounded(high), high, ACT.Copy).then_inc(sems[s[0], "hi"], 1)

            stages = dict(round=round_piece, finish=finish, memT=memT, score0=score0, turn0=turn0, mixT=mixT,
                          out0=out0, xvT=expertT, xlT=expertT, xvT2=expertT, xlT2=expertT,
                          v1=v1, qT=qT, kT=kT, ck=ck, scores=scores, maskedT=maskedT, nT=nT, nT2=nT2, cq=cq, cv=cv,
                          coT=coT, gate1=gate1,
                          q2=q2, v2=v2, oT2=oT2, w1=w1)

            act.wait_ge(consts_in, 16 * 4)
            act.activation(tgates[:, :], gates[:, :], ACT.Tanh).then_inc(setup_a, 1)
            act.wait_ge(primed, 1)

            run(act, stages)

        @block.gpsimd
        def _(pool):
            def to_rstd(ph, it, s, bank):
                u = s[1]
                rms = ph.layer < 2
                experts = s[0] in ("norm_self", "norm_mlp")
                mean, var = aggr[:, u, :, 0], aggr[:, u, :, 1]
                pool.wait_ge(*after(ph, it, s, "aggr"))
                if rms:
                    pool.tensor_tensor(ms[:, u, 0, :], mean, mean, ALU.mult).then_inc(sems[s[0], "square"], 1)
                    pool.wait_ge(*after(ph, it, s, "square"))
                    pool.tensor_tensor(ms[:, u, 1, :], ms[:, u, 0, :], var, ALU.add).then_inc(sems[s[0], "mean"], 1)
                    pool.wait_ge(*after(ph, it, s, "mean"))
                    var = ms[:, u, 1, :]
                pool.tensor_tensor(ms[:, u, 2, :], var, eps[:, 0 if rms else 1, :], ALU.add)\
                  .then_inc(sems[s[0], "eps"], 1)
                if experts:
                    pool.tensor_copy(vm_here[:, u, :, :], vm[:, rows(it, u), :])
                pool.wait_ge(*after(ph, it, s, "eps"))
                r = ms[:, u, 3, :] if experts else rstd[:, u, :, 0]
                pool.tensor_tensor(r, ms[:, u, 2, :], minus_half[:, :], ALU.pow)\
                  .then_inc(sems[s[0], "pow" if experts else "rstd"], 1)
                if experts:
                    pool.wait_ge(*after(ph, it, s, "pow"))
                    pool.tensor_tensor(rstd[:, u, :, :], ms[:, u, 3, :].unsqueeze(2).broadcast_to([P, ROWS, EXPERTS]),
                                            vm_here[:, u, :, :], ALU.mult).then_inc(sems[s[0], "rstd"], 1)

            def qk(ph, it, s, bank):
                u, b = s[1:]
                pool.wait_ge(*after(ph, it, s, "halves"))
                pool.tensor_tensor(qk_of(u, b), *rot_of(u, b), ALU.add).then_inc(sems[s[0], "sum"], 1)

            def mask(ph, it, s, bank):
                u, b = s[1:]
                pool.wait_ge(*after(ph, it, ("values", "self", u, b, GROUPS - 1), "normed"))
                pool.tensor_tensor(xn[u][:, b, :, :],
                                        o[u][:, 1024 + b * D:1024 + (b + 1) * D].unsqueeze(1).broadcast_to([P, EXPERTS, D]),
                                        vm_here[:, u, b, :].unsqueeze(2).broadcast_to([P, EXPERTS, D]), ALU.mult)\
                  .then_inc(sems[s[0], "done"], 1)

            def spread_keys(ph, it, s, bank):
                kind, u, b, half = s[1:]
                w = views[u]
                pool.wait_ge(*after(ph, it, ({"self": "kT", "cross": "ck"}[kind], u), "flat"))
                if (b, half) == (0, 0):
                    other, back = ("cross", 1) if kind == "self" else ("self", 0)
                    pool.wait_ge(*after(ph, it, ("scores", other, u, ROWS - 1, GROUPS - 1), "exp", back))
                n = HEADS // 2
                if kind == "self":
                    src, rows_of = w.k_flat[:, (2 * b + half) * P:(2 * b + half + 1) * P], head_rows[:, 0:n]
                else:
                    src, rows_of = w.ck_flat[:, b * P:(b + 1) * P], head_rows[:, (half + 1) * n:(half + 2) * n]
                pool.tensor_tensor(w.k1[:, b, half * n:(half + 1) * n, :], src.unsqueeze(1).broadcast_to([P, n, P]),
                                        rows_of.unsqueeze(2).broadcast_to([P, n, P]), ALU.mult)\
                  .then_inc(sems[s[0], "done"], 1)

            def zero(ph, it, s, bank):
                n = s[1]
                if n < EXPERTS:
                    pool.wait_ge(*after(PHASES[2], ITERS - 1, ("up1", B_, n, F1C // 2 - 1), "mm"))
                    return pool.memset(kbd[n][:, :], 0.0).then_inc(sems[s[0], "done"], 1)
                pool.wait_ge(*after(PHASES[2], ITERS - 1, ("down", B_), "mm"))
                for u in range(UNITS):
                    t = pool.memset(v_view("media", u)[:, :, :, HD2], 1.0)
                t.then_inc(sems[s[0], "done"], 1)

            stages = dict(zero=zero, spread=spread_keys, out0=to_rstd, norm_self=to_rstd, norm_mlp=to_rstd,
                          norm_cross=to_rstd, norm_q=to_rstd, norm_ff=to_rstd, qk=qk, mask=mask)

            for (kind, event), n in PRIME.items():
                if n:
                    pool.sem_inc(sems[kind, event], n)
            pool.sem_inc(primed, 1)
            pool.wait_ge(setup_v, VECTOR_SETUP)
            for u in range(UNITS):
                for kind in ("self", "cross"):
                    t = pool.memset(v_view(kind, u)[:, :, :, head_width(kind)], 1.0)
            t.then_inc(ones_beside, 1)
            run(pool, stages)



def by_chunk(w, rows_to=None):
    k, n = w.shape
    rows_to = rows_to or k
    if rows_to > k:
        w = np.concatenate([w, np.zeros((rows_to - k, n), w.dtype)])
    return w.reshape(rows_to // P, P, n).transpose(1, 0, 2).reshape(P, -1)


def wide(w, cols):
    return np.concatenate([w, np.zeros((w.shape[0], cols - w.shape[1]), w.dtype)], axis=1)


def kernel(**inputs):
    import concourse.bacc as bacc
    from concourse.bass_utils import run_bass_kernel_spmd

    a = {k: np.asarray(v) for k, v in inputs.items()}
    l0 = lambda n: a["L0_xattn_" + n]
    l1 = lambda n: a["L1_xattn_" + n]
    arrays = {
        "x": a["x"].transpose(1, 0, 2),
        "xT": a["x"].transpose(2, 0, 1).reshape(DC, P, B * P).transpose(1, 0, 2),
        "ctxT": a["ctx_1024"].transpose(2, 0, 1),
        "w0": np.concatenate([l0("W_mem").T, by_chunk(l0("W_gate").T)], axis=1),
        "rows0": np.broadcast_to(np.stack([l0("b_gate"), l0("norm_w")]), (P, 2, D)),
        "w1a": np.concatenate(
            [by_chunk(l1(n)) for n in ("v_qkv", "l_qkv", "v_dense", "l_dense", "cq_w", "ckv_w", "cdense_w")], axis=1),
        "w1b": np.concatenate(
            [by_chunk(wide(l1(n), F1C * P)) for n in ("v_gate", "v_up", "l_gate", "l_up")]
            + [by_chunk(l1(n), F1C * P) for n in ("v_down", "l_down")], axis=1),
    }
    for n in (2, 3):
        ln = lambda name: a[f"L{n}_xattn_{name}"]
        arrays[f"w{n}a"] = np.concatenate([by_chunk(ln("Wq")), ln("Wkv"), by_chunk(ln("Wo"))], axis=1)
        arrays[f"w{n}b"] = np.concatenate([by_chunk(ln("W1")), by_chunk(ln("W2"))], axis=1)
    vecs = [l1("ln_in_w"), l1("ln_post_cross_w"), l1("ln_post_attn_w")]
    for n in (2, 3):
        vecs += [a[f"L{n}_xattn_ln_{x}"] for x in ("q_g", "q_b", "ff_g", "ff_b")]
    arrays["vec"] = np.stack(vecs).reshape(-1, DC, P).transpose(2, 0, 1).reshape(P, -1)
    arrays["gates"] = np.broadcast_to(
        np.concatenate([a["L2_xattn_attn_gate"], a["L2_xattn_ff_gate"], a["L3_xattn_attn_gate"], a["L3_xattn_ff_gate"]]),
        (P, 4))
    kinds = a["mask_BxS_ik0"].T
    arrays["tt"] = np.stack([kinds, np.concatenate([kinds[1:], np.zeros((1, B), kinds.dtype)])], axis=1)
    arrays["media"] = a["mask_BxS2_bk0"].reshape(1, B * P)
    arrays["pos"] = np.broadcast_to(a["pos_1xS"], (P, P))
    f = np.float32
    inv = f(1.0) / f(ROPE_BASE) ** (np.arange(0, HD1, 2, dtype=f) / f(HD1))
    freq = np.outer(np.arange(P, dtype=f), inv).astype(f)
    arrays["rope_tab"] = np.concatenate([np.cos(freq), np.cos(freq), -np.sin(freq), np.sin(freq)], axis=1).astype(f)
    arrays["token"] = np.arange(P, dtype=f).reshape(P, 1)
    arrays["ident"] = np.eye(P, dtype=f)
    arrays["causal"] = np.where(np.tril(np.ones((P, P), bool)), f(0), f(MASKED))
    part = np.arange(P)[:, None]
    arrays["head_rows"] = np.concatenate(
        [part // HD1 == np.arange(P // HD1), part // HDC == np.arange(P // HDC)], axis=1).astype(f)

    arrays["consts"] = np.concatenate([arrays.pop(n).reshape(P, -1) for n in CONSTS], axis=1)

    nc = bacc.Bacc("TRN2", target_bir_lowering=False, num_devices=1)
    given, dram = {}, {}
    for name, array in arrays.items():
        array = np.ascontiguousarray(array)
        given[f"in_{name}"] = array
        dram[name] = nc.dram_tensor(f"in_{name}", array.shape, mybir.dt.from_np(array.dtype), kind="ExternalInput").ap()
    out = nc.dram_tensor("out", (P, B, D), F32, kind="ExternalOutput").ap()
    build(nc, dram, out)
    result = run_bass_kernel_spmd(nc, [given], core_ids=[0])
    return result.results[0]["out"].transpose(1, 0, 2)
```
